# Optimizing a Trainium2 kernel written in Bass

```python
import numpy as np
import jax
import jax.numpy as jnp

def _softmax(x, axis=-1):
    return jax.nn.softmax(x, axis=axis)

def _gelu(x):
    return jax.nn.gelu(x, approximate=True)

def _silu(x):
    return jax.nn.silu(x)

def _sigmoid(x):
    return jax.nn.sigmoid(x)

def _layernorm(x, axis=-1, eps=1e-05):
    m = jnp.mean(x, axis=axis, keepdims=True)
    v = jnp.var(x, axis=axis, keepdims=True)
    return (x - m) / jnp.sqrt(v + eps)

def _scatter_add(tgt, idx, src, axis=0):
    return tgt.at[idx].add(src)

def _segment_sum(src, seg, n):
    return jax.ops.segment_sum(src, seg, n)
kernel_name = 'mk_perceiver_d1_seqx_r2_7343de'

def setup_inputs(seed: int=0):
    np.random.seed(seed)
    _w = jnp.asarray

    def _rec_inputs():
        import jax
        import jax.numpy as jnp
        _rk = jax.random.key(seed)
        x = -0.0002928 + 1 * jax.random.normal(jax.random.fold_in(_rk, 1), (16, 64, 512), jnp.float32)
        _lenS = 64 - jax.random.randint(jax.random.fold_in(_rk, 7), (16,), 0, max(1, 64 // 4) + 1, jnp.int32)
        _lenS2 = 1601 - jax.random.randint(jax.random.fold_in(_rk, 8), (16,), 0, max(1, 1601 // 4) + 1, jnp.int32)
        _ctx_1024P = jax.random.normal(jax.random.fold_in(_rk, 11), (16, 16, 512), jnp.float32)
        _ctx_1024c = jax.random.dirichlet(jax.random.fold_in(_rk, 511), 0.3 * jnp.ones((16,), jnp.float32), (16, 1601))
        _ctx_1024t = jnp.einsum('bsk,bkd->bsd', _ctx_1024c, _ctx_1024P)
        _ctx_1024t = _ctx_1024t * jax.lax.rsqrt(jnp.mean(jnp.square(_ctx_1024t)) + 1e-12) * 0.953939
        ctx_1024 = -1.39393e-06 + 0.999914 * (_ctx_1024t + 0.3 * jax.random.normal(jax.random.fold_in(_rk, 611), (16, 1601, 512), jnp.float32))
        return (x, ctx_1024)
    x, ctx_1024 = _rec_inputs()

    def _L0_xattn_setup():
        import jax, jax.numpy as jnp
        import numpy as np
        MODEL_DIM = 512
        NUM_HEADS = 16
        HEAD_DIM = MODEL_DIM // NUM_HEADS
        SCALE = HEAD_DIM ** (-0.5)
        key = jax.random.key(seed)
        ks = jax.random.split(key, 8)
        B, LQ, LC = (2, 1024, 1024)
        std = MODEL_DIM ** (-0.5)
        return {'query': jax.random.normal(ks[0], (B, LQ, MODEL_DIM), jnp.float32), 'context': jax.random.normal(ks[1], (B, LC, MODEL_DIM), jnp.float32), 'Wq': jax.random.normal(ks[2], (MODEL_DIM, MODEL_DIM), jnp.float32) * std, 'bq': jnp.zeros((MODEL_DIM,), jnp.float32), 'Wkv': jax.random.normal(ks[3], (MODEL_DIM, 2 * MODEL_DIM), jnp.float32) * std, 'bkv': jnp.zeros((2 * MODEL_DIM,), jnp.float32), 'Wout': jax.random.normal(ks[4], (MODEL_DIM, MODEL_DIM), jnp.float32) * std, 'bout': jnp.zeros((MODEL_DIM,), jnp.float32)}
    _L0_xattn_all = _L0_xattn_setup()
    _L0_xattn_in = {k: v for k, v in _L0_xattn_all.items() if k in ('Wq', 'bq', 'Wkv', 'bkv', 'Wout', 'bout')}
    del _L0_xattn_all

    def _L0_attn_setup():
        import jax, jax.numpy as jnp
        import numpy as np
        B, N, D = (2, 4096, 512)
        H = 16
        HD = D // H
        EPS = 1e-06

        def _feature_map(a):
            return jax.nn.elu(a) + 1.0
        key = jax.random.key(seed)
        ks = jax.random.split(key, 5)
        scale = 1.0 / np.sqrt(D)
        return {'x': jax.random.normal(ks[0], (B, N, D), dtype=jnp.float32), 'Wq': jax.random.normal(ks[1], (D, D), dtype=jnp.float32) * scale, 'Wk': jax.random.normal(ks[2], (D, D), dtype=jnp.float32) * scale, 'Wv': jax.random.normal(ks[3], (D, D), dtype=jnp.float32) * scale, 'Wo': jax.random.normal(ks[4], (D, D), dtype=jnp.float32) * scale}
    _L0_attn_all = _L0_attn_setup()
    _L0_attn_in = {k: v for k, v in _L0_attn_all.items() if k in ('Wq', 'Wk', 'Wv', 'Wo')}
    del _L0_attn_all

    def _L0_ffn_setup():
        import jax, jax.numpy as jnp
        import numpy as np
        HIDDEN = 512
        INTER = 1024
        NUM_EXPERTS = 8
        TOPK = 2
        STD = 0.02
        key = jax.random.key(seed)
        k1, k2, k3, k4 = jax.random.split(key, 4)
        return {'hidden_states': jax.random.normal(k1, (1, 1024, HIDDEN), dtype=jnp.float32), 'w1': jax.random.normal(k2, (NUM_EXPERTS, 2 * INTER, HIDDEN), dtype=jnp.float32) * STD, 'w2': jax.random.normal(k3, (NUM_EXPERTS, HIDDEN, INTER), dtype=jnp.float32) * STD, 'router_w': jax.random.normal(k4, (NUM_EXPERTS, HIDDEN), dtype=jnp.float32) * STD}
    _L0_ffn_all = _L0_ffn_setup()
    _L0_ffn_in = {k: v for k, v in _L0_ffn_all.items() if k in ('w1', 'w2', 'router_w')}
    del _L0_ffn_all
    return {'x': x, 'ctx_1024': ctx_1024, 'L0_xattn_Wq': _L0_xattn_in['Wq'], 'L0_xattn_bq': _L0_xattn_in['bq'], 'L0_xattn_Wkv': _L0_xattn_in['Wkv'], 'L0_xattn_bkv': _L0_xattn_in['bkv'], 'L0_xattn_Wout': _L0_xattn_in['Wout'], 'L0_xattn_bout': _L0_xattn_in['bout'], 'L0_attn_Wq': _L0_attn_in['Wq'], 'L0_attn_Wk': _L0_attn_in['Wk'], 'L0_attn_Wv': _L0_attn_in['Wv'], 'L0_attn_Wo': _L0_attn_in['Wo'], 'L0_ffn_w1': _L0_ffn_in['w1'], 'L0_ffn_w2': _L0_ffn_in['w2'], 'L0_ffn_router_w': _L0_ffn_in['router_w']}

def reference(x, ctx_1024, L0_xattn_Wq, L0_xattn_bq, L0_xattn_Wkv, L0_xattn_bkv, L0_xattn_Wout, L0_xattn_bout, L0_attn_Wq, L0_attn_Wk, L0_attn_Wv, L0_attn_Wo, L0_ffn_w1, L0_ffn_w2, L0_ffn_router_w):
    import jax
    import jax.numpy as jnp

    def _L0_xattn_ref(query, context, Wq, bq, Wkv, bkv, Wout, bout):
        import jax, jax.numpy as jnp
        import numpy as np
        MODEL_DIM = 512
        NUM_HEADS = 16
        HEAD_DIM = MODEL_DIM // NUM_HEADS
        SCALE = HEAD_DIM ** (-0.5)
        B, LQ, _ = query.shape
        LC = context.shape[1]
        H, D = (NUM_HEADS, HEAD_DIM)
        q = query @ Wq + bq
        kv = context @ Wkv + bkv
        kv = kv.reshape(B, LC, H, D, 2)
        k = jnp.transpose(kv[..., 0], (0, 2, 1, 3))
        v = jnp.transpose(kv[..., 1], (0, 2, 1, 3))
        q = jnp.transpose(q.reshape(B, LQ, H, D), (0, 2, 1, 3))
        scores = jnp.einsum('bhid,bhjd->bhij', q, k) * SCALE
        attn = jax.nn.softmax(scores, axis=-1)
        out = jnp.einsum('bhij,bhjd->bhid', attn, v)
        out = jnp.transpose(out, (0, 2, 1, 3)).reshape(B, LQ, H * D)
        return out @ Wout + bout

    def _L0_attn_ref(x, Wq, Wk, Wv, Wo):
        import jax, jax.numpy as jnp
        import numpy as np
        B, N, D = (2, 4096, 512)
        H = 16
        HD = D // H
        EPS = 1e-06

        def _feature_map(a):
            return jax.nn.elu(a) + 1.0
        b, n, d = x.shape
        q = _feature_map((x @ Wq.T).reshape(b, n, H, HD))
        k = _feature_map((x @ Wk.T).reshape(b, n, H, HD))
        v = (x @ Wv.T).reshape(b, n, H, HD)
        kv = jnp.einsum('bnhd,bnhm->bhdm', k, v)
        k_sum = k.sum(axis=1)
        numerator = jnp.einsum('bnhd,bhdm->bnhm', q, kv)
        denominator = jnp.einsum('bnhd,bhd->bnh', q, k_sum)[..., None]
        out = numerator / (denominator + EPS)
        out = out.reshape(b, n, d)
        return out @ Wo.T

    def _L0_ffn_ref(hidden_states, w1, w2, router_w):
        import jax, jax.numpy as jnp
        import numpy as np
        HIDDEN = 512
        INTER = 1024
        NUM_EXPERTS = 8
        TOPK = 2
        STD = 0.02
        orig_shape = hidden_states.shape
        dtype = hidden_states.dtype
        x = hidden_states.reshape(-1, orig_shape[-1])
        E = w1.shape[0]
        gating = x @ router_w.T
        probs = jax.nn.softmax(gating.astype(jnp.float32), axis=-1)
        topk_w, sel = jax.lax.top_k(probs, TOPK)
        topk_w = topk_w.astype(dtype)
        combine = (jax.nn.one_hot(sel, E, dtype=dtype) * topk_w[..., None]).sum(axis=1)
        h = jnp.einsum('td,eid->tei', x, w1)
        gate = jax.nn.silu(h[..., :INTER])
        y = h[..., INTER:] * gate
        out = jnp.einsum('tei,ehi,te->th', y, w2, combine)
        return out.reshape(orig_shape)
    x = x + _L0_xattn_ref(_layernorm(x, axis=-1), ctx_1024, L0_xattn_Wq, L0_xattn_bq, L0_xattn_Wkv, L0_xattn_bkv, L0_xattn_Wout, L0_xattn_bout)
    x = x + _L0_attn_ref(_layernorm(x, axis=-1), L0_attn_Wq, L0_attn_Wk, L0_attn_Wv, L0_attn_Wo)
    x = x + _L0_ffn_ref(_layernorm(x, axis=-1), L0_ffn_w1, L0_ffn_w2, L0_ffn_router_w)
    return x

_drawn_inputs = setup_inputs


def setup_inputs(seed=0):
    import zlib

    import numpy as np

    out = dict(_drawn_inputs(seed))
    spreads = {'L0_xattn_bq': (0.0, 0.377), 'L0_xattn_bkv': (0.0, 0.1), 'L0_xattn_bout': (0.0, 0.1)}
    factors = {'L0_attn_Wq': 7.692,
     'L0_attn_Wk': 4.494,
     'L0_ffn_w1': 3.458,
     'L0_ffn_w2': 3.347,
     'L0_ffn_router_w': 3.783}
    for name, (base, spread) in spreads.items():
        noise = np.random.default_rng([zlib.crc32(name.encode()), seed]).standard_normal(out[name].shape)
        drawn = base * np.exp(spread * noise) if base else spread * noise
        out[name] = jnp.asarray(drawn.astype(out[name].dtype))
    for name, factor in factors.items():
        out[name] = (out[name] * factor).astype(out[name].dtype)
    return out
```

```python
from contextlib import ExitStack

import concourse.bass as bass
from concourse import mybir

F32 = mybir.dt.float32
F32R = mybir.dt.float32r
U32 = mybir.dt.uint32
I32 = mybir.dt.int32
ALU = mybir.AluOpType
ACT = mybir.ActivationFunctionType
AX = mybir.AxisListType

P = 128
B, LQ, D = 16, 64, 512
LC = 1601
H, HD = 16, 32
SCALE = HD ** -0.5
LN_EPS = 1e-5
LIN_EPS = 1e-6
NT = B * LQ
TT = NT // P
DT = D // P
PAIRS = H // 2
JT = -(-LC // P)
LC2 = LC + 1
CW = 256
CHUNKS = 6
CHUNK_W = [CW] * (CHUNKS - 1) + [LC2 - CW * (CHUNKS - 1)]
CHUNK_MAX = CHUNK_W[-1]
TAIL = LC - (JT - 1) * P
E, INTER = 8, 1024
IT = INTER // P
BANK = 512
BLOCK = 256
SLOTS = (2 * NT + E * (BLOCK - 1)) // BLOCK
RB = BLOCK // P
SCRATCH = 4096
WC = 2


BEHIND = ["VKK", "VV", "VKK", "VV", "VKK", "VV", "VKV", "VVK"]
GAPS = 4


def plan_units():
    ks = [("K", c, g) for c in range(CHUNKS) for g in range(DT)]
    vs = [("V", min(j * P // CW, CHUNKS - 1), j) for j in range(JT)]
    units, gaps = [], []
    for behind in BEHIND:
        gaps.append([])
        for kinds in ("K", "K", behind[0], behind[1:]):
            gaps[-1].append(list(range(len(units), len(units) + len(kinds))))
            units += [(ks if kind == "K" else vs).pop(0) for kind in kinds]
    assert not ks and not vs
    return units, gaps


UNITS, AT = plan_units()
NU = len(UNITS)
LAST_OF_CHUNK = [max(n for n, u in enumerate(UNITS) if u[1] == c) for c in range(CHUNKS)]
K_WHOLE = [UNITS.index(("K", CHUNKS - 1, p // 2)) for p in range(PAIRS)]


def pair_of_unit(n):
    return next(p for p in range(PAIRS) if n in sum(AT[p], []))


def positive(value):
    return not isinstance(value, int) or value > 0


def build(nc, x, ctx, wq, bq, wk, wv, bk, bv, wout, bout, lwq, lwk, lwv, lwo, router, w1, w2, out):
    q_parts = nc.dram_tensor("q_parts", (2, D, NT), F32, kind="Internal").ap()
    attn_t = nc.dram_tensor("attn_t", (D, NT), F32, kind="Internal").ap()
    rows_in = nc.dram_tensor("rows_in", (SLOTS * BLOCK, D), F32, kind="Internal").ap()
    rows_out = nc.dram_tensor("rows_out", (SLOTS * BLOCK, D), F32, kind="Internal").ap()
    with ExitStack() as whole:
        ident = whole.enter_context(nc.sbuf_tensor("ident", [P, P], F32))
        cross_attention(nc, ident, x, ctx, wq, bq, wk, wv, bk, q_parts, attn_t, rows_in)
        x2 = whole.enter_context(nc.sbuf_tensor("x2", [P, TT, D], F32))
        weight = whole.enter_context(nc.sbuf_tensor("weight", [P, TT, 8], F32))
        place = whole.enter_context(nc.sbuf_tensor("place", [P, 2, TT], U32))
        slot_expert = whole.enter_context(nc.sbuf_tensor("slot_expert", [1, SLOTS + 1], I32))
        linear_attention(nc, ident, x, attn_t, bv, wout, bout, lwq, lwk, lwv, lwo, router,
                         x2, weight, place, slot_expert, rows_in)
        experts(nc, ident, x2, weight, place, slot_expert, rows_in, rows_out, w1, w2, out)


def cross_attention(nc, ident, x, ctx, wq, bq, wk, wv, bk, q_parts, attn_t, rows_in):
    with ExitStack() as mem:
        def sb(name, shape, dt=F32):
            return mem.enter_context(nc.sbuf_tensor(name, shape, dt))

        wk_hi = sb("wk_hi", [P, DT, D], F32R)
        wk_lo = sb("wk_lo", [P, DT, D], F32R)
        wv_hi = sb("wv_hi", [P, DT, D], F32R)
        wv_lo = sb("wv_lo", [P, DT, D], F32R)
        bk_sb = sb("bk_sb", [P, DT])
        queries(nc, ident, x, wq, bq, wk, wv, bk, wk_hi, wk_lo, wv_hi, wv_lo, bk_sb, q_parts)
        attend(nc, ident, ctx, wk_hi, wk_lo, wv_hi, wv_lo, bk_sb, q_parts, attn_t, rows_in)


def queries(nc, ident, x, wq, bq, wk, wv, bk, wk_hi, wk_lo, wv_hi, wv_lo, bk_sb, q_parts):
    with ExitStack() as mem:
        def sb(name, shape, dt=F32):
            return mem.enter_context(nc.sbuf_tensor(name, shape, dt))

        def sem(name):
            return mem.enter_context(nc.semaphore(name))

        xs = sb("xs", [P, TT, D])
        xn = sb("xn", [P, TT, D])
        xn_t = sb("xn_t", [P, DT, NT])
        wq_sb = sb("wq_sb", [P, DT, D])
        wk_raw = sb("wk_raw", [P, DT, D])
        wv_raw = sb("wv_raw", [P, DT, D])
        bq_sb = sb("bq_sb", [P, DT])
        stats = sb("stats", [P, TT, 6])
        mean_var = sb("mean_var", [P, TT, 2])
        std = sb("std", [P, TT])
        rstd = sb("rstd", [P, TT])
        q_t = sb("q_t", [P, DT, NT])
        q_hi = sb("q_hi", [P, DT, NT], F32R)
        q_lo = sb("q_lo", [P, DT, NT], F32R)
        ps_t = [mem.enter_context(nc.psum_tensor(f"ps_t{i}", [P, DT, P], F32)) for i in range(2)]
        ps_q = [mem.enter_context(nc.psum_tensor(f"ps_q{i}", [P, BANK], F32)) for i in range(2)]

        x_loaded = [sem(f"x_loaded{i}") for i in range(4)]
        wq_loaded, bias_loaded = sem("wq_loaded"), sem("bias_loaded")
        wk_loaded, wv_loaded = sem("wk_loaded"), sem("wv_loaded")
        ident_zero, ident_made = sem("ident_zero"), sem("ident_made")
        stats_done, var_done, std_done, rstd_done = sem("stats_done"), sem("var_done"), sem("std_done"), sem("rstd_done")
        xn_done, transposed, xnt_done = sem("xn_done"), sem("transposed"), sem("xnt_done")
        q_done, q_copied, q_hi_done, q_lo_done = sem("q_done"), sem("q_copied"), sem("q_hi_done"), sem("q_lo_done")
        w_hi_done, w_lo_done, q_stored = sem("w_hi_done"), sem("w_lo_done"), sem("q_stored")

        block = mem.enter_context(nc.Block())

        @block.sync
        def _(sp):
            xv = x.rearrange("(t p) d -> p t d", p=P)
            for i in range(4):
                sp.dma_start(xs[:, 2 * i:2 * i + 2, :], xv[:, 2 * i:2 * i + 2, :]).then_inc(x_loaded[i], 16)
            sp.dma_start(wq_sb[:], wq.rearrange("(t p) n -> p t n", p=P)).then_inc(wq_loaded, 16)
            sp.dma_start(bq_sb[:], bq).then_inc(bias_loaded, 16)
            sp.dma_start(bk_sb[:], bk).then_inc(bias_loaded, 16)
            sp.dma_start(wk_raw[:], wk.rearrange("(t p) n -> p t n", p=P)).then_inc(wk_loaded, 16)
            sp.dma_start(wv_raw[:], wv.rearrange("(t p) n -> p t n", p=P)).then_inc(wv_loaded, 16)
            sp.wait_ge(q_hi_done, 1)
            sp.dma_start(q_parts[0].rearrange("(g p) n -> p g n", p=P), q_hi[:].bitcast(F32)).then_inc(q_stored, 16)
            sp.wait_ge(q_lo_done, 1)
            sp.dma_start(q_parts[1].rearrange("(g p) n -> p g n", p=P), q_lo[:].bitcast(F32)).then_inc(q_stored, 16)
            sp.wait_ge(q_stored, 32)

        @block.gpsimd
        def _(pool):
            nc.gpsimd.memset(ident[:], 0.0).then_inc(ident_zero, 1)
            pool.wait_ge(ident_zero, 1)
            nc.gpsimd.affine_select(out=ident[:], in_=ident[:], compare_op=ALU.not_equal, fill=1.0, base=0,
                                    pattern=[[-1, P]], channel_multiplier=1).then_inc(ident_made, 1)
            pool.wait_ge(wk_loaded, 16)
            pool.wait_ge(w_hi_done, 1)
            nc.gpsimd.tensor_tensor(wk_lo[:], wk_raw[:], wk_hi[:].bitcast(F32), ALU.subtract).then_inc(w_lo_done, 1)
            pool.wait_ge(wv_loaded, 16)
            pool.wait_ge(w_hi_done, 2)
            nc.gpsimd.tensor_tensor(wv_lo[:], wv_raw[:], wv_hi[:].bitcast(F32), ALU.subtract).then_inc(w_lo_done, 1)

        @block.vector
        def _(dve):
            for t in range(TT):
                dve.wait_ge(x_loaded[t // 2], 16)
                nc.vector.bn_stats(stats[:, t, :], xs[:, t, :]).then_inc(stats_done, 1)
                dve.wait_ge(stats_done, t + 1)
                nc.vector.bn_aggr(mean_var[:, t, :], stats[:, t, :]).then_inc(var_done, 1)
            dve.wait_ge(var_done, TT)
            nc.vector.tensor_scalar(std[:], mean_var[:, :, 1], LN_EPS, None, ALU.add).then_inc(var_done, 1)
            dve.wait_ge(std_done, 1)
            nc.vector.reciprocal(rstd[:], std[:]).then_inc(rstd_done, 1)
            dve.wait_ge(rstd_done, 1)
            for t in range(TT):
                nc.vector.tensor_scalar(xn[:, t, :], xs[:, t, :], mean_var[:, t, 0:1], rstd[:, t:t + 1],
                                        ALU.subtract, ALU.mult).then_inc(xn_done, 1)
            dve.wait_ge(wk_loaded, 16)
            nc.vector.tensor_copy(wk_hi[:], wk_raw[:]).then_inc(w_hi_done, 1)
            dve.wait_ge(wv_loaded, 16)
            nc.vector.tensor_copy(wv_hi[:], wv_raw[:]).then_inc(w_hi_done, 1)
            dve.wait_ge(q_copied, 2 * DT)
            nc.vector.tensor_copy(q_hi[:], q_t[:]).then_inc(q_hi_done, 1)
            dve.wait_ge(q_hi_done, 1)
            nc.vector.tensor_tensor(q_lo[:], q_t[:], q_hi[:].bitcast(F32), ALU.subtract).then_inc(q_lo_done, 1)

        @block.scalar
        def _(act):
            act.wait_ge(var_done, TT + 1)
            nc.scalar.activation(std[:], std[:], ACT.Sqrt).then_inc(std_done, 1)
            for t in range(TT):
                act.wait_ge(transposed, t + 1)
                nc.scalar.copy(xn_t[:, :, t * P:(t + 1) * P], ps_t[t % 2][:]).then_inc(xnt_done, 1)
            act.wait_ge(bias_loaded, 32)
            for n in range(2 * DT):
                g, half = n // 2, n % 2
                act.wait_ge(q_done, n + 1)
                nc.scalar.activation(q_t[:, g, half * BANK:(half + 1) * BANK], ps_q[n % 2][:], ACT.Identity,
                                     bias=bq_sb[:, g:g + 1]).then_inc(q_copied, 1)

        @block.tensor
        def _(pe):
            pe.wait_ge(ident_made, 1)
            for t in range(TT):
                pe.wait_ge(xn_done, t + 1)
                if t >= 2:
                    pe.wait_ge(xnt_done, t - 1)
                for k in range(DT):
                    last = nc.tensor.transpose(ps_t[t % 2][:, k, :], xn[:, t, k * P:(k + 1) * P], ident[:])
                last.then_inc(transposed, 1)
            pe.wait_ge(xnt_done, TT)
            pe.wait_ge(wq_loaded, 16)
            for n in range(2 * DT):
                g, half = n // 2, n % 2
                if n >= 2:
                    pe.wait_ge(q_copied, n - 1)
                for k in range(DT):
                    last = nc.tensor.matmul(ps_q[n % 2][:], wq_sb[:, k, g * P:(g + 1) * P],
                                            xn_t[:, k, half * BANK:(half + 1) * BANK], start=(k == 0), stop=(k == DT - 1))
                last.then_inc(q_done, 1)


def attend(nc, ident, ctx, wk_hi, wk_lo, wv_hi, wv_lo, bk_sb, q_parts, attn_t, rows_in):
    with ExitStack() as mem:
        def sb(name, shape, dt=F32):
            return mem.enter_context(nc.sbuf_tensor(name, shape, dt))

        def sem(name):
            return mem.enter_context(nc.semaphore(name))

        ctx_raw = [sb(f"ctx_raw{i}", [P, DT * CHUNK_MAX]) for i in range(2)]
        ctx_hi = [sb(f"ctx_hi{i}", [P, DT * CHUNK_MAX], F32R) for i in range(2)]
        ctx_lo = [sb(f"ctx_lo{i}", [P, DT * CHUNK_MAX], F32R) for i in range(2)]
        k_t = [sb(f"k_t{i}", [P, DT, LC2]) for i in range(2)]
        v = [sb(f"v{i}", [P, JT, D]) for i in range(2)]
        k_parts = sb("k_parts", [P, LC2], F32R)
        v_parts = sb("v_parts", [P, JT, 2, 2 * HD], F32R)
        q_blocks = [sb(f"q_blocks{i}", [P, PAIRS // 2, 2, P], F32R) for i in range(2)]
        probs = [sb(f"probs{i}", [P, LC]) for i in range(2)]
        probs_t = sb("probs_t", [P, JT, 2, P], F32R)
        row_max = sb("row_max", [P, 2])
        neg_max = sb("neg_max", [P, 2])
        row_sum = sb("row_sum", [P, 2])
        row_inv = sb("row_inv", [P, 2])
        o_sum = sb("o_sum", [2 * HD, 2, P])
        o_t = sb("o_t", [P, DT, LQ])
        zeros = sb("zeros", [P, RB * P // 2])

        ps_s = mem.enter_context(nc.psum_tensor("ps_s", [P, 4 * BANK], F32))
        ps_kv = [mem.enter_context(nc.psum_tensor(f"ps_kv{i}", [P, BANK], F32)) for i in range(2)]
        ps_pt = mem.enter_context(nc.psum_tensor("ps_pt", [P, 4, P], F32))
        ps_o = mem.enter_context(nc.psum_tensor("ps_o", [P, 4, P], F32))
        ps_turned = [ps_pt, ps_o, ps_pt, ps_pt]

        ctx_loaded = [sem("ctx_loaded0"), sem("ctx_loaded1")]
        ctx_hi_done, ctx_lo_done = sem("ctx_hi_done"), sem("ctx_lo_done")
        kv_done, kv_copied = sem("kv_done"), sem("kv_copied")
        zeroed = sem("zeroed")
        q_loaded = [sem("q_loaded0"), sem("q_loaded1")]
        k_hi_done, k_lo_done, v_hi_done, v_lo_done = sem("k_hi_done"), sem("k_lo_done"), sem("v_hi_done"), sem("v_lo_done")
        scores_done, max_done, neg_done, exp_done = sem("scores_done"), sem("max_done"), sem("neg_done"), sem("exp_done")
        inv_done, probs_done = sem("inv_done"), sem("probs_done")
        pt_done, pt_hi_done, pt_lo_done = sem("pt_done"), sem("pt_hi_done"), sem("pt_lo_done")
        pv_done, o_halves, o_done, o_stored = sem("pv_done"), sem("o_halves"), sem("o_done"), sem("o_stored")
        rows_zeroed = sem("rows_zeroed")
        piece = P * (RB * P // 2)
        pieces = SLOTS * BLOCK * D // piece // (B - 1)
        rows_flat = rows_in.rearrange("n d -> (n d)").rearrange("(k p c) -> k p c", p=P, c=RB * P // 2)

        SC = [(c * BANK, min(BANK, LC2 - c * BANK)) for c in range(4)]
        TG = [list(range(g * 4, min(g * 4 + 4, JT))) for g in range(4)]
        NG = len(TG)

        def rows(j):
            return TAIL if j == JT - 1 else P

        block = mem.enter_context(nc.Block())

        def over_batches(engine, batch):
            batch(0, 0, True)
            with engine.Fori(0, (B - 2) // 2) as i:
                batch(i * 2 + 1, 1, True)
                batch(i * 2 + 2, 0, True)
            batch(B - 1, 1, False)

        def later(b, par, p, steps):
            if p + steps < PAIRS:
                return b, par, p + steps
            return None if isinstance(b, int) and b == B - 1 else (b + 1, 1 - par, p + steps - PAIRS)

        def splits_at(b, p, kv):
            found = []
            for c in range(CHUNKS):
                free_at = pair_of_unit(LAST_OF_CHUNK[c]) + 1
                if kv and free_at == p:
                    found.append((b + 1, c + 2) if c + 2 < CHUNKS else (b + 2, c + 2 - CHUNKS))
                if kv and free_at == PAIRS and p == 0 and not (isinstance(b, int) and b == 0):
                    found.append((b + 1, c + 2 - CHUNKS))
            return found

        @block.sync
        def _(sp):
            def load_ctx(b, c):
                n = CHUNKS * b + c
                if positive(n - 1):
                    sp.wait_ge(ctx_lo_done, n - 1)
                w = DT * CHUNK_W[c]
                sp.dma_start(ctx_raw[c % 2][:, 0:w], ctx[b, :, bass.ds(DT * CW * c, w)] if isinstance(b, int)
                             else ctx[bass.ds(b, 1), :, DT * CW * c:DT * CW * c + w].rearrange("a p n -> p (a n)")
                             ).then_inc(ctx_loaded[c % 2], 16)

            def load_q(b, half):
                for part in range(2):
                    for e in range(2):
                        for copy in range(2):
                            src = q_parts[part].rearrange("(n e r) t -> e r n t", e=2, r=HD)[
                                e, :, 4 * half:4 * half + 4, bass.ds(b * LQ, LQ)]
                            row = 2 * HD * copy + HD * e
                            sp.dma_start(q_blocks[half][row:row + HD, :, part, LQ * e:LQ * e + LQ].bitcast(F32), src
                                         ).then_inc(q_loaded[half], 16)

            def batch(b, par, kv):
                for p in range(PAIRS):
                    if p == 1 and positive(b):
                        sp.wait_ge(o_done, PAIRS * b)
                        sp.dma_start(attn_t.rearrange("(g p) n -> p g n", p=P)[:, :, bass.ds((b - 1) * LQ, LQ)],
                                     o_t[:]).then_inc(o_stored, 16)
                    if kv:
                        for k in range(pieces * p // PAIRS, pieces * (p + 1) // PAIRS):
                            sp.dma_start(rows_flat[bass.ds(b * pieces + k, 1)].rearrange("a p c -> (a p) c"), zeros[:]
                                         ).then_inc(rows_zeroed, 16)
                        for b_of, c in splits_at(b, p, kv):
                            load_ctx(b_of, c)
                        if p in (4, PAIRS - 1):
                            sp.wait_ge(scores_done, PAIRS * b + (PAIRS // 2 if p == 4 else PAIRS))
                            load_q(b + 1, 0 if p == 4 else 1)

            for c in range(2):
                load_ctx(0, c)
            sp.wait_ge(zeroed, 5)
            load_q(0, 0)
            load_q(0, 1)
            for c in range(2, CHUNKS + 2):
                load_ctx(c // CHUNKS, c % CHUNKS)
            over_batches(sp, batch)
            sp.wait_ge(o_done, PAIRS * B)
            sp.dma_start(attn_t.rearrange("(g p) n -> p g n", p=P)[:, :, (B - 1) * LQ:], o_t[:]).then_inc(o_stored, 16)
            sp.wait_ge(o_stored, 16 * B)
            sp.wait_ge(rows_zeroed, 16 * pieces * (B - 1))

        @block.gpsimd
        def _(pool):
            def split_ctx(b, c, ks):
                n = CHUNKS * b + c
                w = DT * CHUNK_W[c]
                pool.wait_ge(ctx_hi_done, n + 1)
                if positive(ks):
                    pool.wait_ge(k_lo_done, ks)
                nc.gpsimd.tensor_tensor(ctx_lo[c % 2][:, 0:w], ctx_raw[c % 2][:, 0:w],
                                        ctx_hi[c % 2][:, 0:w].bitcast(F32), ALU.subtract).then_inc(ctx_lo_done, 1)

            def split_k(b, par, p, chunks):
                s, g = p % 2, p // 2
                pool.wait_ge(k_hi_done, PAIRS * b + p + 1)
                pool.wait_ge(ctx_lo_done, chunks)
                if positive(PAIRS * b + p):
                    pool.wait_ge(k_lo_done, PAIRS * b + p)
                nc.gpsimd.tensor_tensor(k_parts[64 - 64 * s:128 - 64 * s, :], k_t[par][64 * s:64 * s + 64, g, :],
                                        k_parts[64 * s:64 * s + 64, :].bitcast(F32), ALU.subtract
                                        ).then_inc(k_lo_done, 1)

            def batch(b, par, kv):
                chunks = CHUNKS * (b + 1) + (2 if isinstance(b, int) and b == 0 else 1)
                for p in range(PAIRS):
                    n = PAIRS * b + p
                    two_on = later(b, par, p, 2)
                    ks = n + 2 if later(b, par, p, 1) else PAIRS * B
                    pool.wait_ge(v_hi_done, n + 1)
                    pool.wait_ge(k_lo_done, ks)
                    nc.gpsimd.tensor_tensor(v_parts[:, :, 1, :], v[par][:, :, 64 * p:64 * p + 64],
                                            v_parts[:, :, 0, :].bitcast(F32), ALU.subtract).then_inc(v_lo_done, 1)
                    for b_of, c in splits_at(b, p, kv):
                        split_ctx(b_of, c, ks)
                        chunks = chunks + 1
                    if two_on:
                        pool.wait_ge(v_lo_done, n + 1)
                        split_k(*two_on, chunks)

            nc.gpsimd.memset(zeros[:], 0.0).then_inc(zeroed, 1)
            for half in range(2):
                nc.gpsimd.memset(q_blocks[half][:].bitcast(F32), 0.0).then_inc(zeroed, 1)
            for par in range(2):
                pool.wait_ge(zeroed, 3 + par)
                nc.gpsimd.memset(v[par][64:128, JT - 1, :], 0.0).then_inc(zeroed, 1)
            pool.wait_ge(zeroed, 5)
            for c in range(CHUNKS + 2):
                split_ctx(c // CHUNKS, c % CHUNKS, 0)
            for p in range(2):
                split_k(0, 0, p, CHUNKS + 2)
            over_batches(pool, batch)

        @block.vector
        def _(dve):
            def split_ctx(b, c):
                n = CHUNKS * b + c
                w = DT * CHUNK_W[c]
                dve.wait_ge(ctx_loaded[c % 2], (b * (CHUNKS // 2) + c // 2 + 1) * 16)
                if positive(n - 1):
                    before, at = (b, c - 2) if c >= 2 else (b - 1, c - 2 + CHUNKS)
                    dve.wait_ge(kv_done, NU * before + LAST_OF_CHUNK[at] + 1)
                nc.vector.tensor_copy(ctx_hi[c % 2][:, 0:w], ctx_raw[c % 2][:, 0:w]).then_inc(ctx_hi_done, 1)

            def split_k(b, par, p):
                s, g = p % 2, p // 2
                if p % 2 == 0:
                    dve.wait_ge(kv_copied, NU * b + K_WHOLE[p] + 1)
                n = PAIRS * b + p
                if positive(n):
                    dve.wait_ge(scores_done, n)
                nc.vector.tensor_copy(k_parts[64 * s:64 * s + 64, :], k_t[par][64 * s:64 * s + 64, g, :]
                                      ).then_inc(k_hi_done, 1)

            def outputs(n, p):
                s, g = p % 2, p // 2
                dve.wait_ge(pv_done, n + 1)
                for part in range(2):
                    nc.vector.tensor_reduce(o_sum[:, part, :], ps_o[64 * part:64 * part + 64, 0:2].rearrange("p h c -> p c h"),
                                            AX.X, ALU.add).then_inc(o_halves, 1)
                dve.wait_ge(o_halves, (n + 1) * 2)
                for e in range(2):
                    ins = nc.vector.tensor_tensor(o_t[64 * s + HD * e:64 * s + HD * e + HD, g, :],
                                                  o_sum[HD * e:HD * e + HD, 0, LQ * e:LQ * e + LQ],
                                                  o_sum[HD * e:HD * e + HD, 1, LQ * e:LQ * e + LQ], ALU.add)
                ins.then_inc(o_done, 1)

            def guard(n, p):
                q = p % 2
                dve.wait_ge(scores_done, n + 1)
                nc.vector.tensor_reduce(row_max[:, q:q + 1], ps_s[:, 0:LC], AX.X, ALU.max).then_inc(max_done, 1)
                dve.wait_ge(max_done, n + 1)
                nc.vector.tensor_scalar(neg_max[:, q:q + 1], row_max[:, q:q + 1], -SCALE, None, ALU.mult
                                        ).then_inc(neg_done, 1)

            def normalise(n, p):
                q = p % 2
                dve.wait_ge(exp_done, n + 1)
                nc.vector.reciprocal(row_inv[:, q:q + 1], row_sum[:, q:q + 1]).then_inc(inv_done, 1)
                dve.wait_ge(inv_done, n + 1)
                nc.vector.tensor_scalar(probs[q][:], probs[q][:], row_inv[:, q:q + 1], None, ALU.mult
                                        ).then_inc(probs_done, 1)

            def rest(n, g):
                m, k, j = rows(TG[g][0]), len(TG[g]), TG[g][0]
                dve.wait_ge(pt_hi_done, n * NG + g + 1)
                nc.vector.tensor_tensor(probs_t[0:m, j:j + k, 1, :], ps_turned[g][0:m, 0:k, :],
                                        probs_t[0:m, j:j + k, 0, :].bitcast(F32), ALU.subtract).then_inc(pt_lo_done, 1)

            def batch(b, par, kv):
                for p in range(PAIRS):
                    n = PAIRS * b + p
                    one_on, two_on = later(b, par, p, 1), later(b, par, p, 2)
                    if p == 1 and positive(b):
                        dve.wait_ge(o_stored, 16 * b)
                    if positive(n):
                        outputs(n - 1, (p - 1) % PAIRS)
                    rest(n, 0)
                    for b_of, c in splits_at(b, p, kv):
                        split_ctx(b_of, c)
                    rest(n, 1)
                    rest(n, 2)
                    if one_on:
                        guard(n + 1, one_on[2])
                    rest(n, 3)
                    if two_on and p != PAIRS - 2:
                        split_k(*two_on)
                    if one_on:
                        normalise(n + 1, one_on[2])
                    if two_on and p == PAIRS - 2:
                        split_k(*two_on)

            for c in range(CHUNKS + 2):
                split_ctx(c // CHUNKS, c % CHUNKS)
            dve.wait_ge(zeroed, 5)
            split_k(0, 0, 0)
            guard(0, 0)
            split_k(0, 0, 1)
            normalise(0, 0)
            over_batches(dve, batch)
            outputs(PAIRS * B - 1, PAIRS - 1)

        @block.scalar
        def _(act):
            def copy_unit(b, par, n):
                kind, c, which = UNITS[n]
                bank = (NU * par + n) % 2
                act.wait_ge(kv_done, NU * b + n + 1)
                if n == 0 and not (isinstance(b, int) and b < 2):
                    act.wait_ge(k_lo_done, PAIRS * (b - 1))
                    act.wait_ge(v_lo_done, PAIRS * (b - 1))
                if kind == "K":
                    w = CHUNK_W[c]
                    nc.scalar.activation(k_t[par][:, which, CW * c:CW * c + w], ps_kv[bank][:, 0:w], ACT.Identity,
                                         bias=bk_sb[:, which:which + 1]).then_inc(kv_copied, 1)
                else:
                    m = rows(which)
                    nc.scalar.copy(v[par][0:m, which, :], ps_kv[bank][0:m, :]).then_inc(kv_copied, 1)

            def copy_group(n, p, g):
                m, k, j = rows(TG[g][0]), len(TG[g]), TG[g][0]
                act.wait_ge(pt_done, n * NG + g + 1)
                if g == 0 and positive(n):
                    act.wait_ge(pv_done, n)
                nc.scalar.copy(probs_t[0:m, j:j + k, 0, :], ps_turned[g][0:m, 0:k, :]).then_inc(pt_hi_done, 1)

            def exponent(n, p):
                q = p % 2
                act.wait_ge(neg_done, n + 1)
                if positive(n - 1):
                    act.wait_ge(pt_done, (n - 1) * NG)
                nc.scalar.activation(probs[q][:], ps_s[:, 0:LC], ACT.Exp, bias=neg_max[:, q:q + 1], scale=SCALE,
                                     accum_out=row_sum[:, q:q + 1]).then_inc(exp_done, 1)

            def round_v(b, par, p):
                n = PAIRS * b + p
                if p == 0:
                    act.wait_ge(kv_copied, NU * (b + 1))
                if positive(n):
                    act.wait_ge(pv_done, n)
                nc.scalar.copy(v_parts[:, :, 0, :], v[par][:, :, 64 * p:64 * p + 64]).then_inc(v_hi_done, 1)

            def batch(b, par, kv):
                for p in range(PAIRS):
                    n = PAIRS * b + p
                    for g in range(NG):
                        copy_group(n, p, g)
                        if g == 0:
                            round_v(b, par, p)
                        if g == NG - 1 and later(b, par, p, 1):
                            exponent(n + 1, (p + 1) % PAIRS)
                        for u in (AT[p][g] if g < 2 else AT[p][2] + AT[p][3] if g == NG - 1 else []) if kv else []:
                            copy_unit(b + 1, 1 - par, u)

            act.wait_ge(zeroed, 5)
            for u in range(NU):
                copy_unit(0, 0, u)
            exponent(0, 0)
            over_batches(act, batch)

        @block.tensor
        def _(pe):
            def unit(b, par, n):
                kind, c, which = UNITS[n]
                bank = ps_kv[(NU * par + n) % 2]
                if n == 0 or UNITS[n - 1][1] != c:
                    pe.wait_ge(ctx_lo_done, CHUNKS * b + c + 1)
                total = NU * b + n
                if positive(total - 1):
                    pe.wait_ge(kv_copied, total - 1)
                w = CHUNK_W[c]
                for k in range(DT):
                    hi = ctx_hi[c % 2][:, k * w:(k + 1) * w]
                    lo = ctx_lo[c % 2][:, k * w:(k + 1) * w]
                    if kind == "K":
                        dims = slice(which * P, (which + 1) * P)
                        o = bank[:, 0:w]
                        passes = [(wk_hi[:, k, dims], hi), (wk_hi[:, k, dims], lo), (wk_lo[:, k, dims], hi)]
                    else:
                        m = rows(which)
                        tile = slice(which * P - c * CW, which * P - c * CW + m)
                        o = bank[0:m, :]
                        passes = [(hi[:, tile], wv_hi[:, k, :]), (hi[:, tile], wv_lo[:, k, :]),
                                  (lo[:, tile], wv_hi[:, k, :])]
                    for i, (still, moving) in enumerate(passes):
                        last = nc.tensor.matmul(o, still, moving, start=(k == 0 and i == 0),
                                                stop=(k == DT - 1 and i == 2))
                last.then_inc(kv_done, 1)

            def scores(b, p):
                n = PAIRS * b + p
                half = p // 4
                pe.wait_ge(k_lo_done, n + 1)
                if p % 4 == 0:
                    pe.wait_ge(q_loaded[half], 128 * (b + 1))
                if positive(n):
                    pe.wait_ge(exp_done, n)
                for part in range(2):
                    for c0, w in SC:
                        last = nc.tensor.matmul(ps_s[:, c0:c0 + w], q_blocks[half][:, p % 4, part, :],
                                                k_parts[:, c0:c0 + w], start=(part == 0), stop=(part == 1))
                last.then_inc(scores_done, 1)

            def values(n):
                pe.wait_ge(pt_lo_done, NG * (n + 1))
                pe.wait_ge(v_lo_done, n + 1)
                if positive(n):
                    pe.wait_ge(o_halves, 2 * n)
                for j in range(JT):
                    m = rows(j)
                    last = nc.tensor.matmul(ps_o[:, 0:2], v_parts[0:m, j, :, :].rearrange("p a b -> p (a b)"),
                                            probs_t[0:m, j, :, :], start=(j == 0), stop=(j == JT - 1))
                last.then_inc(pv_done, 1)

            def turn(n, q, g):
                if g == 0:
                    pe.wait_ge(probs_done, n + 1)
                if g == 1:
                    if positive(n):
                        pe.wait_ge(o_halves, 2 * n)
                elif positive(n * NG + g):
                    pe.wait_ge(pt_lo_done, n * NG + [0, None, 1, 3][g])
                for i, j in enumerate(TG[g]):
                    m = rows(j)
                    last = nc.tensor.transpose(ps_turned[g][0:m, i, :], probs[q][:, j * P:j * P + m], ident[:])
                last.then_inc(pt_done, 1)

            def batch(b, par, kv):
                for p in range(PAIRS):
                    n = PAIRS * b + p
                    one_on = later(b, par, p, 1)

                    def beside(gap):
                        for u in AT[p][gap] if kv else ():
                            unit(b + 1, 1 - par, u)

                    turn(n, p % 2, 0)
                    beside(0)
                    turn(n, p % 2, 1)
                    beside(1)
                    turn(n, p % 2, 2)
                    if one_on:
                        scores(one_on[0], one_on[2])
                    turn(n, p % 2, 3)
                    beside(2)
                    values(n)
                    beside(3)

            for u in range(NU):
                unit(0, 0, u)
            scores(0, 0)
            over_batches(pe, batch)


def linear_attention(nc, ident, x, attn_t, bv, wout, bout, lwq, lwk, lwv, lwo, router,
                     x2, weight, place, slot_expert, rows_in):
    with ExitStack() as mem:
        def sb(name, shape, dt=F32):
            return mem.enter_context(nc.sbuf_tensor(name, shape, dt))

        def sem(name):
            return mem.enter_context(nc.semaphore(name))

        xs = sb("xs2", [P, TT, D])
        o_t = sb("o_t2", [P, DT, NT])
        xn = sb("xn2", [P, TT, D])
        xn_t = o_t
        w_sb = {n: sb(f"{n}_sb", [P, DT, D]) for n in ("wout", "lwq", "lwk", "lwv", "lwo")}
        router_sb = sb("router_sb", [P, DT, E])
        bv_sb = sb("bv_sb", [P, DT])
        bout_sb = sb("bout_sb", [P, D])
        stats = sb("stats2", [P, TT, 6])
        mean_var = sb("mean_var2", [P, TT, 2])
        std = sb("std2", [P, TT])
        rstd = sb("rstd2", [P, TT])
        q_t = sb("lq_t", [P, DT, NT])
        k_f = sb("lk", [P, TT, D])
        v_f = xs
        low = [sb(f"low{i}", [P, BANK]) for i in range(2)]
        expo = [sb(f"expo{i}", [P, BANK]) for i in range(2)]
        ones = sb("ones", [P, 1])
        same_head = sb("same_head", [P, P])
        kv_blocks = [sb(f"kv_blocks{i}", [P, DT, P]) for i in range(2)]
        ks_blocks = [sb(f"ks_blocks{i}", [P, DT, P]) for i in range(2)]
        den = [sb(f"den{i}", [P, DT, LQ]) for i in range(2)]
        att_t = o_t
        logits = sb("logits", [P, TT, E])
        prob = sb("prob", [P, TT, E])
        top = weight
        top_at = sb("top_at", [P, TT, 8], U32)
        top_f = sb("top_f", [P, TT, 8])
        lane = sb("lane", [P, E])
        picked = sb("picked", [P, 2, TT, E])
        chosen = sb("chosen", [P, TT, E])
        before = sb("before", [P, P])
        all_ones = sb("all_ones", [P, P])
        count = sb("count", [P, TT + 1, E])
        blocks = sb("blocks", [P, E])
        end = sb("end", [P, E + 1])
        first = sb("first", [P, E])
        rank = sb("rank", [P, TT, E])
        at = sb("at", [P, 2, TT, E])
        place_f = sb("place_f", [P, 2, TT])
        slot = sb("slot", [P, SLOTS + 1])
        slot_f = sb("slot_f", [P, SLOTS + 1])
        small = sb("small", [P, 4, TT])
        ps = [mem.enter_context(nc.psum_tensor(f"ps_l{i}", [P, BANK], F32)) for i in range(8)]
        xn_t = sb("xn_t2", [P, DT, NT])

        def norm_rows(eng, t, source_ready, source, sems):
            stats_done, aggr_done, var_done, std_done, rstd_done, xn_done = sems
            if t < TT:
                source_ready(t)
                nc.vector.bn_stats(stats[:, t, :], source[:, t, :]).then_inc(stats_done, 1)
                eng.wait_ge(stats_done, t + 1)
                nc.vector.bn_aggr(mean_var[:, t, :], stats[:, t, :]).then_inc(aggr_done, 1)
                eng.wait_ge(aggr_done, t + 1)
                nc.vector.tensor_scalar(std[:, t:t + 1], mean_var[:, t, 1:2], LN_EPS, None, ALU.add).then_inc(var_done, 1)
            if t >= 1:
                r = t - 1
                eng.wait_ge(std_done, r + 1)
                nc.vector.reciprocal(rstd[:, r:r + 1], std[:, r:r + 1]).then_inc(rstd_done, 1)
                eng.wait_ge(rstd_done, r + 1)
                nc.vector.tensor_scalar(xn[:, r, :], source[:, r, :], mean_var[:, r, 0:1], rstd[:, r:r + 1],
                                        ALU.subtract, ALU.mult).then_inc(xn_done, 1)

        with ExitStack() as stage:
            def sem(name):
                return stage.enter_context(nc.semaphore("c1_" + name))

            o_loaded, x_loaded, bias_loaded = sem("o_loaded"), sem("x_loaded"), sem("bias_loaded")
            w_loaded = {n: sem(f"{n}_loaded") for n in w_sb}
            router_loaded = sem("router_loaded")
            o_biased, x_biased, proj_done, x_added = sem("o_biased"), sem("x_biased"), sem("proj_done"), sem("x_added")
            norm_sems = [sem(n) for n in ("stats", "aggr", "var", "std", "rstd", "xn")]
            turned, xnt_done = sem("turned"), sem("xnt_done")
            block = stage.enter_context(nc.Block())

            @block.sync
            def _(sp):
                sp.dma_start(o_t[:], attn_t.rearrange("(g p) n -> p g n", p=P)).then_inc(o_loaded, 16)
                sp.dma_start(bv_sb[:], bv).then_inc(bias_loaded, 16)
                sp.dma_start(bout_sb[:], bout).then_inc(bias_loaded, 16)
                sp.dma_start(w_sb["wout"][:], wout.rearrange("(t p) n -> p t n", p=P)).then_inc(w_loaded["wout"], 16)
                sp.dma_start(xs[:], x.rearrange("(t p) d -> p t d", p=P)).then_inc(x_loaded, 16)
                for name, w in (("lwq", lwq), ("lwk", lwk), ("lwv", lwv), ("lwo", lwo)):
                    sp.dma_start(w_sb[name][:], w.rearrange("(t p) n -> p t n", p=P)).then_inc(w_loaded[name], 16)
                sp.dma_start(router_sb[:], router.rearrange("p (t e) -> p t e", t=DT)).then_inc(router_loaded, 16)
                for name in ("lwq", "lwk", "lwv", "lwo"):
                    sp.wait_ge(w_loaded[name], 16)
                sp.wait_ge(router_loaded, 16)

            @block.scalar
            def _(act):
                act.wait_ge(o_loaded, 16)
                act.wait_ge(bias_loaded, 32)
                for g in range(DT):
                    nc.scalar.activation(o_t[:, g, :], o_t[:, g, :], ACT.Identity, bias=bv_sb[:, g:g + 1]
                                         ).then_inc(o_biased, 1)
                for t in range(TT + 1):
                    if t < TT:
                        act.wait_ge(norm_sems[2], t + 1)
                        nc.scalar.activation(std[:, t:t + 1], std[:, t:t + 1], ACT.Sqrt).then_inc(norm_sems[3], 1)
                    if t >= 1:
                        act.wait_ge(turned, t)
                        nc.scalar.copy(xn_t[:, :, (t - 1) * P:t * P],
                                       ps[4 + (t - 1) % 2][:].rearrange("p (k c) -> p k c", k=DT)).then_inc(xnt_done, 1)

            @block.vector
            def _(dve):
                dve.wait_ge(x_loaded, 16)
                dve.wait_ge(bias_loaded, 32)
                for t in range(TT):
                    nc.vector.tensor_tensor(xs[:, t, :], xs[:, t, :], bout_sb[:], ALU.add).then_inc(x_biased, 1)

                def ready(t):
                    dve.wait_ge(proj_done, t + 1)
                    dve.wait_ge(x_biased, t + 1)
                    nc.vector.tensor_tensor(x2[:, t, :], ps[t % 2][:], xs[:, t, :], ALU.add).then_inc(x_added, 1)
                    dve.wait_ge(x_added, t + 1)

                for t in range(TT + 1):
                    norm_rows(dve, t, ready, x2, norm_sems)

            @block.tensor
            def _(pe):
                pe.wait_ge(o_biased, DT)
                pe.wait_ge(w_loaded["wout"], 16)
                for t in range(TT + 2):
                    if t < TT:
                        if t >= 2:
                            pe.wait_ge(x_added, t - 1)
                        for g in range(DT):
                            last = nc.tensor.matmul(ps[t % 2][:], o_t[:, g, t * P:(t + 1) * P], w_sb["wout"][:, g, :],
                                                    start=(g == 0), stop=(g == DT - 1))
                        last.then_inc(proj_done, 1)
                    if t >= 2:
                        r = t - 2
                        pe.wait_ge(norm_sems[5], r + 1)
                        if r >= 2:
                            pe.wait_ge(xnt_done, r - 1)
                        for k in range(DT):
                            last = nc.tensor.transpose(ps[4 + r % 2][:, k * P:(k + 1) * P], xn[:, r, k * P:(k + 1) * P],
                                                       ident[:])
                        last.then_inc(turned, 1)

        with ExitStack() as stage:
            def sem(name):
                return stage.enter_context(nc.semaphore("c2_" + name))

            made, low_done, expo_done, mapped = sem("made"), sem("low_done"), sem("expo_done"), sem("mapped")
            v_made, v_copied = sem("v_made"), sem("v_copied")
            block = stage.enter_context(nc.Block())
            NF = 2 * TT

            def mapped_to(n):
                if n < TT:
                    return q_t[:, n // 2, (n % 2) * BANK:(n % 2 + 1) * BANK]
                return k_f[:, n - TT, :]

            @block.tensor
            def _(pe):
                for n in range(NF):
                    if n >= 4:
                        pe.wait_ge(mapped, n - 3)
                    for k in range(DT):
                        if n < TT:
                            g, half = n // 2, n % 2
                            still, moving = w_sb["lwq"][:, k, g * P:(g + 1) * P], xn_t[:, k, half * BANK:(half + 1) * BANK]
                        else:
                            t = n - TT
                            still, moving = xn_t[:, k, t * P:(t + 1) * P], w_sb["lwk"][:, k, :]
                        last = nc.tensor.matmul(ps[n % 4][:], still, moving, start=(k == 0), stop=(k == DT - 1))
                    last.then_inc(made, 1)
                for t in range(TT):
                    if t >= 2:
                        pe.wait_ge(v_copied, t - 1)
                    for k in range(DT):
                        last = nc.tensor.matmul(ps[4 + t % 2][:], xn_t[:, k, t * P:(t + 1) * P], w_sb["lwv"][:, k, :],
                                                start=(k == 0), stop=(k == DT - 1))
                    last.then_inc(v_made, 1)

            @block.vector
            def _(dve):
                for n in range(NF + 1):
                    if n < NF:
                        dve.wait_ge(made, n + 1)
                        if n >= 2:
                            dve.wait_ge(expo_done, n - 1)
                        nc.vector.tensor_scalar(low[n % 2][:], ps[n % 4][:], 0.0, None, ALU.min).then_inc(low_done, 1)
                    if n >= 1:
                        r = n - 1
                        dve.wait_ge(expo_done, r + 1)
                        nc.vector.scalar_tensor_tensor(out=mapped_to(r), in0=ps[r % 4][:], scalar=0.0,
                                                       in1=expo[r % 2][:], op0=ALU.max, op1=ALU.add).then_inc(mapped, 1)

            @block.scalar
            def _(act):
                for n in range(NF):
                    act.wait_ge(low_done, n + 1)
                    if n >= 2:
                        act.wait_ge(mapped, n - 1)
                    nc.scalar.activation(expo[n % 2][:], low[n % 2][:], ACT.Exp).then_inc(expo_done, 1)
                for t in range(TT):
                    act.wait_ge(v_made, t + 1)
                    nc.scalar.copy(v_f[:, t, :], ps[4 + t % 2][:]).then_inc(v_copied, 1)

            @block.gpsimd
            def _(pool):
                nc.gpsimd.memset(ones[:], 1.0)
                nc.gpsimd.iota(lane[:], pattern=[[1, E]], base=0, channel_multiplier=0,
                               allow_small_or_imprecise_dtypes=True)

        with ExitStack() as stage:
            def sem(name):
                return stage.enter_context(nc.semaphore("c3_" + name))

            mask_zero, mask_made = sem("mask_zero"), sem("mask_made")
            kv_done, blocks_done, heads_done, den_done, inv_done, att_done = (
                sem("kv_done"), sem("blocks_done"), sem("heads_done"), sem("den_done"), sem("inv_done"), sem("att_done"))
            block = stage.enter_context(nc.Block())

            @block.tensor
            def _(pe):
                for b in range(B + 1):
                    if b < B:
                        t, r0, i = b // 2, LQ * (b % 2), b % 2
                        if b >= 2:
                            pe.wait_ge(blocks_done, b - 1)
                        for g in range(DT):
                            keys = k_f[r0:r0 + LQ, t, g * P:(g + 1) * P]
                            nc.tensor.matmul(ps[i][:, g * P:(g + 1) * P], keys, v_f[r0:r0 + LQ, t, g * P:(g + 1) * P],
                                             start=True, stop=True, skip_group_check=True)
                            last = nc.tensor.matmul(ps[2 + i][:, g:g + 1], keys, ones[r0:r0 + LQ, :],
                                                    start=True, stop=True, skip_group_check=True)
                        last.then_inc(kv_done, 1)
                    if b >= 1:
                        a = b - 1
                        pe.wait_ge(blocks_done, a + 1)
                        if a >= 2:
                            pe.wait_ge(att_done, a - 1)
                        for g in range(DT):
                            q = q_t[:, g, a * LQ:(a + 1) * LQ]
                            nc.tensor.matmul(ps[4 + a % 2][:, g * LQ:(g + 1) * LQ], kv_blocks[a % 2][:, g, :], q,
                                             start=True, stop=True, skip_group_check=True)
                            last = nc.tensor.matmul(ps[4 + a % 2][:, (DT + g) * LQ:(DT + g + 1) * LQ],
                                                    ks_blocks[a % 2][:, g, :], q, start=True, stop=True,
                                                    skip_group_check=True)
                        last.then_inc(heads_done, 1)

            @block.vector
            def _(dve):
                nc.vector.memset(same_head[:], 0.0).then_inc(mask_zero, 1)
                dve.wait_ge(mask_zero, 1)
                for h in range(DT):
                    nc.vector.memset(same_head[HD * h:HD * h + HD, HD * h:HD * h + HD], 1.0).then_inc(mask_made, 1)
                dve.wait_ge(mask_made, DT)
                for b in range(B + 1):
                    if b < B:
                        i = b % 2
                        dve.wait_ge(kv_done, b + 1)
                        if b >= 2:
                            dve.wait_ge(heads_done, b - 1)
                        masks = same_head[:].unsqueeze(1).to_broadcast([P, DT, P])
                        nc.vector.tensor_tensor(kv_blocks[i][:], ps[i][:].rearrange("p (g c) -> p g c", g=DT), masks,
                                                ALU.mult)
                        nc.vector.tensor_tensor(ks_blocks[i][:], masks,
                                                ps[2 + i][:, 0:DT].unsqueeze(2).to_broadcast([P, DT, P]), ALU.mult
                                                ).then_inc(blocks_done, 1)
                    if b >= 1:
                        a = b - 1
                        i = a % 2
                        heads = ps[4 + i][:].rearrange("p (w g c) -> p w g c", w=2, g=DT)
                        dve.wait_ge(heads_done, a + 1)
                        nc.vector.tensor_scalar(den[i][:], heads[:, 1], LIN_EPS, None, ALU.add).then_inc(den_done, 1)
                        dve.wait_ge(den_done, a + 1)
                        nc.vector.reciprocal(den[i][:], den[i][:]).then_inc(inv_done, 1)
                        dve.wait_ge(inv_done, a + 1)
                        nc.vector.tensor_tensor(att_t[:, :, a * LQ:(a + 1) * LQ], heads[:, 0], den[i][:], ALU.mult
                                                ).then_inc(att_done, 1)

        with ExitStack() as stage:
            def sem(name):
                return stage.enter_context(nc.semaphore("c4_" + name))

            proj_done, x_added = sem("proj_done"), sem("x_added")
            norm_sems = [sem(n) for n in ("stats", "aggr", "var", "std", "rstd", "xn")]
            turned, xnt_done = sem("turned"), sem("xnt_done")
            gated, gmax_done, gneg_done, gexp_done, ginv_done, prob_done = (
                sem("gated"), sem("gmax"), sem("gneg"), sem("gexp"), sem("ginv"), sem("prob"))
            top_done, at_done, atf_done, picked_done, chosen_done = (
                sem("top"), sem("at"), sem("atf"), sem("picked"), sem("chosen"))
            consts, step, ranked, placed, dispatched = sem("consts"), sem("step"), sem("ranked"), sem("placed"), sem("dispatched")
            block = stage.enter_context(nc.Block())

            @block.tensor
            def _(pe):
                for t in range(TT + 2):
                    if t < TT:
                        if t >= 2:
                            pe.wait_ge(x_added, t - 1)
                        for g in range(DT):
                            last = nc.tensor.matmul(ps[t % 2][:], att_t[:, g, t * P:(t + 1) * P], w_sb["lwo"][:, g, :],
                                                    start=(g == 0), stop=(g == DT - 1))
                        last.then_inc(proj_done, 1)
                    if t >= 2:
                        r = t - 2
                        pe.wait_ge(norm_sems[5], r + 1)
                        if r >= 2:
                            pe.wait_ge(xnt_done, r - 1)
                        for k in range(DT):
                            last = nc.tensor.transpose(ps[4 + r % 2][:, k * P:(k + 1) * P], xn[:, r, k * P:(k + 1) * P],
                                                       ident[:])
                        last.then_inc(turned, 1)
                pe.wait_ge(xnt_done, TT)
                for t in range(TT):
                    for k in range(DT):
                        last = nc.tensor.matmul(ps[6][:, t * E:(t + 1) * E], xn_t[:, k, t * P:(t + 1) * P],
                                                router_sb[:, k, :], start=(k == 0), stop=(k == DT - 1))
                last.then_inc(gated, 1)
                pe.wait_ge(consts, 3)
                pe.wait_ge(chosen_done, 1)
                picks = chosen[:].rearrange("p t e -> p (t e)")
                nc.tensor.matmul(ps[0][:, 0:TT * E], before[:], picks, start=True, stop=True)
                nc.tensor.matmul(ps[1][:, 0:TT * E], all_ones[:], picks, start=True, stop=True).then_inc(ranked, 1)

            @block.vector
            def _(dve):
                def ready(t):
                    dve.wait_ge(proj_done, t + 1)
                    nc.vector.tensor_tensor(x2[:, t, :], ps[t % 2][:], x2[:, t, :], ALU.add).then_inc(x_added, 1)
                    dve.wait_ge(x_added, t + 1)

                for t in range(TT + 1):
                    norm_rows(dve, t, ready, x2, norm_sems)
                dve.wait_ge(gated, 1)
                nc.vector.tensor_reduce(small[:, 0, :], ps[6][:, 0:TT * E].rearrange("p (t e) -> p t e", t=TT), AX.X,
                                        ALU.max).then_inc(gmax_done, 1)
                dve.wait_ge(gmax_done, 1)
                nc.vector.tensor_scalar(small[:, 1, :], small[:, 0, :], -1.0, None, ALU.mult).then_inc(gneg_done, 1)
                dve.wait_ge(gexp_done, TT)
                nc.vector.reciprocal(small[:, 3, :], small[:, 2, :]).then_inc(ginv_done, 1)
                dve.wait_ge(ginv_done, 1)
                for t in range(TT):
                    nc.vector.tensor_scalar(prob[:, t, :], logits[:, t, :], small[:, 3, t:t + 1], None, ALU.mult
                                            ).then_inc(prob_done, 1)
                for t in range(TT):
                    dve.wait_ge(prob_done, t + 1)
                    nc.vector.max(top[:, t, :], prob[:, t, :]).then_inc(top_done, 1)
                    dve.wait_ge(top_done, t + 1)
                    nc.vector.max_index(top_at[:, t, :], top[:, t, :], prob[:, t, :]).then_inc(at_done, 1)
                dve.wait_ge(at_done, TT)
                nc.vector.tensor_copy(top_f[:], top_at[:]).then_inc(atf_done, 1)
                dve.wait_ge(atf_done, 1)
                for t in range(TT):
                    for k in range(2):
                        nc.vector.tensor_scalar(picked[:, k, t, :], lane[:], top_f[:, t, k:k + 1], None,
                                                ALU.is_equal).then_inc(picked_done, 1)
                dve.wait_ge(picked_done, 2 * TT)
                nc.vector.tensor_tensor(chosen[:], picked[:, 0], picked[:, 1], ALU.add).then_inc(chosen_done, 1)
                steps = [0]

                def then(ins):
                    steps[0] += 1
                    ins.then_inc(step, 1)
                    dve.wait_ge(step, steps[0])

                then(nc.vector.memset(count[:, 0, :], 0.0))
                then(nc.vector.memset(end[:, 0:1], 0.0))
                dve.wait_ge(ranked, 1)
                for t in range(TT):
                    then(nc.vector.tensor_tensor(count[:, t + 1, :], ps[1][:, t * E:(t + 1) * E], count[:, t, :], ALU.add))
                then(nc.vector.tensor_scalar(blocks[:], count[:, TT, :], 0.0, None, ALU.is_gt))
                for j in range(1, NT // BLOCK):
                    then(nc.vector.scalar_tensor_tensor(out=blocks[:], in0=count[:, TT, :], scalar=float(BLOCK * j),
                                                        in1=blocks[:], op0=ALU.is_gt, op1=ALU.add))
                for e in range(E):
                    then(nc.vector.tensor_tensor(end[:, e + 1:e + 2], end[:, e:e + 1], blocks[:, e:e + 1], ALU.add))
                then(nc.vector.tensor_scalar(first[:], end[:, 0:E], float(BLOCK), None, ALU.mult))
                then(nc.vector.tensor_tensor(rank[:], ps[0][:, 0:TT * E].rearrange("p (t e) -> p t e", t=TT),
                                             count[:, 0:TT, :], ALU.add))
                then(nc.vector.tensor_tensor(rank[:], rank[:], first[:].unsqueeze(1).to_broadcast([P, TT, E]), ALU.add))
                for k in range(2):
                    then(nc.vector.tensor_tensor(at[:, k], rank[:], picked[:, k], ALU.mult))
                then(nc.vector.tensor_reduce(place_f[:], at[:], AX.X, ALU.add))
                nc.vector.tensor_copy(place[:], place_f[:]).then_inc(placed, 1)
                then(nc.vector.tensor_scalar(slot_f[:], slot[:], end[:, 1:2], None, ALU.is_ge))
                for e in range(1, E - 1):
                    then(nc.vector.scalar_tensor_tensor(out=slot_f[:], in0=slot[:], scalar=end[:, e + 1:e + 2],
                                                        in1=slot_f[:], op0=ALU.is_ge, op1=ALU.add))
                then(nc.vector.tensor_copy(slot_expert[:], slot_f[0:1, :]))

            @block.gpsimd
            def _(pool):
                nc.gpsimd.memset(all_ones[:], 1.0).then_inc(consts, 1)
                nc.gpsimd.iota(slot[:], pattern=[[1, SLOTS + 1]], base=0, channel_multiplier=0,
                               allow_small_or_imprecise_dtypes=True).then_inc(consts, 1)
                pool.wait_ge(consts, 2)
                nc.gpsimd.affine_select(out=before[:], in_=all_ones[:], compare_op=ALU.is_gt, fill=0.0, base=0,
                                        pattern=[[1, P]], channel_multiplier=-1).then_inc(consts, 1)
                pool.wait_ge(placed, 1)
                for t in range(TT):
                    for k in range(2):
                        nc.gpsimd.indirect_dma_start(
                            out=rows_in, out_offset=bass.IndirectOffsetOnAxis(ap=place[:, k, t:t + 1], axis=0),
                            in_=xn[:, t, :], in_offset=None).then_inc(dispatched, 16)
                pool.wait_ge(dispatched, 16 * 2 * TT)

            @block.scalar
            def _(act):
                for t in range(TT + 1):
                    if t < TT:
                        act.wait_ge(norm_sems[2], t + 1)
                        nc.scalar.activation(std[:, t:t + 1], std[:, t:t + 1], ACT.Sqrt).then_inc(norm_sems[3], 1)
                    if t >= 1:
                        act.wait_ge(turned, t)
                        nc.scalar.copy(xn_t[:, :, (t - 1) * P:t * P],
                                       ps[4 + (t - 1) % 2][:].rearrange("p (k c) -> p k c", k=DT)).then_inc(xnt_done, 1)
                act.wait_ge(gneg_done, 1)
                for t in range(TT):
                    nc.scalar.activation(logits[:, t, :], ps[6][:, t * E:(t + 1) * E], ACT.Exp, bias=small[:, 1, t:t + 1],
                                         accum_out=small[:, 2, t:t + 1]).then_inc(gexp_done, 1)




def experts(nc, ident, x2, weight, place, slot_expert, rows_in, rows_out, w1, w2, out):
    with ExitStack() as mem:
        def sb(name, shape, dt=F32):
            return mem.enter_context(nc.sbuf_tensor(name, shape, dt))

        def sem(name):
            return mem.enter_context(nc.semaphore("e_" + name))

        RAW = 4
        TAKEN = 4
        rows = [sb(f"rows{i}", [P, RB, D]) for i in range(2)]
        rows_hi = [sb(f"rows_hi{i}", [P, DT, BLOCK], F32R) for i in range(2)]
        rows_lo = [sb(f"rows_lo{i}", [P, DT, BLOCK], F32R) for i in range(2)]
        w1_raw = [sb(f"w1_raw{i}", [P, DT, 2, P]) for i in range(RAW)]
        w1_hi = [sb(f"w1_hi{i}", [P, DT, 2, P], F32R) for i in range(RAW)]
        w1_lo = [sb(f"w1_lo{i}", [P, DT, 2, P], F32R) for i in range(RAW)]
        w2_raw = [sb(f"w2_raw{i}", [P, WC, D]) for i in range(2)]
        w2_hi = [sb(f"w2_hi{i}", [P, IT, D], F32R) for i in range(2)]
        w2_lo = [sb(f"w2_lo{i}", [P, IT, D], F32R) for i in range(2)]
        silu = [sb(f"silu{i}", [P, BLOCK]) for i in range(2)]
        y = [sb(f"y{i}", [P, BLOCK]) for i in range(2)]
        y_hi = [sb(f"y_hi{i}", [P, IT, BLOCK], F32R) for i in range(2)]
        y_lo = [sb(f"y_lo{i}", [P, IT, BLOCK], F32R) for i in range(2)]
        down = sb("down", [P, RB, D])
        taken = [sb(f"taken{i}", [P, D]) for i in range(TAKEN)]
        ps_up = [mem.enter_context(nc.psum_tensor(f"ps_up{i}", [P, 2, BLOCK], F32)) for i in range(4)]
        ps_r = [mem.enter_context(nc.psum_tensor(f"ps_r{i}", [P, DT, P], F32)) for i in range(2)]
        ps_d = [mem.enter_context(nc.psum_tensor(f"ps_d{i}", [P, D], F32)) for i in range(2)]

        rows_loaded = [sem("rows_loaded0"), sem("rows_loaded1")]
        w1_loaded = [sem(f"w1_loaded{i}") for i in range(RAW)]
        w2_loaded = [sem(f"w2_loaded{i}") for i in range(2)]
        w1_hi_done, w1_lo_done, w2_hi_done, w2_lo_done = sem("w1_hi"), sem("w1_lo"), sem("w2_hi"), sem("w2_lo")
        rows_turned, rows_hi_done, rows_lo_done = sem("rows_turned"), sem("rows_hi"), sem("rows_lo")
        up_done, silu_done, y_done, y_hi_done, y_lo_done = sem("up"), sem("silu"), sem("y"), sem("y_hi"), sem("y_lo")
        down_done, down_free = sem("down"), sem("down_free")
        down_stored = [sem(f"down_stored{i}") for i in range(RB)]
        taken_done = [sem(f"taken{i}") for i in range(2 * TT)]
        weighed, stored = sem("weighed"), sem("stored")
        AHEAD = 2
        NW2 = IT // WC

        block = mem.enter_context(nc.Block())

        def over_slots(engine, slot):
            slot(0, 0, 0, False)
            with engine.Fori(0, (SLOTS - 3) // 2) as i:
                slot(i * 2 + 1, 1, i, False)
                slot(i * 2 + 2, 0, i + 1, False)
            slot(SLOTS - 2, 1, (SLOTS - 3) // 2, False)
            slot(SLOTS - 1, 0, (SLOTS - 1) // 2, True)

        @block.sync
        def _(sp):
            def slot(s, par, turn, last):
                e = sp.value_load(slot_expert[0:1, bass.ds(s, 1)], min_val=0, max_val=E - 1)
                if positive(s - 1):
                    sp.wait_ge(rows_turned, (s - 1) * RB)
                sp.dma_start(rows[par][:], rows_in[bass.ds(s * BLOCK, BLOCK), :].rearrange("(r p) d -> p r d", p=P)
                             ).then_inc(rows_loaded[par], 16)
                for u in range(IT):
                    n = IT * s + u
                    if positive(n - RAW + 1):
                        sp.wait_ge(w1_lo_done, n - RAW + 1)
                    sp.dma_start(w1_raw[u % RAW][:], w1[bass.ds(e, 1), u].rearrange(
                        "a p (t s c) -> (a p) t s c", t=DT, s=2)).then_inc(w1_loaded[u % RAW], 16)
                    if u % WC == WC - 1:
                        c = u // WC
                        m = NW2 * s + c
                        if positive(m - 1):
                            sp.wait_ge(w2_lo_done, m - 1)
                        sp.dma_start(w2_raw[c % 2][:], w2[bass.ds(e, 1), c].rearrange(
                            "a p (k n) -> (a p) k n", k=WC)).then_inc(w2_loaded[c % 2], 16)

            over_slots(sp, slot)
            ov = out.rearrange("(t p) d -> p t d", p=P)
            for t in range(TT):
                sp.wait_ge(weighed, 2 * t + 2)
                sp.dma_start(ov[:, t, :], x2[:, t, :]).then_inc(stored, 16)
            sp.wait_ge(stored, 16 * TT)

        @block.gpsimd
        def _(pool):
            def slot(s, par, turn, last):
                for c in range(NW2):
                    pool.wait_ge(w2_hi_done, NW2 * s + c + 1)
                    nc.gpsimd.tensor_tensor(w2_lo[par][:, WC * c:WC * c + WC, :], w2_raw[c % 2][:],
                                            w2_hi[par][:, WC * c:WC * c + WC, :].bitcast(F32), ALU.subtract
                                            ).then_inc(w2_lo_done, 1)

            over_slots(pool, slot)
            for r in range(RB):
                pool.wait_ge(down_stored[r], 16 * SLOTS)
            for t in range(TT):
                for k in range(2):
                    n = 2 * t + k
                    if n >= TAKEN:
                        pool.wait_ge(weighed, n - TAKEN + 1)
                    nc.gpsimd.indirect_dma_start(
                        out=taken[n % TAKEN][:], out_offset=None, in_=rows_out,
                        in_offset=bass.IndirectOffsetOnAxis(ap=place[:, k, t:t + 1], axis=0)).then_inc(taken_done[n], 16)

        @block.scalar
        def _(act):
            def split_w1(s, u):
                n = IT * s + u
                act.wait_ge(w1_loaded[u % RAW], 16 * (s * (IT // RAW) + u // RAW + 1))
                if positive(n - RAW + 1):
                    act.wait_ge(up_done, n - RAW + 1)
                nc.scalar.copy(w1_hi[u % RAW][:], w1_raw[u % RAW][:]).then_inc(w1_hi_done, 1)

            def split_w2(s, par, c):
                act.wait_ge(w2_loaded[c % 2], 16 * (s * (NW2 // 2) + c // 2 + 1))
                if c == 0 and positive(s - 1):
                    act.wait_ge(down_done, RB * (s - 1))
                nc.scalar.copy(w2_hi[par][:, WC * c:WC * c + WC, :], w2_raw[c % 2][:]).then_inc(w2_hi_done, 1)

            def round_y(s, par, u):
                act.wait_ge(y_done, IT * s + u + 1)
                if u == 0 and positive(s - 1):
                    act.wait_ge(down_done, RB * (s - 1))
                nc.scalar.copy(y_hi[par][:, u, :], y[u % 2][:]).then_inc(y_hi_done, 1)

            def round_rows(s, par):
                for r in range(RB):
                    act.wait_ge(rows_turned, s * RB + r + 1)
                    nc.scalar.copy(rows_hi[par][:, :, r * P:(r + 1) * P], ps_r[r][:]).then_inc(rows_hi_done, 1)

            def store_down(s, r):
                act.wait_ge(down_done, RB * s + r + 1)
                if positive(s):
                    act.wait_ge(down_stored[r], 16 * s)
                nc.scalar.copy(down[:, r, :], ps_d[r][:]).then_inc(down_free, 1)
                act.wait_ge(down_free, RB * s + r + 1 + RB)
                act.dma_start(rows_out[bass.ds(s * BLOCK + r * P, P), :], down[:, r, :]).then_inc(down_stored[r], 16)

            def slot(s, par, turn, last):
                first = isinstance(s, int) and s == 0
                for u in range(IT):
                    n = IT * s + u
                    if u == 0 and not first:
                        round_y(s - 1, 1 - par, IT - 1)
                    if u + AHEAD < IT:
                        split_w1(s, u + AHEAD)
                    elif not last:
                        split_w1(s + 1, u + AHEAD - IT)
                    if u % WC == 0:
                        split_w2(s, par, u // WC)
                    if u > 0:
                        round_y(s, par, u - 1)
                    act.wait_ge(up_done, n + 1)
                    if positive(n - 1):
                        act.wait_ge(y_done, n - 1)
                    nc.scalar.activation(silu[u % 2][:], ps_up[u % 4][:, 0, :], ACT.Silu).then_inc(silu_done, 1)
                    if u == IT // 2 and not last:
                        round_rows(s + 1, 1 - par)
                    if u == IT // 2 and not first:
                        store_down(s - 1, 0)
                if not first:
                    store_down(s - 1, 1)

            act.sem_inc(down_free, RB)
            for u in range(AHEAD):
                split_w1(0, u)
            round_rows(0, 0)
            over_slots(act, slot)
            round_y(SLOTS - 1, 0, IT - 1)
            for r in range(RB):
                store_down(SLOTS - 1, r)

        @block.vector
        def _(dve):
            def split_w1(s, u):
                dve.wait_ge(w1_hi_done, IT * s + u + 1)
                nc.vector.tensor_tensor(w1_lo[u % RAW][:], w1_raw[u % RAW][:], w1_hi[u % RAW][:].bitcast(F32),
                                        ALU.subtract).then_inc(w1_lo_done, 1)

            def rest_y(s, par, u):
                dve.wait_ge(y_hi_done, IT * s + u + 1)
                nc.vector.tensor_tensor(y_lo[par][:, u, :], y[u % 2][:], y_hi[par][:, u, :].bitcast(F32), ALU.subtract
                                        ).then_inc(y_lo_done, 1)

            def rest_rows(s, par):
                for r in range(RB):
                    dve.wait_ge(rows_hi_done, s * RB + r + 1)
                    nc.vector.tensor_tensor(rows_lo[par][:, :, r * P:(r + 1) * P], ps_r[r][:],
                                            rows_hi[par][:, :, r * P:(r + 1) * P].bitcast(F32), ALU.subtract
                                            ).then_inc(rows_lo_done, 1)

            def slot(s, par, turn, last):
                for u in range(IT):
                    if u == 0 and not (isinstance(s, int) and s == 0):
                        rest_y(s - 1, 1 - par, IT - 1)
                    if u + AHEAD < IT:
                        split_w1(s, u + AHEAD)
                    elif not last:
                        split_w1(s + 1, u + AHEAD - IT)
                    if u > 0:
                        rest_y(s, par, u - 1)
                    dve.wait_ge(silu_done, IT * s + u + 1)
                    nc.vector.tensor_tensor(y[u % 2][:], ps_up[u % 4][:, 1, :], silu[u % 2][:], ALU.mult
                                            ).then_inc(y_done, 1)
                    if u == IT // 2 and not last:
                        rest_rows(s + 1, 1 - par)

            for u in range(AHEAD):
                split_w1(0, u)
            rest_rows(0, 0)
            over_slots(dve, slot)
            rest_y(SLOTS - 1, 0, IT - 1)
            for t in range(TT):
                for k in range(2):
                    n = 2 * t + k
                    dve.wait_ge(taken_done[n], 16)
                    if n:
                        dve.wait_ge(weighed, n)
                    nc.vector.scalar_tensor_tensor(out=x2[:, t, :], in0=taken[n % TAKEN][:], scalar=weight[:, t, k:k + 1],
                                                   in1=x2[:, t, :], op0=ALU.mult, op1=ALU.add).then_inc(weighed, 1)

        @block.tensor
        def _(pe):
            def turn_rows(s, par, turn):
                pe.wait_ge(rows_loaded[par], 16 * (turn + 1))
                if positive(s):
                    pe.wait_ge(rows_lo_done, RB * s)
                for r in range(RB):
                    for k in range(DT):
                        last = nc.tensor.transpose(ps_r[r][:, k, :], rows[par][:, r, k * P:(k + 1) * P], ident[:])
                    last.then_inc(rows_turned, 1)

            def up(s, par, u):
                n = IT * s + u
                pe.wait_ge(w1_lo_done, n + 1)
                if u == 0:
                    pe.wait_ge(rows_lo_done, RB * (s + 1))
                if positive(n - 3):
                    pe.wait_ge(y_done, n - 3)
                for side in range(2):
                    for k in range(DT):
                        hi, lo = w1_hi[u % RAW][:, k, side, :], w1_lo[u % RAW][:, k, side, :]
                        for i, (still, moving) in enumerate([(hi, rows_hi[par]), (hi, rows_lo[par]), (lo, rows_hi[par])]):
                            last = nc.tensor.matmul(ps_up[u % 4][:, side, :], still, moving[:, k, :],
                                                    start=(k == 0 and i == 0), stop=(k == DT - 1 and i == 2))
                last.then_inc(up_done, 1)

            def down_part(s, par, part):
                r, k0 = part * RB // IT, part * RB % IT
                if part == 0:
                    pe.wait_ge(y_lo_done, IT * (s + 1))
                    pe.wait_ge(w2_lo_done, NW2 * (s + 1))
                if k0 == 0:
                    pe.wait_ge(down_free, RB * s + r + 1)
                for k in range(k0, k0 + RB):
                    yh, yl = (y_[par][:, k, r * P:(r + 1) * P] for y_ in (y_hi, y_lo))
                    for i, (still, moving) in enumerate([(yh, w2_hi[par]), (yh, w2_lo[par]), (yl, w2_hi[par])]):
                        last = nc.tensor.matmul(ps_d[r][:], still, moving[:, k, :], start=(k == 0 and i == 0),
                                                stop=(k == IT - 1 and i == 2))
                if k0 + RB == IT:
                    last.then_inc(down_done, 1)

            def slot(s, par, turn, last):
                for u in range(IT):
                    parts = [[], [0, 1], [2], [3], [4], [5], [6, 7], []][u]
                    up(s, par, u)
                    for part in parts if not (isinstance(s, int) and s == 0) else ():
                        down_part(s - 1, 1 - par, part)
                    if u == 3 and not last:
                        turn_rows(s + 1, 1 - par, turn + (1 if par else 0))

            turn_rows(0, 0, 0)
            over_slots(pe, slot)
            for part in range(IT):
                down_part(SLOTS - 1, 0, part)


_OUT = "out_dram"


def kernel(x, ctx_1024, L0_xattn_Wq, L0_xattn_bq, L0_xattn_Wkv, L0_xattn_bkv, L0_xattn_Wout, L0_xattn_bout,
           L0_attn_Wq, L0_attn_Wk, L0_attn_Wv, L0_attn_Wo, L0_ffn_w1, L0_ffn_w2, L0_ffn_router_w):
    import numpy as np
    import concourse.bacc as bacc
    from concourse.bass_utils import run_bass_kernel_spmd

    def by_partition(v):
        return np.asarray(v).reshape(DT, P).T

    ctx = np.zeros((B + 1, DT, P, LC2), np.float32)
    ctx[:B, :, :, :LC] = np.asarray(ctx_1024).transpose(0, 2, 1).reshape(B, DT, P, LC)
    ctx = np.concatenate([ctx[:, :, :, c * CW:c * CW + CHUNK_W[c]].transpose(0, 2, 1, 3).reshape(B + 1, P, -1)
                          for c in range(CHUNKS)], axis=2)
    wkv = np.asarray(L0_xattn_Wkv).reshape(D, D, 2)
    bkv = np.asarray(L0_xattn_bkv).reshape(D, 2)
    w1 = np.asarray(L0_ffn_w1).reshape(E, 2, IT, P, DT, P).transpose(0, 2, 5, 4, 1, 3).reshape(E, IT, P, DT * 2 * P)
    w2 = np.asarray(L0_ffn_w2).reshape(E, D, IT // WC, WC, P).transpose(0, 2, 4, 3, 1).reshape(E, IT // WC, P, WC * D)
    arrays = {
        "x": np.asarray(x).reshape(NT, D),
        "ctx": ctx,
        "wq": L0_xattn_Wq, "bq": by_partition(L0_xattn_bq),
        "wk": wkv[:, :, 0], "wv": wkv[:, :, 1], "bk": by_partition(bkv[:, 0]), "bv": by_partition(bkv[:, 1]),
        "wout": L0_xattn_Wout, "bout": np.broadcast_to(np.asarray(L0_xattn_bout), (P, D)),
        "lwq": np.asarray(L0_attn_Wq).T, "lwk": np.asarray(L0_attn_Wk).T,
        "lwv": np.asarray(L0_attn_Wv).T, "lwo": np.asarray(L0_attn_Wo).T,
        "router": np.asarray(L0_ffn_router_w).reshape(E, DT, P).transpose(2, 1, 0).reshape(P, DT * E),
        "w1": w1, "w2": w2,
    }
    arrays = {f"{n}_dram": np.ascontiguousarray(a) for n, a in arrays.items()}
    nc = bacc.Bacc("TRN2", target_bir_lowering=False, num_devices=1, dynamic_dma_scratch_size=SCRATCH)
    args = [nc.dram_tensor(n, a.shape, F32, kind="ExternalInput").ap() for n, a in arrays.items()]
    args.append(nc.dram_tensor(_OUT, (NT, D), F32, kind="ExternalOutput").ap())
    names = [n[:-5] for n in arrays] + ["out"]
    build(nc, **dict(zip(names, args)))
    r = run_bass_kernel_spmd(nc, [arrays], core_ids=[0])
    return r.results[0][_OUT].reshape(B, LQ, D)
```

```python
from contextlib import ExitStack

import concourse.bass as bass
from concourse import mybir

F32 = mybir.dt.float32
F32R = mybir.dt.float32r
U32 = mybir.dt.uint32
I32 = mybir.dt.int32
ALU = mybir.AluOpType
ACT = mybir.ActivationFunctionType
AX = mybir.AxisListType

P = 128
B, LQ, D = 16, 64, 512
LC = 1601
H, HD = 16, 32
SCALE = HD ** -0.5
LN_EPS = 1e-5
LIN_EPS = 1e-6
NT = B * LQ
TT = NT // P
DT = D // P
PAIRS = H // 2
JT = -(-LC // P)
LC2 = LC + 1
CW = 256
CHUNKS = 6
CHUNK_W = [CW] * (CHUNKS - 1) + [LC2 - CW * (CHUNKS - 1)]
CHUNK_MAX = CHUNK_W[-1]
TAIL = LC - (JT - 1) * P
E, INTER = 8, 1024
IT = INTER // P
BANK = 512
BLOCK = 256
SLOTS = (2 * NT + E * (BLOCK - 1)) // BLOCK
RB = BLOCK // P
SLOTS_MIN = 2 * NT // BLOCK
PAIRS_MAX, PAIRS_MIN = (SLOTS - 2) // 2, (SLOTS_MIN - 2) // 2
SCRATCH = 4096
WC = 2


BEHIND = ["VKK", "VV", "VKK", "VV", "VKK", "VV", "VKV", "VVK"]
GAPS = 4


def plan_units():
    ks = [("K", c, g) for c in range(CHUNKS) for g in range(DT)]
    vs = [("V", min(j * P // CW, CHUNKS - 1), j) for j in range(JT)]
    units, gaps = [], []
    for behind in BEHIND:
        gaps.append([])
        for kinds in ("K", "K", behind[0], behind[1:]):
            gaps[-1].append(list(range(len(units), len(units) + len(kinds))))
            units += [(ks if kind == "K" else vs).pop(0) for kind in kinds]
    assert not ks and not vs
    return units, gaps


UNITS, AT = plan_units()
NU = len(UNITS)
LAST_OF_CHUNK = [max(n for n, u in enumerate(UNITS) if u[1] == c) for c in range(CHUNKS)]
K_WHOLE = [UNITS.index(("K", CHUNKS - 1, p // 2)) for p in range(PAIRS)]


def pair_of_unit(n):
    return next(p for p in range(PAIRS) if n in sum(AT[p], []))


def positive(value):
    return not isinstance(value, int) or value > 0


def build(nc, x, ctx, wq, bq, wk, wv, bk, bv, wout, bout, lwq, lwk, lwv, lwo, router, w1, w2, out):
    q_parts = nc.dram_tensor("q_parts", (2, D, NT), F32, kind="Internal").ap()
    attn_t = nc.dram_tensor("attn_t", (D, NT), F32, kind="Internal").ap()
    rows_in = nc.dram_tensor("rows_in", (SLOTS * BLOCK, D), F32, kind="Internal").ap()
    rows_out = nc.dram_tensor("rows_out", (SLOTS * BLOCK, D), F32, kind="Internal").ap()
    with ExitStack() as whole:
        ident = whole.enter_context(nc.sbuf_tensor("ident", [P, P], F32))
        cross_attention(nc, ident, x, ctx, wq, bq, wk, wv, bk, bv, q_parts, attn_t, rows_in, rows_out)
        x2 = whole.enter_context(nc.sbuf_tensor("x2", [P, TT, D], F32))
        weight = whole.enter_context(nc.sbuf_tensor("weight", [P, TT, 8], F32))
        place = whole.enter_context(nc.sbuf_tensor("place", [P, 2, TT], U32))
        slot_expert = whole.enter_context(nc.sbuf_tensor("slot_expert", [1, SLOTS + 1], I32))
        slot_pairs = whole.enter_context(nc.sbuf_tensor("slot_pairs", [1, 1], I32))
        linear_attention(nc, ident, x, attn_t, wout, bout, lwq, lwk, lwv, lwo, router,
                         x2, weight, place, slot_expert, slot_pairs, rows_in)
        experts(nc, ident, x2, weight, place, slot_expert, slot_pairs, rows_in, rows_out, w1, w2, out)


def cross_attention(nc, ident, x, ctx, wq, bq, wk, wv, bk, bv, q_parts, attn_t, rows_in, rows_out):
    with ExitStack() as mem:
        def sb(name, shape, dt=F32):
            return mem.enter_context(nc.sbuf_tensor(name, shape, dt))

        def sem(name):
            return mem.enter_context(nc.semaphore(name))

        wk_hi = sb("wk_hi", [P, DT, D], F32R)
        wk_lo = sb("wk_lo", [P, DT, D], F32R)
        wv_hi = sb("wv_hi", [P, DT, D], F32R)
        wv_lo = sb("wv_lo", [P, DT, D], F32R)
        bq_sb = sb("bq_sb", [P, DT])
        bk_sb = sb("bk_sb", [P, DT])
        bv_sb = sb("bv_sb", [2 * HD, PAIRS])
        stats = sb("stats", [P, TT, 6])
        mean_var = sb("mean_var", [P, TT, 2])
        std = sb("std", [P, TT])
        rstd = sb("rstd", [P, TT])
        ctx_raw = [sb(f"ctx_raw{i}", [P, DT * CHUNK_MAX]) for i in range(2)]
        ctx_hi = [sb(f"ctx_hi{i}", [P, DT * CHUNK_MAX], F32R) for i in range(2)]
        ctx_lo = [sb(f"ctx_lo{i}", [P, DT * CHUNK_MAX], F32R) for i in range(2)]
        k_t = [sb(f"k_t{i}", [P, DT, LC2]) for i in range(2)]
        v = [sb(f"v{i}", [P, JT, D]) for i in range(2)]
        k_parts = sb("k_parts", [P, LC2], F32R)
        v_parts = sb("v_parts", [P, JT, 2, 2 * HD], F32R)
        q_blocks = [sb(f"q_blocks{i}", [P, PAIRS // 2, 2, P], F32R) for i in range(2)]
        probs_both = sb("probs_both", [P, 2 * LC])
        probs = [probs_both[:, i * LC:(i + 1) * LC] for i in range(2)]
        probs_t = sb("probs_t", [P, JT, 2, P], F32R)
        row_max = sb("row_max", [P, 2])
        neg_max = sb("neg_max", [P, 2])
        row_sum = sb("row_sum", [P, 2])
        row_inv = sb("row_inv", [P, 2])
        o_sum = sb("o_sum", [2 * HD, 2, P])
        o_t = sb("o_t", [P, DT, LQ])
        zeros = sb("zeros", [P, RB * P // 2])

        k_room, v_room = k_t[1][:].rearrange("p g n -> p (g n)"), v[1][:].rearrange("p t n -> p (t n)")
        q_room = probs_t[:].rearrange("p t i n -> p (t i n)")
        xs = k_room[:, 0:TT * D].rearrange("p (t d) -> p t d", t=TT)
        wq_sb = k_room[:, TT * D:(TT + DT) * D].rearrange("p (t d) -> p t d", t=DT)
        xn_t = v_room[:, 0:DT * NT].rearrange("p (t n) -> p t n", t=DT)
        wk_raw = v_room[:, DT * NT:DT * (NT + D)].rearrange("p (t d) -> p t d", t=DT)
        wv_raw = probs_both[:, 0:DT * D].rearrange("p (t d) -> p t d", t=DT)
        q_hi = [q_room[:, i * BANK:(i + 1) * BANK] for i in range(2)]
        q_lo = [q_room[:, (2 + i) * BANK:(3 + i) * BANK] for i in range(2)]

        ps_s = mem.enter_context(nc.psum_tensor("ps_s", [P, 4 * BANK], F32))
        ps_kv = [mem.enter_context(nc.psum_tensor(f"ps_kv{i}", [P, BANK], F32)) for i in range(2)]
        ps_pt = mem.enter_context(nc.psum_tensor("ps_pt", [P, 4, P], F32))
        ps_o = mem.enter_context(nc.psum_tensor("ps_o", [P, 4, P], F32))
        ps_turned = [ps_pt, ps_o, ps_pt, ps_pt]

        x_loaded = [sem(f"x_loaded{i}") for i in range(4)]
        wq_loaded, bias_loaded = sem("wq_loaded"), sem("bias_loaded")
        wk_loaded, wv_loaded = sem("wk_loaded"), sem("wv_loaded")
        ident_zero, ident_made = sem("ident_zero"), sem("ident_made")
        stats_done, var_done, std_done, rstd_done = sem("stats_done"), sem("var_done"), sem("std_done"), sem("rstd_done")
        xn_done, turned, xnt_done = sem("xn_done"), sem("turned"), sem("xnt_done")
        q_done, q_hi_done, q_lo_done = sem("q_done"), sem("q_hi_done"), sem("q_lo_done")
        q_stored = [[sem(f"q_{part}_stored{i}") for i in range(2)] for part in ("hi", "lo")]
        w_hi_done, w_lo_done = sem("w_hi_done"), sem("w_lo_done")

        ctx_loaded = [sem("ctx_loaded0"), sem("ctx_loaded1")]
        ctx_hi_done, ctx_lo_done = sem("ctx_hi_done"), sem("ctx_lo_done")
        kv_done, kv_copied = sem("kv_done"), sem("kv_copied")
        zeroed = sem("zeroed")
        q_loaded = [sem("q_loaded0"), sem("q_loaded1")]
        k_hi_done, k_lo_done, v_hi_done, v_lo_done = sem("k_hi_done"), sem("k_lo_done"), sem("v_hi_done"), sem("v_lo_done")
        scores_done, max_done, neg_done, exp_done = sem("scores_done"), sem("max_done"), sem("neg_done"), sem("exp_done")
        inv_done, probs_done = sem("inv_done"), sem("probs_done")
        pt_done, pt_hi_done, pt_lo_done = sem("pt_done"), sem("pt_hi_done"), sem("pt_lo_done")
        pv_done, o_halves, o_done, o_stored = sem("pv_done"), sem("o_halves"), sem("o_done"), sem("o_stored")
        rows_zeroed, tail_zeroed = sem("rows_zeroed"), sem("tail_zeroed")
        piece = P * (RB * P // 2)
        pieces = SLOTS * BLOCK * D // piece // (B - 1)
        rows_flat = rows_in.rearrange("n d -> (n d)").rearrange("(k p c) -> k p c", p=P, c=RB * P // 2)

        SC = [(c * BANK, min(BANK, LC2 - c * BANK)) for c in range(4)]
        TG = [list(range(g * 4, min(g * 4 + 4, JT))) for g in range(4)]
        NG = len(TG)

        def rows(j):
            return TAIL if j == JT - 1 else P

        TURN_FROM, QUERY_FROM = 8, 16
        NQ = 2 * DT

        def start_steps():
            for u in range(NU):
                yield "unit", u
                if TURN_FROM <= u < TURN_FROM + TT:
                    yield "turn", u - TURN_FROM
                if QUERY_FROM <= u < QUERY_FROM + NQ:
                    yield "query", u - QUERY_FROM

        block = mem.enter_context(nc.Block())

        def over_batches(engine, batch):
            batch(0, 0, True)
            with engine.Fori(0, (B - 2) // 2) as i:
                batch(i * 2 + 1, 1, True)
                batch(i * 2 + 2, 0, True)
            batch(B - 1, 1, False)

        def later(b, par, p, steps):
            if p + steps < PAIRS:
                return b, par, p + steps
            return None if isinstance(b, int) and b == B - 1 else (b + 1, 1 - par, p + steps - PAIRS)

        def splits_at(b, p, kv):
            found = []
            for c in range(CHUNKS):
                free_at = pair_of_unit(LAST_OF_CHUNK[c]) + 1
                if kv and free_at == p:
                    found.append((b + 1, c + 2) if c + 2 < CHUNKS else (b + 2, c + 2 - CHUNKS))
                if kv and free_at == PAIRS and p == 0 and not (isinstance(b, int) and b == 0):
                    found.append((b + 1, c + 2 - CHUNKS))
            return found

        @block.sync
        def _(sp):
            def load_ctx(b, c):
                n = CHUNKS * b + c
                if positive(n - 1):
                    sp.wait_ge(ctx_lo_done, n - 1)
                w = DT * CHUNK_W[c]
                sp.dma_start(ctx_raw[c % 2][:, 0:w], ctx[b, :, bass.ds(DT * CW * c, w)] if isinstance(b, int)
                             else ctx[bass.ds(b, 1), :, DT * CW * c:DT * CW * c + w].rearrange("a p n -> p (a n)")
                             ).then_inc(ctx_loaded[c % 2], 16)

            def load_q(b, half):
                for part in range(2):
                    for e in range(2):
                        for copy in range(2):
                            src = q_parts[part].rearrange("(n e r) t -> e r n t", e=2, r=HD)[
                                e, :, 4 * half:4 * half + 4, bass.ds(b * LQ, LQ)]
                            row = 2 * HD * copy + HD * e
                            sp.dma_start(q_blocks[half][row:row + HD, :, part, LQ * e:LQ * e + LQ].bitcast(F32), src
                                         ).then_inc(q_loaded[half], 16)

            def batch(b, par, kv):
                if not kv:
                    tail = rows_out[(2 * PAIRS_MIN + 3) * BLOCK:, :].rearrange("(p r) d -> p (r d)", p=P)
                    w = zeros.shape[1]
                    sp.dma_start(tail.rearrange("p (r c) -> p r c", c=w),
                                 zeros[:].unsqueeze(1).to_broadcast([P, tail.shape[1] // w, w])).then_inc(tail_zeroed, 16)
                for p in range(PAIRS):
                    if p == 1 and positive(b):
                        sp.wait_ge(o_done, PAIRS * b)
                        sp.dma_start(attn_t.rearrange("(g p) n -> p g n", p=P)[:, :, bass.ds((b - 1) * LQ, LQ)],
                                     o_t[:]).then_inc(o_stored, 16)
                    if kv:
                        for k in range(pieces * p // PAIRS, pieces * (p + 1) // PAIRS):
                            sp.dma_start(rows_flat[bass.ds(b * pieces + k, 1)].rearrange("a p c -> (a p) c"), zeros[:]
                                         ).then_inc(rows_zeroed, 16)
                        for b_of, c in splits_at(b, p, kv):
                            load_ctx(b_of, c)
                        if p in (4, PAIRS - 1):
                            sp.wait_ge(scores_done, PAIRS * b + (PAIRS // 2 if p == 4 else PAIRS))
                            load_q(b + 1, 0 if p == 4 else 1)

            sp.dma_start(wk_raw, wk.rearrange("(t p) n -> p t n", p=P)).then_inc(wk_loaded, 16)
            load_ctx(0, 0)
            sp.dma_start(bk_sb[:], bk).then_inc(bias_loaded, 16)
            sp.dma_start(bv_sb[:], bv).then_inc(bias_loaded, 16)
            sp.dma_start(bq_sb[:], bq).then_inc(bias_loaded, 16)
            sp.dma_start(wv_raw, wv.rearrange("(t p) n -> p t n", p=P)).then_inc(wv_loaded, 16)
            xv = x.rearrange("(t p) d -> p t d", p=P)
            for i in range(4):
                sp.dma_start(xs[:, 2 * i:2 * i + 2, :], xv[:, 2 * i:2 * i + 2, :]).then_inc(x_loaded[i], 16)
            load_ctx(0, 1)
            sp.dma_start(wq_sb, wq.rearrange("(t p) n -> p t n", p=P)).then_inc(wq_loaded, 16)
            for c in range(2, CHUNKS):
                load_ctx(0, c)
            for n in range(NQ):
                g, half = n // 2, n % 2
                if n == NQ // 2:
                    load_ctx(1, 0)
                for part, (done, buf) in enumerate(((q_hi_done, q_hi), (q_lo_done, q_lo))):
                    sp.wait_ge(done, n + 1)
                    sp.dma_start(q_parts[part, g * P:(g + 1) * P, half * BANK:(half + 1) * BANK],
                                 buf[n % 2].bitcast(F32)).then_inc(q_stored[part][n % 2], 16)
            for part in range(2):
                for i in range(2):
                    sp.wait_ge(q_stored[part][i], NQ // 2 * 16)
            sp.wait_ge(zeroed, 5)
            load_q(0, 0)
            load_q(0, 1)
            load_ctx(1, 1)
            over_batches(sp, batch)
            sp.wait_ge(o_done, PAIRS * B)
            sp.dma_start(attn_t.rearrange("(g p) n -> p g n", p=P)[:, :, (B - 1) * LQ:], o_t[:]).then_inc(o_stored, 16)
            sp.wait_ge(o_stored, 16 * B)
            sp.wait_ge(rows_zeroed, 16 * pieces * (B - 1))
            sp.wait_ge(tail_zeroed, 16)

        @block.gpsimd
        def _(pool):
            def split_ctx(b, c, ks):
                n = CHUNKS * b + c
                w = DT * CHUNK_W[c]
                pool.wait_ge(ctx_hi_done, n + 1)
                if positive(ks):
                    pool.wait_ge(k_lo_done, ks)
                nc.gpsimd.tensor_tensor(ctx_lo[c % 2][:, 0:w], ctx_raw[c % 2][:, 0:w],
                                        ctx_hi[c % 2][:, 0:w].bitcast(F32), ALU.subtract).then_inc(ctx_lo_done, 1)

            def split_k(b, par, p, chunks):
                s, g = p % 2, p // 2
                pool.wait_ge(k_hi_done, PAIRS * b + p + 1)
                pool.wait_ge(ctx_lo_done, chunks)
                if positive(PAIRS * b + p):
                    pool.wait_ge(k_lo_done, PAIRS * b + p)
                nc.gpsimd.tensor_tensor(k_parts[64 - 64 * s:128 - 64 * s, :], k_t[par][64 * s:64 * s + 64, g, :],
                                        k_parts[64 * s:64 * s + 64, :].bitcast(F32), ALU.subtract
                                        ).then_inc(k_lo_done, 1)

            def batch(b, par, kv):
                chunks = CHUNKS * (b + 1) + (2 if isinstance(b, int) and b == 0 else 1)
                for p in range(PAIRS):
                    n = PAIRS * b + p
                    two_on = later(b, par, p, 2)
                    ks = n + 2 if later(b, par, p, 1) else PAIRS * B
                    pool.wait_ge(v_hi_done, n + 1)
                    pool.wait_ge(k_lo_done, ks)
                    nc.gpsimd.tensor_tensor(v_parts[:, :, 1, :], v[par][:, :, 64 * p:64 * p + 64],
                                            v_parts[:, :, 0, :].bitcast(F32), ALU.subtract).then_inc(v_lo_done, 1)
                    for b_of, c in splits_at(b, p, kv):
                        split_ctx(b_of, c, ks)
                        chunks = chunks + 1
                    if two_on:
                        pool.wait_ge(v_lo_done, n + 1)
                        split_k(*two_on, chunks)

            nc.gpsimd.memset(ident[:], 0.0).then_inc(ident_zero, 1)
            pool.wait_ge(ident_zero, 1)
            nc.gpsimd.affine_select(out=ident[:], in_=ident[:], compare_op=ALU.not_equal, fill=1.0, base=0,
                                    pattern=[[-1, P]], channel_multiplier=1).then_inc(ident_made, 1)
            nc.gpsimd.memset(zeros[:], 0.0).then_inc(zeroed, 1)
            for half in range(2):
                nc.gpsimd.memset(q_blocks[half][:].bitcast(F32), 0.0).then_inc(zeroed, 1)
            for par in range(2):
                pool.wait_ge(zeroed, 3 + par)
                nc.gpsimd.memset(v[par][64:128, JT - 1, :], 0.0).then_inc(zeroed, 1)
            pool.wait_ge(zeroed, 5)
            for c in range(CHUNKS + 2):
                split_ctx(c // CHUNKS, c % CHUNKS, 0)
            for p in range(2):
                split_k(0, 0, p, CHUNKS + 2)
            over_batches(pool, batch)

        @block.vector
        def _(dve):
            def split_ctx(b, c):
                n = CHUNKS * b + c
                w = DT * CHUNK_W[c]
                dve.wait_ge(ctx_loaded[c % 2], (b * (CHUNKS // 2) + c // 2 + 1) * 16)
                if positive(n - 1):
                    before, at = (b, c - 2) if c >= 2 else (b - 1, c - 2 + CHUNKS)
                    dve.wait_ge(kv_done, NU * before + LAST_OF_CHUNK[at] + 1)
                nc.vector.tensor_copy(ctx_hi[c % 2][:, 0:w], ctx_raw[c % 2][:, 0:w]).then_inc(ctx_hi_done, 1)

            def split_k(b, par, p):
                s, g = p % 2, p // 2
                if p % 2 == 0:
                    dve.wait_ge(kv_copied, NU * b + K_WHOLE[p] + 1)
                n = PAIRS * b + p
                if positive(n):
                    dve.wait_ge(scores_done, n)
                nc.vector.tensor_copy(k_parts[64 * s:64 * s + 64, :], k_t[par][64 * s:64 * s + 64, g, :]
                                      ).then_inc(k_hi_done, 1)

            def outputs(n, p):
                s, g = p % 2, p // 2
                dve.wait_ge(pv_done, n + 1)
                for part in range(2):
                    nc.vector.tensor_reduce(o_sum[:, part, :], ps_o[64 * part:64 * part + 64, 0:2].rearrange("p h c -> p c h"),
                                            AX.X, ALU.add).then_inc(o_halves, 1)
                dve.wait_ge(o_halves, (n + 1) * 2)
                for e in range(2):
                    own = slice(HD * e, HD * e + HD)
                    ins = nc.vector.scalar_tensor_tensor(
                        out=o_t[64 * s + HD * e:64 * s + HD * e + HD, g, :], in0=o_sum[own, 0, LQ * e:LQ * e + LQ],
                        scalar=bv_sb[own, p:p + 1], in1=o_sum[own, 1, LQ * e:LQ * e + LQ], op0=ALU.add, op1=ALU.add)
                ins.then_inc(o_done, 1)

            def guard(n, p):
                q = p % 2
                dve.wait_ge(scores_done, n + 1)
                nc.vector.tensor_reduce(row_max[:, q:q + 1], ps_s[:, 0:LC], AX.X, ALU.max).then_inc(max_done, 1)
                dve.wait_ge(max_done, n + 1)
                nc.vector.tensor_scalar(neg_max[:, q:q + 1], row_max[:, q:q + 1], -SCALE, None, ALU.mult
                                        ).then_inc(neg_done, 1)

            def normalise(n, p):
                q = p % 2
                dve.wait_ge(exp_done, n + 1)
                nc.vector.reciprocal(row_inv[:, q:q + 1], row_sum[:, q:q + 1]).then_inc(inv_done, 1)
                dve.wait_ge(inv_done, n + 1)
                nc.vector.tensor_scalar(probs[q], probs[q], row_inv[:, q:q + 1], None, ALU.mult
                                        ).then_inc(probs_done, 1)

            def rest(n, g):
                m, k, j = rows(TG[g][0]), len(TG[g]), TG[g][0]
                dve.wait_ge(pt_hi_done, n * NG + g + 1)
                nc.vector.tensor_tensor(probs_t[0:m, j:j + k, 1, :], ps_turned[g][0:m, 0:k, :],
                                        probs_t[0:m, j:j + k, 0, :].bitcast(F32), ALU.subtract).then_inc(pt_lo_done, 1)

            def batch(b, par, kv):
                for p in range(PAIRS):
                    n = PAIRS * b + p
                    one_on, two_on = later(b, par, p, 1), later(b, par, p, 2)
                    if p == 1 and positive(b):
                        dve.wait_ge(o_stored, 16 * b)
                    if positive(n):
                        outputs(n - 1, (p - 1) % PAIRS)
                    rest(n, 0)
                    for b_of, c in splits_at(b, p, kv):
                        split_ctx(b_of, c)
                    rest(n, 1)
                    rest(n, 2)
                    if one_on:
                        guard(n + 1, one_on[2])
                    rest(n, 3)
                    if two_on and p != PAIRS - 2:
                        split_k(*two_on)
                    if one_on:
                        normalise(n + 1, one_on[2])
                    if two_on and p == PAIRS - 2:
                        split_k(*two_on)

            def rest_of_weights(i, raw, hi, lo):
                dve.wait_ge(w_hi_done, i + 1)
                nc.vector.tensor_tensor(lo[:], raw, hi[:].bitcast(F32), ALU.subtract).then_inc(w_lo_done, 1)

            def norm_x():
                for t in range(TT):
                    dve.wait_ge(x_loaded[t // 2], 16)
                    nc.vector.bn_stats(stats[:, t, :], xs[:, t, :]).then_inc(stats_done, 1)
                    dve.wait_ge(stats_done, t + 1)
                    nc.vector.bn_aggr(mean_var[:, t, :], stats[:, t, :]).then_inc(var_done, 1)
                dve.wait_ge(var_done, TT)
                nc.vector.tensor_scalar(std[:], mean_var[:, :, 1], LN_EPS, None, ALU.add).then_inc(var_done, 1)
                dve.wait_ge(std_done, 1)
                nc.vector.reciprocal(rstd[:], std[:]).then_inc(rstd_done, 1)
                dve.wait_ge(rstd_done, 1)
                for t in range(TT):
                    nc.vector.tensor_scalar(xs[:, t, :], xs[:, t, :], mean_var[:, t, 0:1], rstd[:, t:t + 1],
                                            ALU.subtract, ALU.mult).then_inc(xn_done, 1)

            def rest_of_query(n):
                dve.wait_ge(q_hi_done, n + 1)
                if n >= 2:
                    dve.wait_ge(q_stored[1][n % 2], n // 2 * 16)
                nc.vector.scalar_tensor_tensor(
                    out=q_lo[n % 2], in0=ps_s[:, n % 4 * BANK:(n % 4 + 1) * BANK], scalar=bq_sb[:, n // 2:n // 2 + 1],
                    in1=q_hi[n % 2].bitcast(F32), op0=ALU.add, op1=ALU.subtract).then_inc(q_lo_done, 1)

            split_ctx(0, 0)
            rest_of_weights(0, wk_raw, wk_hi, wk_lo)
            rest_of_weights(1, wv_raw, wv_hi, wv_lo)
            split_ctx(0, 1)
            norm_x()
            split_ctx(0, 2)
            split_ctx(0, 3)
            dve.wait_ge(bias_loaded, 48)
            for n in range(NQ):
                if QUERY_FROM + n == LAST_OF_CHUNK[2] + 1:
                    split_ctx(0, 4)
                rest_of_query(n)
            split_ctx(0, 5)
            for c in range(2):
                split_ctx(1, c)
            dve.wait_ge(zeroed, 5)
            split_k(0, 0, 0)
            guard(0, 0)
            split_k(0, 0, 1)
            normalise(0, 0)
            over_batches(dve, batch)
            outputs(PAIRS * B - 1, PAIRS - 1)

        @block.scalar
        def _(act):
            def copy_unit(b, par, n):
                kind, c, which = UNITS[n]
                bank = (NU * par + n) % 2
                act.wait_ge(kv_done, NU * b + n + 1)
                if n == 0 and not (isinstance(b, int) and b < 2):
                    act.wait_ge(k_lo_done, PAIRS * (b - 1))
                    act.wait_ge(v_lo_done, PAIRS * (b - 1))
                if kind == "K":
                    w = CHUNK_W[c]
                    nc.scalar.activation(k_t[par][:, which, CW * c:CW * c + w], ps_kv[bank][:, 0:w], ACT.Identity,
                                         bias=bk_sb[:, which:which + 1]).then_inc(kv_copied, 1)
                else:
                    m = rows(which)
                    nc.scalar.copy(v[par][0:m, which, :], ps_kv[bank][0:m, :]).then_inc(kv_copied, 1)

            def copy_group(n, p, g):
                m, k, j = rows(TG[g][0]), len(TG[g]), TG[g][0]
                act.wait_ge(pt_done, n * NG + g + 1)
                if g == 0 and positive(n):
                    act.wait_ge(pv_done, n)
                nc.scalar.copy(probs_t[0:m, j:j + k, 0, :], ps_turned[g][0:m, 0:k, :]).then_inc(pt_hi_done, 1)

            def exponent(n, p):
                q = p % 2
                act.wait_ge(neg_done, n + 1)
                if positive(n - 1):
                    act.wait_ge(pt_done, (n - 1) * NG)
                nc.scalar.activation(probs[q], ps_s[:, 0:LC], ACT.Exp, bias=neg_max[:, q:q + 1], scale=SCALE,
                                     accum_out=row_sum[:, q:q + 1]).then_inc(exp_done, 1)

            def round_v(b, par, p):
                n = PAIRS * b + p
                if p == 0:
                    act.wait_ge(kv_copied, NU * (b + 1))
                if positive(n):
                    act.wait_ge(pv_done, n)
                nc.scalar.copy(v_parts[:, :, 0, :], v[par][:, :, 64 * p:64 * p + 64]).then_inc(v_hi_done, 1)

            def batch(b, par, kv):
                for p in range(PAIRS):
                    n = PAIRS * b + p
                    for g in range(NG):
                        copy_group(n, p, g)
                        if g == 0:
                            round_v(b, par, p)
                        if g == NG - 1 and later(b, par, p, 1):
                            exponent(n + 1, (p + 1) % PAIRS)
                        for u in (AT[p][g] if g < 2 else AT[p][2] + AT[p][3] if g == NG - 1 else []) if kv else []:
                            copy_unit(b + 1, 1 - par, u)

            for i, (loaded, raw, hi) in enumerate(((wk_loaded, wk_raw, wk_hi), (wv_loaded, wv_raw, wv_hi))):
                act.wait_ge(loaded, 16)
                nc.scalar.copy(hi[:], raw).then_inc(w_hi_done, 1)
            act.wait_ge(zeroed, 5)
            act.wait_ge(bias_loaded, 48)
            for kind, k in start_steps():
                if kind == "unit":
                    copy_unit(0, 0, k)
                    if k == TURN_FROM - 3:
                        act.wait_ge(var_done, TT + 1)
                        nc.scalar.activation(std[:], std[:], ACT.Sqrt).then_inc(std_done, 1)
                elif kind == "turn":
                    act.wait_ge(turned, k + 1)
                    nc.scalar.copy(xn_t[:, :, k * P:(k + 1) * P], (ps_pt, ps_o)[k % 2][:]).then_inc(xnt_done, 1)
                else:
                    act.wait_ge(q_done, k + 1)
                    if k >= 2:
                        act.wait_ge(q_lo_done, k - 1)
                        act.wait_ge(q_stored[0][k % 2], k // 2 * 16)
                    nc.scalar.activation(q_hi[k % 2], ps_s[:, k % 4 * BANK:(k % 4 + 1) * BANK], ACT.Identity,
                                         bias=bq_sb[:, k // 2:k // 2 + 1]).then_inc(q_hi_done, 1)
            exponent(0, 0)
            over_batches(act, batch)

        @block.tensor
        def _(pe):
            def unit(b, par, n):
                kind, c, which = UNITS[n]
                bank = ps_kv[(NU * par + n) % 2]
                if n == 0 or UNITS[n - 1][1] != c:
                    pe.wait_ge(ctx_lo_done, CHUNKS * b + c + 1)
                total = NU * b + n
                if positive(total - 1):
                    pe.wait_ge(kv_copied, total - 1)
                w = CHUNK_W[c]
                for k in range(DT):
                    hi = ctx_hi[c % 2][:, k * w:(k + 1) * w]
                    lo = ctx_lo[c % 2][:, k * w:(k + 1) * w]
                    if kind == "K":
                        dims = slice(which * P, (which + 1) * P)
                        o = bank[:, 0:w]
                        passes = [(wk_hi[:, k, dims], hi), (wk_hi[:, k, dims], lo), (wk_lo[:, k, dims], hi)]
                    else:
                        m = rows(which)
                        tile = slice(which * P - c * CW, which * P - c * CW + m)
                        o = bank[0:m, :]
                        passes = [(hi[:, tile], wv_hi[:, k, :]), (hi[:, tile], wv_lo[:, k, :]),
                                  (lo[:, tile], wv_hi[:, k, :])]
                    for i, (still, moving) in enumerate(passes):
                        last = nc.tensor.matmul(o, still, moving, start=(k == 0 and i == 0),
                                                stop=(k == DT - 1 and i == 2))
                last.then_inc(kv_done, 1)

            def scores(b, p):
                n = PAIRS * b + p
                half = p // 4
                pe.wait_ge(k_lo_done, n + 1)
                if p % 4 == 0:
                    pe.wait_ge(q_loaded[half], 128 * (b + 1))
                if positive(n):
                    pe.wait_ge(exp_done, n)
                for part in range(2):
                    for c0, w in SC:
                        last = nc.tensor.matmul(ps_s[:, c0:c0 + w], q_blocks[half][:, p % 4, part, :],
                                                k_parts[:, c0:c0 + w], start=(part == 0), stop=(part == 1))
                last.then_inc(scores_done, 1)

            def values(n):
                pe.wait_ge(pt_lo_done, NG * (n + 1))
                pe.wait_ge(v_lo_done, n + 1)
                if positive(n):
                    pe.wait_ge(o_halves, 2 * n)
                for j in range(JT):
                    m = rows(j)
                    last = nc.tensor.matmul(ps_o[:, 0:2], v_parts[0:m, j, :, :].rearrange("p a b -> p (a b)"),
                                            probs_t[0:m, j, :, :], start=(j == 0), stop=(j == JT - 1))
                last.then_inc(pv_done, 1)

            def turn(n, q, g):
                if g == 0:
                    pe.wait_ge(probs_done, n + 1)
                if g == 1:
                    if positive(n):
                        pe.wait_ge(o_halves, 2 * n)
                elif positive(n * NG + g):
                    pe.wait_ge(pt_lo_done, n * NG + [0, None, 1, 3][g])
                for i, j in enumerate(TG[g]):
                    m = rows(j)
                    last = nc.tensor.transpose(ps_turned[g][0:m, i, :], probs[q][:, j * P:j * P + m], ident[:])
                last.then_inc(pt_done, 1)

            def batch(b, par, kv):
                for p in range(PAIRS):
                    n = PAIRS * b + p
                    one_on = later(b, par, p, 1)

                    def beside(gap):
                        for u in AT[p][gap] if kv else ():
                            unit(b + 1, 1 - par, u)

                    turn(n, p % 2, 0)
                    beside(0)
                    turn(n, p % 2, 1)
                    beside(1)
                    turn(n, p % 2, 2)
                    if one_on:
                        scores(one_on[0], one_on[2])
                    turn(n, p % 2, 3)
                    beside(2)
                    values(n)
                    beside(3)

            pe.wait_ge(ident_made, 1)
            for kind, k in start_steps():
                if kind == "unit":
                    if k == 0:
                        pe.wait_ge(w_lo_done, 1)
                    elif UNITS[k][0] == "V" and UNITS[k][2] == 0:
                        pe.wait_ge(w_lo_done, 2)
                    unit(0, 0, k)
                elif kind == "turn":
                    pe.wait_ge(xn_done, k + 1)
                    if k >= 2:
                        pe.wait_ge(xnt_done, k - 1)
                    for i in range(DT):
                        last = nc.tensor.transpose((ps_pt, ps_o)[k % 2][:, i, :], xs[:, k, i * P:(i + 1) * P], ident[:])
                    last.then_inc(turned, 1)
                else:
                    g, half = k // 2, k % 2
                    if k == 0:
                        pe.wait_ge(wq_loaded, 16)
                        pe.wait_ge(xnt_done, TT)
                    if k >= 4:
                        pe.wait_ge(q_lo_done, k - 3)
                    for i in range(DT):
                        last = nc.tensor.matmul(ps_s[:, k % 4 * BANK:(k % 4 + 1) * BANK], wq_sb[:, i, g * P:(g + 1) * P],
                                                xn_t[:, i, half * BANK:(half + 1) * BANK],
                                                start=(i == 0), stop=(i == DT - 1))
                    last.then_inc(q_done, 1)
            pe.wait_ge(q_lo_done, NQ)
            scores(0, 0)
            over_batches(pe, batch)


def linear_attention(nc, ident, x, attn_t, wout, bout, lwq, lwk, lwv, lwo, router,
                     x2, weight, place, slot_expert, slot_pairs, rows_in):
    with ExitStack() as mem:
        def sb(name, shape, dt=F32):
            return mem.enter_context(nc.sbuf_tensor(name, shape, dt))

        def sem(name):
            return mem.enter_context(nc.semaphore(name))

        xs = sb("xs2", [P, TT, D])
        o_t = sb("o_t2", [P, DT, NT])
        xn = sb("xn2", [P, TT, D])
        xn_t = sb("xn_t2", [P, DT, NT])
        w_sb = {n: sb(f"{n}_sb", [P, DT, D]) for n in ("wout", "lwq", "lwk", "lwv", "lwo")}
        router_sb = sb("router_sb", [P, DT, E])
        bout_sb = sb("bout_sb", [P, D])
        stats = sb("stats2", [P, TT, 6])
        mean_var = sb("mean_var2", [P, TT, 2])
        std = sb("std2", [P, TT])
        rstd = sb("rstd2", [P, TT])
        q_t = sb("lq_t", [P, DT, NT])
        k_f = sb("lk", [P, TT, D])
        low = [sb(f"low{i}", [P, BANK]) for i in range(2)]
        expo = [sb(f"expo{i}", [P, BANK]) for i in range(2)]
        v_two = [sb(f"v_two{i}", [P, DT, 2, P]) for i in range(2)]
        ones_two = sb("ones_two", [P, 2])
        same_head = sb("same_head", [P, P])
        head_of = sb("head_of", [P, DT])
        kv_blocks = [sb(f"kv_blocks{i}", [P, DT, 2, P + DT]) for i in range(2)]
        den = [sb(f"den{i}", [P, 2, 2, DT]) for i in range(2)]
        att = [sb(f"att{i}", [P, D]) for i in range(2)]
        att_t = [sb(f"att_t{i}", [P, DT, P]) for i in range(2)]
        logits = sb("logits", [P, TT, E])
        prob = sb("prob", [P, TT, E])
        top = weight
        top_at = sb("top_at", [P, TT, 8], U32)
        top_f = sb("top_f", [P, TT, 8])
        lane = sb("lane", [P, E])
        picked = sb("picked", [P, 2, TT, E])
        chosen = sb("chosen", [P, TT, E])
        before = sb("before", [P, P])
        all_ones = sb("all_ones", [P, P])
        count = sb("count", [P, TT + 1, E])
        blocks = sb("blocks", [P, E])
        end = sb("end", [P, E + 1])
        first = sb("first", [P, E])
        rank = sb("rank", [P, TT, E])
        at = sb("at", [P, 2, TT, E])
        place_f = sb("place_f", [P, 2, TT])
        slot = sb("slot", [P, SLOTS + 1])
        slot_f = sb("slot_f", [P, SLOTS + 1])
        pair_f = sb("pair_f", [P, PAIRS_MAX])
        pairs_f = sb("pairs_f", [P, 1])
        small = sb("small", [P, 4, TT])
        ps = [mem.enter_context(nc.psum_tensor(f"ps_l{i}", [P, BANK], F32)) for i in range(4)]
        ps_kv = mem.enter_context(nc.psum_tensor("ps_lkv", [P, 2, BANK], F32))
        ps_heads = mem.enter_context(nc.psum_tensor("ps_lheads", [P, 2, BANK], F32))

        def norm_rows(eng, t, source_ready, source, sems):
            stats_done, aggr_done, var_done, std_done, rstd_done, xn_done = sems
            if t < TT:
                source_ready(t)
                nc.vector.bn_stats(stats[:, t, :], source[:, t, :]).then_inc(stats_done, 1)
                eng.wait_ge(stats_done, t + 1)
                nc.vector.bn_aggr(mean_var[:, t, :], stats[:, t, :]).then_inc(aggr_done, 1)
                eng.wait_ge(aggr_done, t + 1)
                nc.vector.tensor_scalar(std[:, t:t + 1], mean_var[:, t, 1:2], LN_EPS, None, ALU.add).then_inc(var_done, 1)
            if t >= 1:
                r = t - 1
                eng.wait_ge(std_done, r + 1)
                nc.vector.reciprocal(rstd[:, r:r + 1], std[:, r:r + 1]).then_inc(rstd_done, 1)
                eng.wait_ge(rstd_done, r + 1)
                nc.vector.tensor_scalar(xn[:, r, :], source[:, r, :], mean_var[:, r, 0:1], rstd[:, r:r + 1],
                                        ALU.subtract, ALU.mult).then_inc(xn_done, 1)

        with ExitStack() as stage:
            def sem(name):
                return stage.enter_context(nc.semaphore("c1_" + name))

            o_loaded = [sem(f"o_loaded{i}") for i in range(4)]
            x_loaded = [sem(f"x_loaded{i}") for i in range(4)]
            bias_loaded = sem("bias_loaded")
            w_loaded = {n: sem(f"{n}_loaded") for n in w_sb}
            router_loaded = sem("router_loaded")
            x_biased, proj_done, x_added = sem("x_biased"), sem("proj_done"), sem("x_added")
            norm_sems = [sem(n) for n in ("stats", "aggr", "var", "std", "rstd", "xn")]
            turned, xnt_done = sem("turned"), sem("xnt_done")
            block = stage.enter_context(nc.Block())

            @block.sync
            def _(sp):
                sp.dma_start(w_sb["wout"][:], wout.rearrange("(t p) n -> p t n", p=P)).then_inc(w_loaded["wout"], 16)
                for i in range(4):
                    part = slice(i * NT // 4, (i + 1) * NT // 4)
                    sp.dma_start(o_t[:, :, part], attn_t.rearrange("(g p) n -> p g n", p=P)[:, :, part]
                                 ).then_inc(o_loaded[i], 16)
                    if i == 0:
                        sp.dma_start(bout_sb[:], bout).then_inc(bias_loaded, 16)
                    sp.dma_start(xs[:, 2 * i:2 * i + 2, :], x.rearrange("(t p) d -> p t d", p=P)[:, 2 * i:2 * i + 2, :]
                                 ).then_inc(x_loaded[i], 16)
                for name, w in (("lwq", lwq), ("lwk", lwk), ("lwv", lwv), ("lwo", lwo)):
                    sp.dma_start(w_sb[name][:], w.rearrange("(t p) n -> p t n", p=P)).then_inc(w_loaded[name], 16)
                sp.dma_start(router_sb[:], router.rearrange("p (t e) -> p t e", t=DT)).then_inc(router_loaded, 16)
                for name in ("lwq", "lwk", "lwv", "lwo"):
                    sp.wait_ge(w_loaded[name], 16)
                sp.wait_ge(router_loaded, 16)

            @block.scalar
            def _(act):
                for t in range(TT + 1):
                    if t < TT:
                        act.wait_ge(norm_sems[2], t + 1)
                        nc.scalar.activation(std[:, t:t + 1], std[:, t:t + 1], ACT.Sqrt).then_inc(norm_sems[3], 1)
                    if t >= 1:
                        act.wait_ge(turned, t)
                        nc.scalar.copy(xn_t[:, :, (t - 1) * P:t * P],
                                       ps[2 + (t - 1) % 2][:].rearrange("p (k c) -> p k c", k=DT)).then_inc(xnt_done, 1)

            @block.vector
            def _(dve):
                def add_bias(t):
                    dve.wait_ge(x_loaded[t // 2], 16)
                    nc.vector.tensor_tensor(xs[:, t, :], xs[:, t, :], bout_sb[:], ALU.add).then_inc(x_biased, 1)

                def ready(t):
                    if t + 2 < TT:
                        add_bias(t + 2)
                    dve.wait_ge(proj_done, t + 1)
                    dve.wait_ge(x_biased, t + 1)
                    nc.vector.tensor_tensor(x2[:, t, :], ps[t % 2][:], xs[:, t, :], ALU.add).then_inc(x_added, 1)
                    dve.wait_ge(x_added, t + 1)

                dve.wait_ge(bias_loaded, 16)
                for t in range(2):
                    add_bias(t)
                for t in range(TT + 1):
                    norm_rows(dve, t, ready, x2, norm_sems)

            @block.tensor
            def _(pe):
                pe.wait_ge(w_loaded["wout"], 16)
                for t in range(TT + 2):
                    if t < TT:
                        pe.wait_ge(o_loaded[t * 4 // TT], 16)
                        if t >= 2:
                            pe.wait_ge(x_added, t - 1)
                        for g in range(DT):
                            last = nc.tensor.matmul(ps[t % 2][:], o_t[:, g, t * P:(t + 1) * P], w_sb["wout"][:, g, :],
                                                    start=(g == 0), stop=(g == DT - 1))
                        last.then_inc(proj_done, 1)
                    if t >= 2:
                        r = t - 2
                        pe.wait_ge(norm_sems[5], r + 1)
                        if r >= 2:
                            pe.wait_ge(xnt_done, r - 1)
                        for k in range(DT):
                            last = nc.tensor.transpose(ps[2 + r % 2][:, k * P:(k + 1) * P], xn[:, r, k * P:(k + 1) * P],
                                                       ident[:])
                        last.then_inc(turned, 1)

        with ExitStack() as stage:
            def sem(name):
                return stage.enter_context(nc.semaphore("c2_" + name))

            made, low_done, expo_done, mapped = sem("made"), sem("low_done"), sem("expo_done"), sem("mapped")
            v_made, v_copied, zero_done, consts_done = sem("v_made"), sem("v_copied"), sem("zero_done"), sem("consts_done")
            kv_done, blocks_done, heads_done, den_done, inv_done, att_done = (
                sem("kv_done"), sem("blocks_done"), sem("heads_done"), sem("den_done"), sem("inv_done"), sem("att_done"))
            att_turned, att_copied = sem("att_turned"), sem("att_copied")
            proj_done, x_added = sem("proj_done"), sem("x_added")
            norm_sems = [sem(n) for n in ("stats", "aggr", "var", "std", "rstd", "xn")]
            turned, xnt_done = sem("turned"), sem("xnt_done")
            block = stage.enter_context(nc.Block())
            NF = 2 * TT
            ps_map = [ps_heads[:, 0], ps_heads[:, 1], ps[2][:], ps[3][:]]
            ps_v, ps_ks, ps_turn, ps_proj = ps[0], ps[1], ps[2], ps[3]
            kv_of = [ps_kv[:, i, :].rearrange("p (n c) -> p n c", n=DT) for i in range(2)]
            heads = ps_heads[:, :, 0:2 * (P + DT)].rearrange("p i (g c) -> p i g c", g=2)
            KV, HEADS, ATT_T, PROJ, TURN = 1, 2, 3, 4, 6

            def mapped_to(n):
                if n < TT:
                    return q_t[:, n // 2, (n % 2) * BANK:(n % 2 + 1) * BANK]
                return k_f[:, n - TT, :]

            @block.tensor
            def _(pe):
                for n in range(NF):
                    if n >= 4:
                        pe.wait_ge(mapped, n - 3)
                    for k in range(DT):
                        if n < TT:
                            g, half = n // 2, n % 2
                            still, moving = w_sb["lwq"][:, k, g * P:(g + 1) * P], xn_t[:, k, half * BANK:(half + 1) * BANK]
                        else:
                            t = n - TT
                            still, moving = xn_t[:, k, t * P:(t + 1) * P], w_sb["lwk"][:, k, :]
                        last = nc.tensor.matmul(ps_map[n % 4], still, moving, start=(k == 0), stop=(k == DT - 1))
                    last.then_inc(made, 1)
                for t in range(TT + TURN):
                    if t < TT:
                        if t >= 1:
                            pe.wait_ge(v_copied, 2 * t)
                        for k in range(DT):
                            last = nc.tensor.matmul(ps_v[:], xn_t[:, k, t * P:(t + 1) * P], w_sb["lwv"][:, k, :],
                                                    start=(k == 0), stop=(k == DT - 1))
                        last.then_inc(v_made, 1)
                    r = t - KV
                    if 0 <= r < TT:
                        pe.wait_ge(mapped, TT + r + 1)
                        pe.wait_ge(v_copied, 2 * r + 2)
                        pe.wait_ge(consts_done, 1)
                        if r >= 1:
                            pe.wait_ge(blocks_done, r)
                        for g in range(DT):
                            keys = k_f[:, r, g * P:(g + 1) * P]
                            nc.tensor.matmul(ps_kv[:, g // 2, (g % 2) * 2 * P:(g % 2 + 1) * 2 * P], keys,
                                             v_two[r % 2][:, g].rearrange("p b c -> p (b c)"),
                                             start=True, stop=True, skip_group_check=True)
                            last = nc.tensor.matmul(ps_ks[:, 2 * g:2 * g + 2], keys, ones_two[:],
                                                    start=True, stop=True, skip_group_check=True)
                        last.then_inc(kv_done, 1)
                    r = t - HEADS
                    if 0 <= r < TT:
                        pe.wait_ge(blocks_done, r + 1)
                        if r == 0:
                            pe.wait_ge(mapped, NF)
                        else:
                            pe.wait_ge(att_done, r)
                        for b in range(2):
                            for g in range(DT):
                                last = nc.tensor.matmul(heads[LQ * b:LQ * b + LQ, g // 2, g % 2, :],
                                                        q_t[:, g, (2 * r + b) * LQ:(2 * r + b + 1) * LQ],
                                                        kv_blocks[r % 2][:, g, b, :],
                                                        start=True, stop=True, skip_group_check=True)
                        last.then_inc(heads_done, 1)
                    r = t - ATT_T
                    if 0 <= r < TT:
                        pe.wait_ge(att_done, r + 1)
                        if r - (TURN - ATT_T) >= 1:
                            pe.wait_ge(xnt_done, r - (TURN - ATT_T))
                        if r >= 1:
                            pe.wait_ge(att_copied, r)
                        for k in range(DT):
                            last = nc.tensor.transpose(ps_turn[:, k * P:(k + 1) * P], att[r % 2][:, k * P:(k + 1) * P],
                                                       ident[:])
                        last.then_inc(att_turned, 1)
                    r = t - PROJ
                    if 0 <= r < TT:
                        pe.wait_ge(att_copied, r + 1)
                        if r >= 1:
                            pe.wait_ge(x_added, r)
                        for g in range(DT):
                            last = nc.tensor.matmul(ps_proj[:], att_t[r % 2][:, g, :], w_sb["lwo"][:, g, :],
                                                    start=(g == 0), stop=(g == DT - 1))
                        last.then_inc(proj_done, 1)
                    r = t - TURN
                    if 0 <= r < TT:
                        pe.wait_ge(norm_sems[5], r + 1)
                        pe.wait_ge(att_copied, min(TT, r + 1 + TURN - ATT_T))
                        if r >= 1:
                            pe.wait_ge(xnt_done, r)
                        for k in range(DT):
                            last = nc.tensor.transpose(ps_turn[:, k * P:(k + 1) * P], xn[:, r, k * P:(k + 1) * P],
                                                       ident[:])
                        last.then_inc(turned, 1)

            @block.vector
            def _(dve):
                for i in range(2):
                    nc.vector.memset(v_two[i][:], 0.0).then_inc(zero_done, 1)
                for buf in (same_head, head_of, ones_two):
                    nc.vector.memset(buf[:], 0.0).then_inc(zero_done, 1)
                dve.wait_ge(zero_done, 5)
                for h in range(DT):
                    nc.vector.memset(same_head[HD * h:HD * h + HD, HD * h:HD * h + HD], 1.0)
                    nc.vector.memset(head_of[HD * h:HD * h + HD, h:h + 1], 1.0)
                for b in range(2):
                    last = nc.vector.memset(ones_two[LQ * b:LQ * b + LQ, b:b + 1], 1.0)
                last.then_inc(consts_done, 1)
                for n in range(NF + 1):
                    if n < NF:
                        dve.wait_ge(made, n + 1)
                        if n >= 2:
                            dve.wait_ge(expo_done, n - 1)
                        nc.vector.tensor_scalar(low[n % 2][:], ps_map[n % 4], 0.0, None, ALU.min).then_inc(low_done, 1)
                    if n >= 1:
                        r = n - 1
                        dve.wait_ge(expo_done, r + 1)
                        nc.vector.scalar_tensor_tensor(out=mapped_to(r), in0=ps_map[r % 4], scalar=0.0,
                                                       in1=expo[r % 2][:], op0=ALU.max, op1=ALU.add).then_inc(mapped, 1)

                def ready(t):
                    dve.wait_ge(proj_done, t + 1)
                    nc.vector.tensor_tensor(x2[:, t, :], ps_proj[:], x2[:, t, :], ALU.add).then_inc(x_added, 1)
                    dve.wait_ge(x_added, t + 1)

                dve.wait_ge(consts_done, 1)
                for t in range(TT + TURN):
                    r = t - KV
                    if 0 <= r < TT:
                        dve.wait_ge(kv_done, r + 1)
                        if r >= 2:
                            dve.wait_ge(heads_done, r - 1)
                        for i in range(2):
                            nc.vector.tensor_tensor(
                                kv_blocks[r % 2][:, 2 * i:2 * i + 2, :, 0:P].rearrange("p g b c -> p (g b) c"), kv_of[i],
                                same_head[:].unsqueeze(1).to_broadcast([P, DT, P]), ALU.mult)
                        nc.vector.tensor_tensor(
                            kv_blocks[r % 2][:, :, :, P:].rearrange("p g b c -> p (g b) c"),
                            head_of[:].unsqueeze(1).to_broadcast([P, 2 * DT, DT]),
                            ps_ks[:, 0:2 * DT].unsqueeze(2).to_broadcast([P, 2 * DT, DT]), ALU.mult).then_inc(blocks_done, 1)
                    r = t - HEADS
                    if 0 <= r < TT:
                        dve.wait_ge(heads_done, r + 1)
                        nc.vector.tensor_scalar(den[r % 2][:], heads[:, :, :, P:], LIN_EPS, None, ALU.add
                                                ).then_inc(den_done, 1)
                        dve.wait_ge(den_done, r + 1)
                        nc.vector.reciprocal(den[r % 2][:], den[r % 2][:]).then_inc(inv_done, 1)
                        dve.wait_ge(inv_done, r + 1)
                        if r >= 2:
                            dve.wait_ge(att_turned, r - 1)
                        for i in range(2):
                            last = nc.vector.tensor_tensor(
                                att[r % 2][:, i * 2 * P:(i + 1) * 2 * P].rearrange("p (g h c) -> p g h c", g=2, h=DT),
                                heads[:, i, :, 0:P].rearrange("p g (h c) -> p g h c", h=DT),
                                den[r % 2][:, i].unsqueeze(3).to_broadcast([P, 2, DT, HD]), ALU.mult)
                        last.then_inc(att_done, 1)
                    r = t - PROJ
                    if 0 <= r <= TT:
                        norm_rows(dve, r, ready, x2, norm_sems)

            @block.scalar
            def _(act):
                for n in range(NF):
                    act.wait_ge(low_done, n + 1)
                    if n >= 2:
                        act.wait_ge(mapped, n - 1)
                    nc.scalar.activation(expo[n % 2][:], low[n % 2][:], ACT.Exp).then_inc(expo_done, 1)
                act.wait_ge(zero_done, 5)
                for t in range(TT + TURN):
                    if t < TT:
                        act.wait_ge(v_made, t + 1)
                        if t >= 2:
                            act.wait_ge(kv_done, t - 1)
                        for b in range(2):
                            nc.scalar.copy(v_two[t % 2][LQ * b:LQ * b + LQ, :, b, :],
                                           ps_v[LQ * b:LQ * b + LQ, :].rearrange("p (g c) -> p g c", g=DT)
                                           ).then_inc(v_copied, 1)
                    r = t - ATT_T
                    if 0 <= r < TT:
                        act.wait_ge(att_turned, r + 1)
                        if r >= 2:
                            act.wait_ge(proj_done, r - 1)
                        nc.scalar.copy(att_t[r % 2][:], ps_turn[:].rearrange("p (k c) -> p k c", k=DT)
                                       ).then_inc(att_copied, 1)
                    r = t - PROJ
                    if 0 <= r < TT:
                        act.wait_ge(norm_sems[2], r + 1)
                        nc.scalar.activation(std[:, r:r + 1], std[:, r:r + 1], ACT.Sqrt).then_inc(norm_sems[3], 1)
                    r = t - TURN
                    if 0 <= r < TT:
                        act.wait_ge(turned, r + 1)
                        nc.scalar.copy(xn_t[:, :, r * P:(r + 1) * P], ps_turn[:].rearrange("p (k c) -> p k c", k=DT)
                                       ).then_inc(xnt_done, 1)

            @block.gpsimd
            def _(pool):
                nc.gpsimd.iota(lane[:], pattern=[[1, E]], base=0, channel_multiplier=0,
                               allow_small_or_imprecise_dtypes=True)

        with ExitStack() as stage:
            def sem(name):
                return stage.enter_context(nc.semaphore("c3_" + name))

            gated, gmax_done, gneg_done, gexp_done, ginv_done, prob_done = (
                sem("gated"), sem("gmax"), sem("gneg"), sem("gexp"), sem("ginv"), sem("prob"))
            top_done, at_done, atf_done, picked_done, chosen_done = (
                sem("top"), sem("at"), sem("atf"), sem("picked"), sem("chosen"))
            consts, step, ranked, placed, dispatched = sem("consts"), sem("step"), sem("ranked"), sem("placed"), sem("dispatched")
            block = stage.enter_context(nc.Block())

            @block.tensor
            def _(pe):
                for t in range(TT):
                    for k in range(DT):
                        last = nc.tensor.matmul(ps[2][:, t * E:(t + 1) * E], xn_t[:, k, t * P:(t + 1) * P],
                                                router_sb[:, k, :], start=(k == 0), stop=(k == DT - 1))
                last.then_inc(gated, 1)
                pe.wait_ge(consts, 3)
                pe.wait_ge(chosen_done, 1)
                picks = chosen[:].rearrange("p t e -> p (t e)")
                nc.tensor.matmul(ps[0][:, 0:TT * E], before[:], picks, start=True, stop=True)
                nc.tensor.matmul(ps[1][:, 0:TT * E], all_ones[:], picks, start=True, stop=True).then_inc(ranked, 1)

            @block.vector
            def _(dve):
                dve.wait_ge(gated, 1)
                nc.vector.tensor_reduce(small[:, 0, :], ps[2][:, 0:TT * E].rearrange("p (t e) -> p t e", t=TT), AX.X,
                                        ALU.max).then_inc(gmax_done, 1)
                dve.wait_ge(gmax_done, 1)
                nc.vector.tensor_scalar(small[:, 1, :], small[:, 0, :], -1.0, None, ALU.mult).then_inc(gneg_done, 1)
                dve.wait_ge(gexp_done, TT)
                nc.vector.reciprocal(small[:, 3, :], small[:, 2, :]).then_inc(ginv_done, 1)
                dve.wait_ge(ginv_done, 1)
                nc.vector.tensor_tensor(prob[:], logits[:], small[:, 3, :].unsqueeze(2).to_broadcast([P, TT, E]),
                                        ALU.mult).then_inc(prob_done, 1)
                dve.wait_ge(prob_done, 1)
                for t in range(TT):
                    nc.vector.max(top[:, t, :], prob[:, t, :]).then_inc(top_done, 1)
                    dve.wait_ge(top_done, t + 1)
                    nc.vector.max_index(top_at[:, t, :], top[:, t, :], prob[:, t, :]).then_inc(at_done, 1)
                dve.wait_ge(at_done, TT)
                nc.vector.tensor_copy(top_f[:], top_at[:]).then_inc(atf_done, 1)
                dve.wait_ge(atf_done, 1)
                for k in range(2):
                    nc.vector.tensor_tensor(picked[:, k], lane[:].unsqueeze(1).to_broadcast([P, TT, E]),
                                            top_f[:, :, k:k + 1].to_broadcast([P, TT, E]), ALU.is_equal
                                            ).then_inc(picked_done, 1)
                dve.wait_ge(picked_done, 2)
                nc.vector.tensor_tensor(chosen[:], picked[:, 0], picked[:, 1], ALU.add).then_inc(chosen_done, 1)
                steps = [0]

                def then(ins):
                    steps[0] += 1
                    ins.then_inc(step, 1)
                    dve.wait_ge(step, steps[0])

                then(nc.vector.memset(count[:, 0, :], 0.0))
                then(nc.vector.memset(end[:, 0:1], 0.0))
                dve.wait_ge(ranked, 1)
                for t in range(TT):
                    then(nc.vector.tensor_tensor(count[:, t + 1, :], ps[1][:, t * E:(t + 1) * E], count[:, t, :], ALU.add))
                then(nc.vector.tensor_scalar(blocks[:], count[:, TT, :], 0.0, None, ALU.is_gt))
                for j in range(1, NT // BLOCK):
                    then(nc.vector.scalar_tensor_tensor(out=blocks[:], in0=count[:, TT, :], scalar=float(BLOCK * j),
                                                        in1=blocks[:], op0=ALU.is_gt, op1=ALU.add))
                for e in range(E):
                    then(nc.vector.tensor_tensor(end[:, e + 1:e + 2], end[:, e:e + 1], blocks[:, e:e + 1], ALU.add))
                then(nc.vector.tensor_scalar(first[:], end[:, 0:E], float(BLOCK), None, ALU.mult))
                then(nc.vector.tensor_tensor(rank[:], ps[0][:, 0:TT * E].rearrange("p (t e) -> p t e", t=TT),
                                             count[:, 0:TT, :], ALU.add))
                then(nc.vector.tensor_tensor(rank[:], rank[:], first[:].unsqueeze(1).to_broadcast([P, TT, E]), ALU.add))
                for k in range(2):
                    then(nc.vector.tensor_tensor(at[:, k], rank[:], picked[:, k], ALU.mult))
                then(nc.vector.tensor_reduce(place_f[:], at[:], AX.X, ALU.add))
                nc.vector.tensor_copy(place[:], place_f[:]).then_inc(placed, 1)
                then(nc.vector.tensor_scalar(slot_f[:], slot[:], end[:, 1:2], None, ALU.is_ge))
                for e in range(1, E - 1):
                    then(nc.vector.scalar_tensor_tensor(out=slot_f[:], in0=slot[:], scalar=end[:, e + 1:e + 2],
                                                        in1=slot_f[:], op0=ALU.is_ge, op1=ALU.add))
                then(nc.vector.tensor_copy(slot_expert[:], slot_f[0:1, :]))
                then(nc.vector.tensor_scalar(pair_f[:], slot[:, 0:PAIRS_MAX], 2.0, 3.0, ALU.mult, ALU.add))
                then(nc.vector.tensor_scalar(pair_f[:], pair_f[:], end[:, E:E + 1], None, ALU.is_lt))
                then(nc.vector.tensor_reduce(pairs_f[:], pair_f[:], AX.X, ALU.add))
                then(nc.vector.tensor_copy(slot_pairs[:], pairs_f[0:1, :]))

            @block.gpsimd
            def _(pool):
                nc.gpsimd.memset(all_ones[:], 1.0).then_inc(consts, 1)
                nc.gpsimd.iota(slot[:], pattern=[[1, SLOTS + 1]], base=0, channel_multiplier=0,
                               allow_small_or_imprecise_dtypes=True).then_inc(consts, 1)
                pool.wait_ge(consts, 2)
                nc.gpsimd.affine_select(out=before[:], in_=all_ones[:], compare_op=ALU.is_gt, fill=0.0, base=0,
                                        pattern=[[1, P]], channel_multiplier=-1).then_inc(consts, 1)
                pool.wait_ge(placed, 1)
                for t in range(TT):
                    for k in range(2):
                        nc.gpsimd.indirect_dma_start(
                            out=rows_in, out_offset=bass.IndirectOffsetOnAxis(ap=place[:, k, t:t + 1], axis=0),
                            in_=xn[:, t, :], in_offset=None).then_inc(dispatched, 16)
                pool.wait_ge(dispatched, 16 * 2 * TT)

            @block.scalar
            def _(act):
                act.wait_ge(gneg_done, 1)
                for t in range(TT):
                    nc.scalar.activation(logits[:, t, :], ps[2][:, t * E:(t + 1) * E], ACT.Exp, bias=small[:, 1, t:t + 1],
                                         accum_out=small[:, 2, t:t + 1]).then_inc(gexp_done, 1)




def experts(nc, ident, x2, weight, place, slot_expert, slot_pairs, rows_in, rows_out, w1, w2, out):
    with ExitStack() as mem:
        def sb(name, shape, dt=F32):
            return mem.enter_context(nc.sbuf_tensor(name, shape, dt))

        def sem(name):
            return mem.enter_context(nc.semaphore("e_" + name))

        RAW = 4
        TAKEN = 4
        rows = [sb(f"rows{i}", [P, RB, D]) for i in range(2)]
        rows_hi = [sb(f"rows_hi{i}", [P, DT, BLOCK], F32R) for i in range(2)]
        rows_lo = [sb(f"rows_lo{i}", [P, DT, BLOCK], F32R) for i in range(2)]
        w1_raw = [sb(f"w1_raw{i}", [P, DT, 2, P]) for i in range(RAW)]
        w1_hi = [sb(f"w1_hi{i}", [P, DT, 2, P], F32R) for i in range(RAW)]
        w1_lo = [sb(f"w1_lo{i}", [P, DT, 2, P], F32R) for i in range(RAW)]
        w2_raw = [sb(f"w2_raw{i}", [P, WC, D]) for i in range(2)]
        w2_hi = [sb(f"w2_hi{i}", [P, IT, D], F32R) for i in range(2)]
        w2_lo = [sb(f"w2_lo{i}", [P, IT, D], F32R) for i in range(2)]
        silu = [sb(f"silu{i}", [P, BLOCK]) for i in range(2)]
        y = [sb(f"y{i}", [P, BLOCK]) for i in range(2)]
        y_hi = [sb(f"y_hi{i}", [P, IT, BLOCK], F32R) for i in range(2)]
        y_lo = [sb(f"y_lo{i}", [P, IT, BLOCK], F32R) for i in range(2)]
        down = sb("down", [P, RB, D])
        taken = [sb(f"taken{i}", [P, D]) for i in range(TAKEN)]
        ps_up = [mem.enter_context(nc.psum_tensor(f"ps_up{i}", [P, 2, BLOCK], F32)) for i in range(4)]
        ps_r = [mem.enter_context(nc.psum_tensor(f"ps_r{i}", [P, DT, P], F32)) for i in range(2)]
        ps_d = [mem.enter_context(nc.psum_tensor(f"ps_d{i}", [P, D], F32)) for i in range(2)]

        rows_loaded = [sem("rows_loaded0"), sem("rows_loaded1")]
        w1_loaded = [sem(f"w1_loaded{i}") for i in range(RAW)]
        w2_loaded = [sem(f"w2_loaded{i}") for i in range(2)]
        w1_hi_done, w1_lo_done, w2_hi_done, w2_lo_done = sem("w1_hi"), sem("w1_lo"), sem("w2_hi"), sem("w2_lo")
        rows_turned, rows_hi_done, rows_lo_done = sem("rows_turned"), sem("rows_hi"), sem("rows_lo")
        up_done, silu_done, y_done, y_hi_done, y_lo_done = sem("up"), sem("silu"), sem("y"), sem("y_hi"), sem("y_lo")
        down_done, down_free = sem("down"), sem("down_free")
        down_stored = [sem(f"down_stored{i}") for i in range(RB)]
        taken_done = [sem(f"taken{i}") for i in range(TAKEN)]
        weighed, stored, all_stored = sem("weighed"), sem("stored"), sem("all_stored")
        stored_mark = sb("stored_mark", [P, 1])
        AHEAD = 2
        NW2 = IT // WC

        block = mem.enter_context(nc.Block())

        def over_slots(engine, slot):
            pairs = engine.value_load(slot_pairs[0:1, 0:1], min_val=PAIRS_MIN, max_val=PAIRS_MAX)
            slot(0, 0, 0, False)
            with engine.Fori(0, PAIRS_MAX) as i:
                with engine.If(i < pairs):
                    slot(i * 2 + 1, 1, i, False)
                    slot(i * 2 + 2, 0, i + 1, False)
            slot(pairs * 2 + 1, 1, pairs, False)
            slot(pairs * 2 + 2, 0, pairs + 1, True)
            return pairs * 2 + 2

        @block.sync
        def _(sp):
            def slot(s, par, turn, last):
                e = sp.value_load(slot_expert[0:1, bass.ds(s, 1)], min_val=0, max_val=E - 1)
                if positive(s - 1):
                    sp.wait_ge(rows_turned, (s - 1) * RB)
                sp.dma_start(rows[par][:], rows_in[bass.ds(s * BLOCK, BLOCK), :].rearrange("(r p) d -> p r d", p=P)
                             ).then_inc(rows_loaded[par], 16)
                for u in range(IT):
                    n = IT * s + u
                    if positive(n - RAW + 1):
                        sp.wait_ge(w1_lo_done, n - RAW + 1)
                    sp.dma_start(w1_raw[u % RAW][:], w1[bass.ds(e, 1), u].rearrange(
                        "a p (t s c) -> (a p) t s c", t=DT, s=2)).then_inc(w1_loaded[u % RAW], 16)
                    if u % WC == WC - 1:
                        c = u // WC
                        m = NW2 * s + c
                        if positive(m - 1):
                            sp.wait_ge(w2_lo_done, m - 1)
                        sp.dma_start(w2_raw[c % 2][:], w2[bass.ds(e, 1), c].rearrange(
                            "a p (k n) -> (a p) k n", k=WC)).then_inc(w2_loaded[c % 2], 16)

            over_slots(sp, slot)
            ov = out.rearrange("(t p) d -> p t d", p=P)
            for t in range(TT):
                sp.wait_ge(weighed, 2 * t + 2)
                sp.dma_start(ov[:, t, :], x2[:, t, :]).then_inc(stored, 16)
            sp.wait_ge(stored, 16 * TT)

        @block.gpsimd
        def _(pool):
            def slot(s, par, turn, last):
                for c in range(NW2):
                    pool.wait_ge(w2_hi_done, NW2 * s + c + 1)
                    nc.gpsimd.tensor_tensor(w2_lo[par][:, WC * c:WC * c + WC, :], w2_raw[c % 2][:],
                                            w2_hi[par][:, WC * c:WC * c + WC, :].bitcast(F32), ALU.subtract
                                            ).then_inc(w2_lo_done, 1)

            end = over_slots(pool, slot)
            for r in range(RB):
                pool.wait_ge(down_stored[r], 16 * (end + 1))
            nc.gpsimd.tensor_tensor(stored_mark[:], ident[:, 0:1], ident[:, 1:2], ALU.subtract).then_inc(all_stored, 1)
            pool.wait_ge(all_stored, 1)
            for t in range(TT):
                for k in range(2):
                    n = 2 * t + k
                    if n >= TAKEN:
                        pool.wait_ge(weighed, n - TAKEN + 1)
                    nc.gpsimd.indirect_dma_start(
                        out=taken[n % TAKEN][:], out_offset=None, in_=rows_out,
                        in_offset=bass.IndirectOffsetOnAxis(ap=place[:, k, t:t + 1], axis=0)).then_inc(taken_done[n % TAKEN], 16)

        @block.scalar
        def _(act):
            def split_w1(s, u):
                n = IT * s + u
                act.wait_ge(w1_loaded[u % RAW], 16 * (s * (IT // RAW) + u // RAW + 1))
                if positive(n - RAW + 1):
                    act.wait_ge(up_done, n - RAW + 1)
                nc.scalar.copy(w1_hi[u % RAW][:], w1_raw[u % RAW][:]).then_inc(w1_hi_done, 1)

            def split_w2(s, par, c):
                act.wait_ge(w2_loaded[c % 2], 16 * (s * (NW2 // 2) + c // 2 + 1))
                if c == 0 and positive(s - 1):
                    act.wait_ge(down_done, RB * (s - 1))
                nc.scalar.copy(w2_hi[par][:, WC * c:WC * c + WC, :], w2_raw[c % 2][:]).then_inc(w2_hi_done, 1)

            def round_y(s, par, u):
                act.wait_ge(y_done, IT * s + u + 1)
                if u == 0 and positive(s - 1):
                    act.wait_ge(down_done, RB * (s - 1))
                nc.scalar.copy(y_hi[par][:, u, :], y[u % 2][:]).then_inc(y_hi_done, 1)

            def round_rows(s, par):
                for r in range(RB):
                    act.wait_ge(rows_turned, s * RB + r + 1)
                    nc.scalar.copy(rows_hi[par][:, :, r * P:(r + 1) * P], ps_r[r][:]).then_inc(rows_hi_done, 1)

            def store_down(s, r):
                act.wait_ge(down_done, RB * s + r + 1)
                if positive(s):
                    act.wait_ge(down_stored[r], 16 * s)
                nc.scalar.copy(down[:, r, :], ps_d[r][:]).then_inc(down_free, 1)
                act.wait_ge(down_free, RB * s + r + 1 + RB)
                act.dma_start(rows_out[bass.ds(s * BLOCK + r * P, P), :], down[:, r, :]).then_inc(down_stored[r], 16)

            def slot(s, par, turn, last):
                first = isinstance(s, int) and s == 0
                for u in range(IT):
                    n = IT * s + u
                    if u == 0 and not first:
                        round_y(s - 1, 1 - par, IT - 1)
                    if u + AHEAD < IT:
                        split_w1(s, u + AHEAD)
                    elif not last:
                        split_w1(s + 1, u + AHEAD - IT)
                    if u % WC == 0:
                        split_w2(s, par, u // WC)
                    if u > 0:
                        round_y(s, par, u - 1)
                    act.wait_ge(up_done, n + 1)
                    if positive(n - 1):
                        act.wait_ge(y_done, n - 1)
                    nc.scalar.activation(silu[u % 2][:], ps_up[u % 4][:, 0, :], ACT.Silu).then_inc(silu_done, 1)
                    if u == IT // 2 and not last:
                        round_rows(s + 1, 1 - par)
                    if u == IT // 2 and not first:
                        store_down(s - 1, 0)
                if not first:
                    store_down(s - 1, 1)

            act.sem_inc(down_free, RB)
            for u in range(AHEAD):
                split_w1(0, u)
            round_rows(0, 0)
            end = over_slots(act, slot)
            round_y(end, 0, IT - 1)
            for r in range(RB):
                store_down(end, r)

        @block.vector
        def _(dve):
            def split_w1(s, u):
                dve.wait_ge(w1_hi_done, IT * s + u + 1)
                nc.vector.tensor_tensor(w1_lo[u % RAW][:], w1_raw[u % RAW][:], w1_hi[u % RAW][:].bitcast(F32),
                                        ALU.subtract).then_inc(w1_lo_done, 1)

            def rest_y(s, par, u):
                dve.wait_ge(y_hi_done, IT * s + u + 1)
                nc.vector.tensor_tensor(y_lo[par][:, u, :], y[u % 2][:], y_hi[par][:, u, :].bitcast(F32), ALU.subtract
                                        ).then_inc(y_lo_done, 1)

            def rest_rows(s, par):
                for r in range(RB):
                    dve.wait_ge(rows_hi_done, s * RB + r + 1)
                    nc.vector.tensor_tensor(rows_lo[par][:, :, r * P:(r + 1) * P], ps_r[r][:],
                                            rows_hi[par][:, :, r * P:(r + 1) * P].bitcast(F32), ALU.subtract
                                            ).then_inc(rows_lo_done, 1)

            def slot(s, par, turn, last):
                for u in range(IT):
                    if u == 0 and not (isinstance(s, int) and s == 0):
                        rest_y(s - 1, 1 - par, IT - 1)
                    if u + AHEAD < IT:
                        split_w1(s, u + AHEAD)
                    elif not last:
                        split_w1(s + 1, u + AHEAD - IT)
                    if u > 0:
                        rest_y(s, par, u - 1)
                    dve.wait_ge(silu_done, IT * s + u + 1)
                    nc.vector.tensor_tensor(y[u % 2][:], ps_up[u % 4][:, 1, :], silu[u % 2][:], ALU.mult
                                            ).then_inc(y_done, 1)
                    if u == IT // 2 and not last:
                        rest_rows(s + 1, 1 - par)

            for u in range(AHEAD):
                split_w1(0, u)
            rest_rows(0, 0)
            end = over_slots(dve, slot)
            rest_y(end, 0, IT - 1)
            for t in range(TT):
                for k in range(2):
                    n = 2 * t + k
                    dve.wait_ge(taken_done[n % TAKEN], 16 * (n // TAKEN + 1))
                    if n:
                        dve.wait_ge(weighed, n)
                    nc.vector.scalar_tensor_tensor(out=x2[:, t, :], in0=taken[n % TAKEN][:], scalar=weight[:, t, k:k + 1],
                                                   in1=x2[:, t, :], op0=ALU.mult, op1=ALU.add).then_inc(weighed, 1)

        @block.tensor
        def _(pe):
            def turn_rows(s, par, turn):
                pe.wait_ge(rows_loaded[par], 16 * (turn + 1))
                if positive(s):
                    pe.wait_ge(rows_lo_done, RB * s)
                for r in range(RB):
                    for k in range(DT):
                        last = nc.tensor.transpose(ps_r[r][:, k, :], rows[par][:, r, k * P:(k + 1) * P], ident[:])
                    last.then_inc(rows_turned, 1)

            def up(s, par, u):
                n = IT * s + u
                pe.wait_ge(w1_lo_done, n + 1)
                if u == 0:
                    pe.wait_ge(rows_lo_done, RB * (s + 1))
                if positive(n - 3):
                    pe.wait_ge(y_done, n - 3)
                for side in range(2):
                    for k in range(DT):
                        hi, lo = w1_hi[u % RAW][:, k, side, :], w1_lo[u % RAW][:, k, side, :]
                        for i, (still, moving) in enumerate([(hi, rows_hi[par]), (hi, rows_lo[par]), (lo, rows_hi[par])]):
                            last = nc.tensor.matmul(ps_up[u % 4][:, side, :], still, moving[:, k, :],
                                                    start=(k == 0 and i == 0), stop=(k == DT - 1 and i == 2))
                last.then_inc(up_done, 1)

            def down_part(s, par, part):
                r, k0 = part * RB // IT, part * RB % IT
                if part == 0:
                    pe.wait_ge(y_lo_done, IT * (s + 1))
                    pe.wait_ge(w2_lo_done, NW2 * (s + 1))
                if k0 == 0:
                    pe.wait_ge(down_free, RB * s + r + 1)
                for k in range(k0, k0 + RB):
                    yh, yl = (y_[par][:, k, r * P:(r + 1) * P] for y_ in (y_hi, y_lo))
                    for i, (still, moving) in enumerate([(yh, w2_hi[par]), (yh, w2_lo[par]), (yl, w2_hi[par])]):
                        last = nc.tensor.matmul(ps_d[r][:], still, moving[:, k, :], start=(k == 0 and i == 0),
                                                stop=(k == IT - 1 and i == 2))
                if k0 + RB == IT:
                    last.then_inc(down_done, 1)

            def slot(s, par, turn, last):
                for u in range(IT):
                    parts = [[], [0, 1], [2], [3], [4], [5], [6, 7], []][u]
                    up(s, par, u)
                    for part in parts if not (isinstance(s, int) and s == 0) else ():
                        down_part(s - 1, 1 - par, part)
                    if u == 3 and not last:
                        turn_rows(s + 1, 1 - par, turn + (1 if par else 0))

            turn_rows(0, 0, 0)
            end = over_slots(pe, slot)
            for part in range(IT):
                down_part(end, 0, part)


_OUT = "out_dram"


def kernel(x, ctx_1024, L0_xattn_Wq, L0_xattn_bq, L0_xattn_Wkv, L0_xattn_bkv, L0_xattn_Wout, L0_xattn_bout,
           L0_attn_Wq, L0_attn_Wk, L0_attn_Wv, L0_attn_Wo, L0_ffn_w1, L0_ffn_w2, L0_ffn_router_w):
    import numpy as np
    import concourse.bacc as bacc
    from concourse.bass_utils import run_bass_kernel_spmd

    def by_partition(v):
        return np.asarray(v).reshape(DT, P).T

    ctx = np.zeros((B + 1, DT, P, LC2), np.float32)
    ctx[:B, :, :, :LC] = np.asarray(ctx_1024).transpose(0, 2, 1).reshape(B, DT, P, LC)
    ctx = np.concatenate([ctx[:, :, :, c * CW:c * CW + CHUNK_W[c]].transpose(0, 2, 1, 3).reshape(B + 1, P, -1)
                          for c in range(CHUNKS)], axis=2)
    wkv = np.asarray(L0_xattn_Wkv).reshape(D, D, 2)
    bkv = np.asarray(L0_xattn_bkv).reshape(D, 2)
    w1 = np.asarray(L0_ffn_w1).reshape(E, 2, IT, P, DT, P).transpose(0, 2, 5, 4, 1, 3).reshape(E, IT, P, DT * 2 * P)
    w2 = np.asarray(L0_ffn_w2).reshape(E, D, IT // WC, WC, P).transpose(0, 2, 4, 3, 1).reshape(E, IT // WC, P, WC * D)
    arrays = {
        "x": np.asarray(x).reshape(NT, D),
        "ctx": ctx,
        "wq": L0_xattn_Wq, "bq": by_partition(L0_xattn_bq),
        "wk": wkv[:, :, 0], "wv": wkv[:, :, 1], "bk": by_partition(bkv[:, 0]), "bv": bkv[:, 1].reshape(PAIRS, 2 * HD).T,
        "wout": L0_xattn_Wout, "bout": np.broadcast_to(np.asarray(L0_xattn_bout), (P, D)),
        "lwq": np.asarray(L0_attn_Wq).T, "lwk": np.asarray(L0_attn_Wk).T,
        "lwv": np.asarray(L0_attn_Wv).T, "lwo": np.asarray(L0_attn_Wo).T,
        "router": np.asarray(L0_ffn_router_w).reshape(E, DT, P).transpose(2, 1, 0).reshape(P, DT * E),
        "w1": w1, "w2": w2,
    }
    arrays = {f"{n}_dram": np.ascontiguousarray(a) for n, a in arrays.items()}
    nc = bacc.Bacc("TRN2", target_bir_lowering=False, num_devices=1, dynamic_dma_scratch_size=SCRATCH)
    args = [nc.dram_tensor(n, a.shape, F32, kind="ExternalInput").ap() for n, a in arrays.items()]
    args.append(nc.dram_tensor(_OUT, (NT, D), F32, kind="ExternalOutput").ap())
    names = [n[:-5] for n in arrays] + ["out"]
    build(nc, **dict(zip(names, args)))
    r = run_bass_kernel_spmd(nc, [arrays], core_ids=[0])
    return r.results[0][_OUT].reshape(B, LQ, D)
```

```python
from contextlib import ExitStack

import concourse.bass as bass
from concourse import mybir

F32 = mybir.dt.float32
F32R = mybir.dt.float32r
U32 = mybir.dt.uint32
I32 = mybir.dt.int32
ALU = mybir.AluOpType
ACT = mybir.ActivationFunctionType
AX = mybir.AxisListType

P = 128
B, LQ, D = 16, 64, 512
LC = 1601
H, HD = 16, 32
SCALE = HD ** -0.5
LN_EPS = 1e-5
LIN_EPS = 1e-6
NT = B * LQ
TT = NT // P
DT = D // P
PAIRS = H // 2
JT = -(-LC // P)
LC2 = LC + 1
CW = 256
CHUNKS = 6
CHUNK_W = [CW] * (CHUNKS - 1) + [LC2 - CW * (CHUNKS - 1)]
CHUNK_MAX = CHUNK_W[-1]
TAIL = LC - (JT - 1) * P
E, INTER = 8, 1024
IT = INTER // P
BANK = 512
BLOCK = 384
SLOTS = (2 * NT + E * (BLOCK - 1)) // BLOCK
SLOTS += SLOTS % 2
RB = BLOCK // P
SLOTS_MIN = -(-2 * NT // BLOCK)
PAIRS_MAX, PAIRS_MIN = (SLOTS - 2) // 2, (SLOTS_MIN - 1) // 2
ZERO_W = 256
ZERO_ROWS = P * ZERO_W // D
ZERO_PIECES = -(-SLOTS * BLOCK // (ZERO_ROWS * (B - 1)))
SCRATCH = 4096
WC = 2


BEHIND = ["VKK", "VV", "VKK", "VV", "VKK", "VV", "VKV", "VVK"]


def plan_units():
    ks = [("K", c, g) for c in range(CHUNKS) for g in range(DT)]
    vs = [("V", min(j * P // CW, CHUNKS - 1), j) for j in range(JT)]
    units, gaps = [], []
    for behind in BEHIND:
        gaps.append([])
        for kinds in ("K", "K", behind[0], behind[1:]):
            gaps[-1].append(list(range(len(units), len(units) + len(kinds))))
            units += [(ks if kind == "K" else vs).pop(0) for kind in kinds]
    assert not ks and not vs
    return units, gaps


UNITS, AT = plan_units()
NU = len(UNITS)
LAST_OF_CHUNK = [max(n for n, u in enumerate(UNITS) if u[1] == c) for c in range(CHUNKS)]
K_WHOLE = [UNITS.index(("K", CHUNKS - 1, p // 2)) for p in range(PAIRS)]


def pair_of_unit(n):
    return next(p for p in range(PAIRS) if n in sum(AT[p], []))


def positive(value):
    return not isinstance(value, int) or value > 0


def build(nc, x, ctx, wq, bq, wk, wv, bk, bv, wout, bout, lwq, lwk, lwv, lwo, router, w1, w2, out):
    q_parts = nc.dram_tensor("q_parts", (2, D, NT), F32, kind="Internal").ap()
    attn_t = nc.dram_tensor("attn_t", (D, NT), F32, kind="Internal").ap()
    rows_in = nc.dram_tensor("rows_in", ((B - 1) * ZERO_PIECES * ZERO_ROWS, D), F32, kind="Internal").ap()
    rows_out = nc.dram_tensor("rows_out", (SLOTS * BLOCK, D), F32, kind="Internal").ap()
    with ExitStack() as whole:
        ident = whole.enter_context(nc.sbuf_tensor("ident", [P, P], F32))
        cross_attention(nc, ident, x, ctx, wq, bq, wk, wv, bk, bv, q_parts, attn_t, rows_in, rows_out)
        x2 = whole.enter_context(nc.sbuf_tensor("x2", [P, TT, D], F32))
        xn = whole.enter_context(nc.sbuf_tensor("xn2", [P, TT, D], F32))
        weight = whole.enter_context(nc.sbuf_tensor("weight", [P, TT, 8], F32))
        place = whole.enter_context(nc.sbuf_tensor("place", [P, 2, TT], U32))
        slot_expert = whole.enter_context(nc.sbuf_tensor("slot_expert", [1, SLOTS + 1], I32))
        slot_pairs = whole.enter_context(nc.sbuf_tensor("slot_pairs", [1, 1], I32))
        linear_attention(nc, ident, x, attn_t, wout, bout, lwq, lwk, lwv, lwo, router,
                         x2, xn, weight, place, slot_expert, slot_pairs)
        experts(nc, ident, x2, xn, weight, place, slot_expert, slot_pairs, rows_in, rows_out, w1, w2, out)


def cross_attention(nc, ident, x, ctx, wq, bq, wk, wv, bk, bv, q_parts, attn_t, rows_in, rows_out):
    with ExitStack() as mem:
        def sb(name, shape, dt=F32):
            return mem.enter_context(nc.sbuf_tensor(name, shape, dt))

        def sem(name):
            return mem.enter_context(nc.semaphore(name))

        wk_hi = sb("wk_hi", [P, DT, D], F32R)
        wk_lo = sb("wk_lo", [P, DT, D], F32R)
        wv_hi = sb("wv_hi", [P, DT, D], F32R)
        wv_lo = sb("wv_lo", [P, DT, D], F32R)
        bq_sb = sb("bq_sb", [P, DT])
        bk_sb = sb("bk_sb", [P, DT])
        bv_sb = sb("bv_sb", [2 * HD, PAIRS])
        stats = sb("stats", [P, TT, 6])
        mean_var = sb("mean_var", [P, TT, 2])
        std = sb("std", [P, TT])
        rstd = sb("rstd", [P, TT])
        ctx_raw = [sb(f"ctx_raw{i}", [P, DT * CHUNK_MAX]) for i in range(2)]
        ctx_hi = [sb(f"ctx_hi{i}", [P, DT * CHUNK_MAX], F32R) for i in range(2)]
        ctx_lo = [sb(f"ctx_lo{i}", [P, DT * CHUNK_MAX], F32R) for i in range(2)]
        k_t = [sb(f"k_t{i}", [P, DT, LC2]) for i in range(2)]
        v = [sb(f"v{i}", [P, JT, D]) for i in range(2)]
        k_parts = sb("k_parts", [P, LC2], F32R)
        v_parts = sb("v_parts", [P, JT, 2, 2 * HD], F32R)
        q_blocks = [sb(f"q_blocks{i}", [P, PAIRS // 2, 2, P], F32R) for i in range(2)]
        probs_both = sb("probs_both", [P, 2 * LC])
        probs = [probs_both[:, i * LC:(i + 1) * LC] for i in range(2)]
        probs_t = sb("probs_t", [P, JT, 2, P], F32R)
        row_max = sb("row_max", [P, 2])
        neg_max = sb("neg_max", [P, 2])
        row_sum = sb("row_sum", [P, 2])
        row_inv = sb("row_inv", [P, 2])
        o_sum = sb("o_sum", [2 * HD, 2, P])
        o_t = sb("o_t", [P, DT, LQ])
        zeros = sb("zeros", [P, ZERO_W])

        k_room, v_room = k_t[1][:].rearrange("p g n -> p (g n)"), v[1][:].rearrange("p t n -> p (t n)")
        q_room = probs_t[:].rearrange("p t i n -> p (t i n)")
        xs = k_room[:, 0:TT * D].rearrange("p (t d) -> p t d", t=TT)
        wq_sb = k_room[:, TT * D:(TT + DT) * D].rearrange("p (t d) -> p t d", t=DT)
        xn_t = v_room[:, 0:DT * NT].rearrange("p (t n) -> p t n", t=DT)
        wk_raw = v_room[:, DT * NT:DT * (NT + D)].rearrange("p (t d) -> p t d", t=DT)
        wv_raw = probs_both[:, 0:DT * D].rearrange("p (t d) -> p t d", t=DT)
        q_hi = [q_room[:, i * BANK:(i + 1) * BANK] for i in range(2)]
        q_lo = [q_room[:, (2 + i) * BANK:(3 + i) * BANK] for i in range(2)]

        ps_s = mem.enter_context(nc.psum_tensor("ps_s", [P, 4 * BANK], F32))
        ps_kv = [mem.enter_context(nc.psum_tensor(f"ps_kv{i}", [P, BANK], F32)) for i in range(2)]
        ps_pt = mem.enter_context(nc.psum_tensor("ps_pt", [P, 4, P], F32))
        ps_o = mem.enter_context(nc.psum_tensor("ps_o", [P, 4, P], F32))
        ps_turned = {True: [ps_pt, ps_o, ps_pt, ps_pt],
                     False: [ps_pt, ps_o] + [bank[:].rearrange("p (k c) -> p k c", c=P) for bank in ps_kv]}

        x_loaded = [sem(f"x_loaded{i}") for i in range(4)]
        wq_loaded, bias_loaded = sem("wq_loaded"), sem("bias_loaded")
        wk_loaded, wv_loaded = sem("wk_loaded"), sem("wv_loaded")
        ident_zero, ident_made = sem("ident_zero"), sem("ident_made")
        stats_done, var_done, std_done, rstd_done = sem("stats_done"), sem("var_done"), sem("std_done"), sem("rstd_done")
        xn_done, turned, xnt_done = sem("xn_done"), sem("turned"), sem("xnt_done")
        q_done, q_hi_done, q_lo_done = sem("q_done"), sem("q_hi_done"), sem("q_lo_done")
        q_stored = [[sem(f"q_{part}_stored{i}") for i in range(2)] for part in ("hi", "lo")]
        w_hi_done, w_lo_done = sem("w_hi_done"), sem("w_lo_done")

        ctx_loaded = [sem("ctx_loaded0"), sem("ctx_loaded1")]
        ctx_hi_done, ctx_lo_done = sem("ctx_hi_done"), sem("ctx_lo_done")
        kv_done, kv_copied = sem("kv_done"), sem("kv_copied")
        zeroed = sem("zeroed")
        q_loaded = [sem("q_loaded0"), sem("q_loaded1")]
        k_hi_done, k_lo_done, v_hi_done, v_lo_done = sem("k_hi_done"), sem("k_lo_done"), sem("v_hi_done"), sem("v_lo_done")
        scores_done, max_done, neg_done, exp_done = sem("scores_done"), sem("max_done"), sem("neg_done"), sem("exp_done")
        inv_done, probs_done = sem("inv_done"), sem("probs_done")
        pt_done, pt_hi_done, pt_lo_done = sem("pt_done"), sem("pt_hi_done"), sem("pt_lo_done")
        pv_done, o_halves, o_done, o_stored = sem("pv_done"), sem("o_halves"), sem("o_done"), sem("o_stored")
        rows_zeroed, tail_zeroed = sem("rows_zeroed"), sem("tail_zeroed")
        pieces = ZERO_PIECES
        rows_flat = rows_in.rearrange("n d -> (n d)").rearrange("(k p c) -> k p c", p=P, c=ZERO_W)

        SC = [(c * BANK, min(BANK, LC2 - c * BANK)) for c in range(4)]
        TG = [list(range(g * 4, min(g * 4 + 4, JT))) for g in range(4)]
        NG = len(TG)

        def rows(j):
            return TAIL if j == JT - 1 else P

        TURN_FROM, QUERY_FROM = 8, 16
        NQ = 2 * DT

        def start_steps():
            for u in range(NU):
                yield "unit", u
                if TURN_FROM <= u < TURN_FROM + TT:
                    yield "turn", u - TURN_FROM
                if QUERY_FROM <= u < QUERY_FROM + NQ:
                    yield "query", u - QUERY_FROM

        block = mem.enter_context(nc.Block())

        def over_batches(engine, batch):
            batch(0, 0, True)
            with engine.Fori(0, (B - 2) // 2) as i:
                batch(i * 2 + 1, 1, True)
                batch(i * 2 + 2, 0, True)
            batch(B - 1, 1, False)

        def later(b, par, p, steps):
            if p + steps < PAIRS:
                return b, par, p + steps
            return None if isinstance(b, int) and b == B - 1 else (b + 1, 1 - par, p + steps - PAIRS)

        def splits_at(b, p, kv):
            found = []
            for c in range(CHUNKS):
                free_at = pair_of_unit(LAST_OF_CHUNK[c]) + 1
                if kv and free_at == p:
                    found.append((b + 1, c + 2) if c + 2 < CHUNKS else (b + 2, c + 2 - CHUNKS))
                if kv and free_at == PAIRS and p == 0 and not (isinstance(b, int) and b == 0):
                    found.append((b + 1, c + 2 - CHUNKS))
            return found

        @block.sync
        def _(sp):
            def load_ctx(b, c):
                n = CHUNKS * b + c
                if positive(n - 1):
                    sp.wait_ge(ctx_lo_done, n - 1)
                w = DT * CHUNK_W[c]
                sp.dma_start(ctx_raw[c % 2][:, 0:w], ctx[b, :, bass.ds(DT * CW * c, w)] if isinstance(b, int)
                             else ctx[bass.ds(b, 1), :, DT * CW * c:DT * CW * c + w].rearrange("a p n -> p (a n)")
                             ).then_inc(ctx_loaded[c % 2], 16)

            def load_q(b, half):
                for part in range(2):
                    for e in range(2):
                        for copy in range(2):
                            src = q_parts[part].rearrange("(n e r) t -> e r n t", e=2, r=HD)[
                                e, :, 4 * half:4 * half + 4, bass.ds(b * LQ, LQ)]
                            row = 2 * HD * copy + HD * e
                            sp.dma_start(q_blocks[half][row:row + HD, :, part, LQ * e:LQ * e + LQ].bitcast(F32), src
                                         ).then_inc(q_loaded[half], 16)

            def batch(b, par, kv):
                if not kv:
                    tail = rows_out[(2 * PAIRS_MIN + 2) * BLOCK:, :].rearrange("(p r) d -> p (r d)", p=P)
                    w = zeros.shape[1]
                    sp.dma_start(tail.rearrange("p (r c) -> p r c", c=w),
                                 zeros[:].unsqueeze(1).to_broadcast([P, tail.shape[1] // w, w])).then_inc(tail_zeroed, 16)
                for p in range(PAIRS):
                    if p == 1 and positive(b):
                        sp.wait_ge(o_done, PAIRS * b)
                        sp.dma_start(attn_t.rearrange("(g p) n -> p g n", p=P)[:, :, bass.ds((b - 1) * LQ, LQ)],
                                     o_t[:]).then_inc(o_stored, 16)
                    if kv:
                        for k in range(pieces * p // PAIRS, pieces * (p + 1) // PAIRS):
                            sp.dma_start(rows_flat[bass.ds(b * pieces + k, 1)].rearrange("a p c -> (a p) c"), zeros[:]
                                         ).then_inc(rows_zeroed, 16)
                        for b_of, c in splits_at(b, p, kv):
                            load_ctx(b_of, c)
                        if p in (4, PAIRS - 1):
                            sp.wait_ge(scores_done, PAIRS * b + (PAIRS // 2 if p == 4 else PAIRS))
                            load_q(b + 1, 0 if p == 4 else 1)

            sp.dma_start(wk_raw, wk.rearrange("(t p) n -> p t n", p=P)).then_inc(wk_loaded, 16)
            load_ctx(0, 0)
            sp.dma_start(bk_sb[:], bk).then_inc(bias_loaded, 16)
            sp.dma_start(bv_sb[:], bv).then_inc(bias_loaded, 16)
            sp.dma_start(bq_sb[:], bq).then_inc(bias_loaded, 16)
            sp.dma_start(wv_raw, wv.rearrange("(t p) n -> p t n", p=P)).then_inc(wv_loaded, 16)
            xv = x.rearrange("(t p) d -> p t d", p=P)
            for i in range(4):
                sp.dma_start(xs[:, 2 * i:2 * i + 2, :], xv[:, 2 * i:2 * i + 2, :]).then_inc(x_loaded[i], 16)
            load_ctx(0, 1)
            sp.dma_start(wq_sb, wq.rearrange("(t p) n -> p t n", p=P)).then_inc(wq_loaded, 16)
            for c in range(2, CHUNKS):
                load_ctx(0, c)
            for n in range(NQ):
                g, half = n // 2, n % 2
                if n == NQ // 2:
                    load_ctx(1, 0)
                for part, (done, buf) in enumerate(((q_hi_done, q_hi), (q_lo_done, q_lo))):
                    sp.wait_ge(done, n + 1)
                    sp.dma_start(q_parts[part, g * P:(g + 1) * P, half * BANK:(half + 1) * BANK],
                                 buf[n % 2].bitcast(F32)).then_inc(q_stored[part][n % 2], 16)
            for part in range(2):
                for i in range(2):
                    sp.wait_ge(q_stored[part][i], NQ // 2 * 16)
            sp.wait_ge(zeroed, 5)
            load_q(0, 0)
            load_q(0, 1)
            load_ctx(1, 1)
            over_batches(sp, batch)
            sp.wait_ge(o_done, PAIRS * B)
            sp.dma_start(attn_t.rearrange("(g p) n -> p g n", p=P)[:, :, (B - 1) * LQ:], o_t[:]).then_inc(o_stored, 16)
            sp.wait_ge(o_stored, 16 * B)
            sp.wait_ge(rows_zeroed, 16 * pieces * (B - 1))
            sp.wait_ge(tail_zeroed, 16)

        @block.gpsimd
        def _(pool):
            def split_ctx(b, c, ks):
                n = CHUNKS * b + c
                w = DT * CHUNK_W[c]
                pool.wait_ge(ctx_hi_done, n + 1)
                if positive(ks):
                    pool.wait_ge(k_lo_done, ks)
                nc.gpsimd.tensor_tensor(ctx_lo[c % 2][:, 0:w], ctx_raw[c % 2][:, 0:w],
                                        ctx_hi[c % 2][:, 0:w].bitcast(F32), ALU.subtract).then_inc(ctx_lo_done, 1)

            def split_k(b, par, p, chunks):
                s, g = p % 2, p // 2
                pool.wait_ge(k_hi_done, PAIRS * b + p + 1)
                pool.wait_ge(ctx_lo_done, chunks)
                if positive(PAIRS * b + p):
                    pool.wait_ge(k_lo_done, PAIRS * b + p)
                nc.gpsimd.tensor_tensor(k_parts[64 - 64 * s:128 - 64 * s, :], k_t[par][64 * s:64 * s + 64, g, :],
                                        k_parts[64 * s:64 * s + 64, :].bitcast(F32), ALU.subtract
                                        ).then_inc(k_lo_done, 1)

            def batch(b, par, kv):
                chunks = CHUNKS * (b + 1) + (2 if isinstance(b, int) and b == 0 else 1)
                for p in range(PAIRS):
                    n = PAIRS * b + p
                    two_on = later(b, par, p, 2)
                    ks = n + 2 if later(b, par, p, 1) else PAIRS * B
                    pool.wait_ge(v_hi_done, n + 1)
                    pool.wait_ge(k_lo_done, ks)
                    nc.gpsimd.tensor_tensor(v_parts[:, :, 1, :], v[par][:, :, 64 * p:64 * p + 64],
                                            v_parts[:, :, 0, :].bitcast(F32), ALU.subtract).then_inc(v_lo_done, 1)
                    for b_of, c in splits_at(b, p, kv):
                        split_ctx(b_of, c, ks)
                        chunks = chunks + 1
                    if two_on:
                        pool.wait_ge(v_lo_done, n + 1)
                        split_k(*two_on, chunks)

            nc.gpsimd.memset(ident[:], 0.0).then_inc(ident_zero, 1)
            pool.wait_ge(ident_zero, 1)
            nc.gpsimd.affine_select(out=ident[:], in_=ident[:], compare_op=ALU.not_equal, fill=1.0, base=0,
                                    pattern=[[-1, P]], channel_multiplier=1).then_inc(ident_made, 1)
            nc.gpsimd.memset(zeros[:], 0.0).then_inc(zeroed, 1)
            for half in range(2):
                nc.gpsimd.memset(q_blocks[half][:].bitcast(F32), 0.0).then_inc(zeroed, 1)
            for par in range(2):
                pool.wait_ge(zeroed, 3 + par)
                nc.gpsimd.memset(v[par][64:128, JT - 1, :], 0.0).then_inc(zeroed, 1)
            pool.wait_ge(zeroed, 5)
            for c in range(CHUNKS + 2):
                split_ctx(c // CHUNKS, c % CHUNKS, 0)
            for p in range(2):
                split_k(0, 0, p, CHUNKS + 2)
            over_batches(pool, batch)

        @block.vector
        def _(dve):
            def split_ctx(b, c):
                n = CHUNKS * b + c
                w = DT * CHUNK_W[c]
                dve.wait_ge(ctx_loaded[c % 2], (b * (CHUNKS // 2) + c // 2 + 1) * 16)
                if positive(n - 1):
                    before, at = (b, c - 2) if c >= 2 else (b - 1, c - 2 + CHUNKS)
                    dve.wait_ge(kv_done, NU * before + LAST_OF_CHUNK[at] + 1)
                nc.vector.tensor_copy(ctx_hi[c % 2][:, 0:w], ctx_raw[c % 2][:, 0:w]).then_inc(ctx_hi_done, 1)

            def split_k(b, par, p):
                s, g = p % 2, p // 2
                if p % 2 == 0:
                    dve.wait_ge(kv_copied, NU * b + K_WHOLE[p] + 1)
                n = PAIRS * b + p
                if positive(n):
                    dve.wait_ge(scores_done, n)
                nc.vector.tensor_copy(k_parts[64 * s:64 * s + 64, :], k_t[par][64 * s:64 * s + 64, g, :]
                                      ).then_inc(k_hi_done, 1)

            def outputs(n, p):
                s, g = p % 2, p // 2
                dve.wait_ge(pv_done, n + 1)
                for part in range(2):
                    nc.vector.tensor_reduce(o_sum[:, part, :], ps_o[64 * part:64 * part + 64, 0:2].rearrange("p h c -> p c h"),
                                            AX.X, ALU.add).then_inc(o_halves, 1)
                dve.wait_ge(o_halves, (n + 1) * 2)
                for e in range(2):
                    own = slice(HD * e, HD * e + HD)
                    ins = nc.vector.scalar_tensor_tensor(
                        out=o_t[64 * s + HD * e:64 * s + HD * e + HD, g, :], in0=o_sum[own, 0, LQ * e:LQ * e + LQ],
                        scalar=bv_sb[own, p:p + 1], in1=o_sum[own, 1, LQ * e:LQ * e + LQ], op0=ALU.add, op1=ALU.add)
                ins.then_inc(o_done, 1)

            def guard(n, p):
                q = p % 2
                dve.wait_ge(scores_done, n + 1)
                nc.vector.tensor_reduce(row_max[:, q:q + 1], ps_s[:, 0:LC], AX.X, ALU.max).then_inc(max_done, 1)
                dve.wait_ge(max_done, n + 1)
                nc.vector.tensor_scalar(neg_max[:, q:q + 1], row_max[:, q:q + 1], -SCALE, None, ALU.mult
                                        ).then_inc(neg_done, 1)

            def normalise(n, p):
                q = p % 2
                dve.wait_ge(exp_done, n + 1)
                nc.vector.reciprocal(row_inv[:, q:q + 1], row_sum[:, q:q + 1]).then_inc(inv_done, 1)
                dve.wait_ge(inv_done, n + 1)
                nc.vector.tensor_scalar(probs[q], probs[q], row_inv[:, q:q + 1], None, ALU.mult
                                        ).then_inc(probs_done, 1)

            def rest(n, g, kv):
                m, k, j = rows(TG[g][0]), len(TG[g]), TG[g][0]
                dve.wait_ge(pt_hi_done, n * NG + g + 1)
                nc.vector.tensor_tensor(probs_t[0:m, j:j + k, 1, :], ps_turned[kv][g][0:m, 0:k, :],
                                        probs_t[0:m, j:j + k, 0, :].bitcast(F32), ALU.subtract).then_inc(pt_lo_done, 1)

            def batch(b, par, kv):
                for p in range(PAIRS):
                    n = PAIRS * b + p
                    one_on, two_on = later(b, par, p, 1), later(b, par, p, 2)
                    if p == 1 and positive(b):
                        dve.wait_ge(o_stored, 16 * b)
                    if positive(n):
                        outputs(n - 1, (p - 1) % PAIRS)
                    rest(n, 0, kv)
                    for b_of, c in splits_at(b, p, kv):
                        split_ctx(b_of, c)
                    rest(n, 1, kv)
                    rest(n, 2, kv)
                    if one_on:
                        guard(n + 1, one_on[2])
                    rest(n, 3, kv)
                    if two_on and p != PAIRS - 2:
                        split_k(*two_on)
                    if one_on:
                        normalise(n + 1, one_on[2])
                    if two_on and p == PAIRS - 2:
                        split_k(*two_on)

            def rest_of_weights(i, raw, hi, lo):
                dve.wait_ge(w_hi_done, i + 1)
                nc.vector.tensor_tensor(lo[:], raw, hi[:].bitcast(F32), ALU.subtract).then_inc(w_lo_done, 1)

            def norm_x():
                for t in range(TT):
                    dve.wait_ge(x_loaded[t // 2], 16)
                    nc.vector.bn_stats(stats[:, t, :], xs[:, t, :]).then_inc(stats_done, 1)
                    dve.wait_ge(stats_done, t + 1)
                    nc.vector.bn_aggr(mean_var[:, t, :], stats[:, t, :]).then_inc(var_done, 1)
                dve.wait_ge(var_done, TT)
                nc.vector.tensor_scalar(std[:], mean_var[:, :, 1], LN_EPS, None, ALU.add).then_inc(var_done, 1)
                dve.wait_ge(std_done, 1)
                nc.vector.reciprocal(rstd[:], std[:]).then_inc(rstd_done, 1)
                dve.wait_ge(rstd_done, 1)
                for t in range(TT):
                    nc.vector.tensor_scalar(xs[:, t, :], xs[:, t, :], mean_var[:, t, 0:1], rstd[:, t:t + 1],
                                            ALU.subtract, ALU.mult).then_inc(xn_done, 1)

            def rest_of_query(n):
                dve.wait_ge(q_hi_done, n + 1)
                if n >= 2:
                    dve.wait_ge(q_stored[1][n % 2], n // 2 * 16)
                nc.vector.scalar_tensor_tensor(
                    out=q_lo[n % 2], in0=ps_s[:, n % 4 * BANK:(n % 4 + 1) * BANK], scalar=bq_sb[:, n // 2:n // 2 + 1],
                    in1=q_hi[n % 2].bitcast(F32), op0=ALU.add, op1=ALU.subtract).then_inc(q_lo_done, 1)

            split_ctx(0, 0)
            rest_of_weights(0, wk_raw, wk_hi, wk_lo)
            rest_of_weights(1, wv_raw, wv_hi, wv_lo)
            split_ctx(0, 1)
            norm_x()
            split_ctx(0, 2)
            split_ctx(0, 3)
            dve.wait_ge(bias_loaded, 48)
            for n in range(NQ):
                if QUERY_FROM + n == LAST_OF_CHUNK[2] + 1:
                    split_ctx(0, 4)
                rest_of_query(n)
            split_ctx(0, 5)
            for c in range(2):
                split_ctx(1, c)
            dve.wait_ge(zeroed, 5)
            split_k(0, 0, 0)
            guard(0, 0)
            split_k(0, 0, 1)
            normalise(0, 0)
            over_batches(dve, batch)
            outputs(PAIRS * B - 1, PAIRS - 1)

        @block.scalar
        def _(act):
            def copy_unit(b, par, n):
                kind, c, which = UNITS[n]
                bank = (NU * par + n) % 2
                act.wait_ge(kv_done, NU * b + n + 1)
                if n == 0 and not (isinstance(b, int) and b < 2):
                    act.wait_ge(k_lo_done, PAIRS * (b - 1))
                    act.wait_ge(v_lo_done, PAIRS * (b - 1))
                if kind == "K":
                    w = CHUNK_W[c]
                    nc.scalar.activation(k_t[par][:, which, CW * c:CW * c + w], ps_kv[bank][:, 0:w], ACT.Identity,
                                         bias=bk_sb[:, which:which + 1]).then_inc(kv_copied, 1)
                else:
                    m = rows(which)
                    nc.scalar.copy(v[par][0:m, which, :], ps_kv[bank][0:m, :]).then_inc(kv_copied, 1)

            def copy_group(n, g, kv):
                m, k, j = rows(TG[g][0]), len(TG[g]), TG[g][0]
                act.wait_ge(pt_done, n * NG + g + 1)
                if g == 0 and positive(n):
                    act.wait_ge(pv_done, n)
                nc.scalar.copy(probs_t[0:m, j:j + k, 0, :], ps_turned[kv][g][0:m, 0:k, :]).then_inc(pt_hi_done, 1)

            def exponent(n, p):
                q = p % 2
                act.wait_ge(neg_done, n + 1)
                if positive(n - 1):
                    act.wait_ge(pt_done, (n - 1) * NG)
                nc.scalar.activation(probs[q], ps_s[:, 0:LC], ACT.Exp, bias=neg_max[:, q:q + 1], scale=SCALE,
                                     accum_out=row_sum[:, q:q + 1]).then_inc(exp_done, 1)

            def round_v(b, par, p):
                n = PAIRS * b + p
                if p == 0:
                    act.wait_ge(kv_copied, NU * (b + 1))
                if positive(n):
                    act.wait_ge(pv_done, n)
                nc.scalar.copy(v_parts[:, :, 0, :], v[par][:, :, 64 * p:64 * p + 64]).then_inc(v_hi_done, 1)

            def batch(b, par, kv):
                for p in range(PAIRS):
                    n = PAIRS * b + p
                    for g in range(NG):
                        copy_group(n, g, kv)
                        if g == 0:
                            round_v(b, par, p)
                        if g == NG - 1 and later(b, par, p, 1):
                            exponent(n + 1, (p + 1) % PAIRS)
                        for u in (AT[p][g] if g < 2 else AT[p][2] + AT[p][3] if g == NG - 1 else []) if kv else []:
                            copy_unit(b + 1, 1 - par, u)

            for i, (loaded, raw, hi) in enumerate(((wk_loaded, wk_raw, wk_hi), (wv_loaded, wv_raw, wv_hi))):
                act.wait_ge(loaded, 16)
                nc.scalar.copy(hi[:], raw).then_inc(w_hi_done, 1)
            act.wait_ge(zeroed, 5)
            act.wait_ge(bias_loaded, 48)
            for kind, k in start_steps():
                if kind == "unit":
                    copy_unit(0, 0, k)
                    if k == TURN_FROM - 3:
                        act.wait_ge(var_done, TT + 1)
                        nc.scalar.activation(std[:], std[:], ACT.Sqrt).then_inc(std_done, 1)
                elif kind == "turn":
                    act.wait_ge(turned, k + 1)
                    nc.scalar.copy(xn_t[:, :, k * P:(k + 1) * P], (ps_pt, ps_o)[k % 2][:]).then_inc(xnt_done, 1)
                else:
                    act.wait_ge(q_done, k + 1)
                    if k >= 2:
                        act.wait_ge(q_lo_done, k - 1)
                        act.wait_ge(q_stored[0][k % 2], k // 2 * 16)
                    nc.scalar.activation(q_hi[k % 2], ps_s[:, k % 4 * BANK:(k % 4 + 1) * BANK], ACT.Identity,
                                         bias=bq_sb[:, k // 2:k // 2 + 1]).then_inc(q_hi_done, 1)
            exponent(0, 0)
            over_batches(act, batch)

        @block.tensor
        def _(pe):
            def unit(b, par, n):
                kind, c, which = UNITS[n]
                bank = ps_kv[(NU * par + n) % 2]
                if n == 0 or UNITS[n - 1][1] != c:
                    pe.wait_ge(ctx_lo_done, CHUNKS * b + c + 1)
                total = NU * b + n
                if positive(total - 1):
                    pe.wait_ge(kv_copied, total - 1)
                w = CHUNK_W[c]
                for k in range(DT):
                    hi = ctx_hi[c % 2][:, k * w:(k + 1) * w]
                    lo = ctx_lo[c % 2][:, k * w:(k + 1) * w]
                    if kind == "K":
                        dims = slice(which * P, (which + 1) * P)
                        o = bank[:, 0:w]
                        passes = [(wk_hi[:, k, dims], hi), (wk_hi[:, k, dims], lo), (wk_lo[:, k, dims], hi)]
                    else:
                        m = rows(which)
                        tile = slice(which * P - c * CW, which * P - c * CW + m)
                        o = bank[0:m, :]
                        passes = [(hi[:, tile], wv_hi[:, k, :]), (hi[:, tile], wv_lo[:, k, :]),
                                  (lo[:, tile], wv_hi[:, k, :])]
                    for i, (still, moving) in enumerate(passes):
                        last = nc.tensor.matmul(o, still, moving, start=(k == 0 and i == 0),
                                                stop=(k == DT - 1 and i == 2))
                last.then_inc(kv_done, 1)

            def scores(b, p):
                n = PAIRS * b + p
                half = p // 4
                pe.wait_ge(k_lo_done, n + 1)
                if p % 4 == 0:
                    pe.wait_ge(q_loaded[half], 128 * (b + 1))
                if positive(n):
                    pe.wait_ge(exp_done, n)
                for part in range(2):
                    for c0, w in SC:
                        last = nc.tensor.matmul(ps_s[:, c0:c0 + w], q_blocks[half][:, p % 4, part, :],
                                                k_parts[:, c0:c0 + w], start=(part == 0), stop=(part == 1))
                last.then_inc(scores_done, 1)

            def values(n):
                pe.wait_ge(pt_lo_done, NG * (n + 1))
                pe.wait_ge(v_lo_done, n + 1)
                if positive(n):
                    pe.wait_ge(o_halves, 2 * n)
                for j in range(JT):
                    m = rows(j)
                    last = nc.tensor.matmul(ps_o[:, 0:2], v_parts[0:m, j, :, :].rearrange("p a b -> p (a b)"),
                                            probs_t[0:m, j, :, :], start=(j == 0), stop=(j == JT - 1))
                last.then_inc(pv_done, 1)

            def turn(n, q, g, kv):
                if g == 0:
                    pe.wait_ge(probs_done, n + 1)
                if g == 1:
                    if positive(n):
                        pe.wait_ge(o_halves, 2 * n)
                elif not kv:
                    pe.wait_ge(pt_lo_done, n * NG)
                    if g >= 2:
                        pe.wait_ge(kv_copied, NU * B)
                elif positive(n * NG + g):
                    pe.wait_ge(pt_lo_done, n * NG + [0, None, 1, 3][g])
                for i, j in enumerate(TG[g]):
                    m = rows(j)
                    last = nc.tensor.transpose(ps_turned[kv][g][0:m, i, :], probs[q][:, j * P:j * P + m], ident[:])
                last.then_inc(pt_done, 1)

            def batch(b, par, kv):
                for p in range(PAIRS):
                    n = PAIRS * b + p
                    one_on = later(b, par, p, 1)

                    def beside(gap):
                        for u in AT[p][gap] if kv else ():
                            unit(b + 1, 1 - par, u)

                    turn(n, p % 2, 0, kv)
                    beside(0)
                    turn(n, p % 2, 1, kv)
                    beside(1)
                    turn(n, p % 2, 2, kv)
                    if one_on:
                        scores(one_on[0], one_on[2])
                    turn(n, p % 2, 3, kv)
                    beside(2)
                    values(n)
                    beside(3)

            pe.wait_ge(ident_made, 1)
            for kind, k in start_steps():
                if kind == "unit":
                    if k == 0:
                        pe.wait_ge(w_lo_done, 1)
                    elif UNITS[k][0] == "V" and UNITS[k][2] == 0:
                        pe.wait_ge(w_lo_done, 2)
                    unit(0, 0, k)
                elif kind == "turn":
                    pe.wait_ge(xn_done, k + 1)
                    if k >= 2:
                        pe.wait_ge(xnt_done, k - 1)
                    for i in range(DT):
                        last = nc.tensor.transpose((ps_pt, ps_o)[k % 2][:, i, :], xs[:, k, i * P:(i + 1) * P], ident[:])
                    last.then_inc(turned, 1)
                else:
                    g, half = k // 2, k % 2
                    if k == 0:
                        pe.wait_ge(wq_loaded, 16)
                        pe.wait_ge(xnt_done, TT)
                    if k >= 4:
                        pe.wait_ge(q_lo_done, k - 3)
                    for i in range(DT):
                        last = nc.tensor.matmul(ps_s[:, k % 4 * BANK:(k % 4 + 1) * BANK], wq_sb[:, i, g * P:(g + 1) * P],
                                                xn_t[:, i, half * BANK:(half + 1) * BANK],
                                                start=(i == 0), stop=(i == DT - 1))
                    last.then_inc(q_done, 1)
            pe.wait_ge(q_lo_done, NQ)
            scores(0, 0)
            over_batches(pe, batch)


def linear_attention(nc, ident, x, attn_t, wout, bout, lwq, lwk, lwv, lwo, router,
                     x2, xn, weight, place, slot_expert, slot_pairs):
    with ExitStack() as mem:
        def sb(name, shape, dt=F32):
            return mem.enter_context(nc.sbuf_tensor(name, shape, dt))

        def sem(name):
            return mem.enter_context(nc.semaphore(name))

        xs = sb("xs2", [P, TT, D])
        o_t = sb("o_t2", [P, DT, NT])
        xn_hi = sb("xn_hi", [P, DT, NT], F32R)
        xn_lo = sb("xn_lo", [P, DT, NT], F32R)
        SPLIT = ("lwq", "lwk", "lwv")
        w_hi = {n: sb(f"{n}_hi", [P, DT, D], F32R) for n in SPLIT}
        w_lo = {n: sb(f"{n}_lo", [P, DT, D], F32R) for n in SPLIT}
        w_sb = {n: sb(f"{n}_sb", [P, DT, D]) for n in ("wout", "lwo")}
        router_sb = sb("router_sb", [P, DT, E])
        bout_sb = sb("bout_sb", [P, D])
        stats = sb("stats2", [P, TT, 6])
        mean_var = sb("mean_var2", [P, TT, 2])
        std = sb("std2", [P, TT])
        rstd = sb("rstd2", [P, TT])
        q_t = o_t
        xn_t = q_t
        k_f = sb("lk", [P, TT, D])
        w_raw = {"lwq": k_f[:, 0:DT, :], "lwk": k_f[:, DT:2 * DT, :], "lwv": sb("lwv_raw", [P, DT, D])[:]}
        low = [sb(f"low{i}", [P, BANK]) for i in range(2)]
        expo = [sb(f"expo{i}", [P, BANK]) for i in range(2)]
        v_two = [xs[:, 2 * i:2 * i + 2, :].rearrange("p t d -> p (t d)").rearrange("p (g b c) -> p g b c", g=DT, b=2)
                 for i in range(2)]
        ones_two = sb("ones_two", [P, 2])
        same_head = sb("same_head", [P, P])
        head_of = sb("head_of", [P, DT])
        kv_blocks = [sb(f"kv_blocks{i}", [P, DT, 2, P + DT]) for i in range(2)]
        den = [sb(f"den{i}", [P, 2, 2, DT]) for i in range(2)]
        att = [sb(f"att{i}", [P, D]) for i in range(2)]
        att_t = [sb(f"att_t{i}", [P, DT, P]) for i in range(2)]
        logits = sb("logits", [P, TT, E])
        prob = sb("prob", [P, TT, E])
        top = weight
        top_at = sb("top_at", [P, TT, 8], U32)
        top_f = sb("top_f", [P, TT, 8])
        lane = sb("lane", [P, E])
        picked = sb("picked", [P, 2, TT, E])
        chosen = sb("chosen", [P, TT, E])
        before = sb("before", [P, P])
        all_ones = sb("all_ones", [P, P])
        count = sb("count", [P, TT + 1, E])
        blocks = sb("blocks", [P, E])
        end = sb("end", [P, E + 1])
        first = sb("first", [P, E])
        rank = sb("rank", [P, TT, E])
        at = sb("at", [P, 2, TT, E])
        place_f = sb("place_f", [P, 2, TT])
        slot = sb("slot", [P, SLOTS + 1])
        slot_f = sb("slot_f", [P, SLOTS + 1])
        pair_f = sb("pair_f", [P, PAIRS_MAX])
        pairs_f = sb("pairs_f", [P, 1])
        small = sb("small", [P, 4, TT])
        ps = [mem.enter_context(nc.psum_tensor(f"ps_l{i}", [P, BANK], F32)) for i in range(4)]
        ps_kv = mem.enter_context(nc.psum_tensor("ps_lkv", [P, 2, BANK], F32))
        ps_heads = mem.enter_context(nc.psum_tensor("ps_lheads", [P, 2, BANK], F32))

        def norm_rows(eng, t, source_ready, source, sems):
            stats_done, aggr_done, var_done, std_done, rstd_done, xn_done = sems
            if t < TT:
                source_ready(t)
                nc.vector.bn_stats(stats[:, t, :], source[:, t, :]).then_inc(stats_done, 1)
                eng.wait_ge(stats_done, t + 1)
                nc.vector.bn_aggr(mean_var[:, t, :], stats[:, t, :]).then_inc(aggr_done, 1)
                eng.wait_ge(aggr_done, t + 1)
                nc.vector.tensor_scalar(std[:, t:t + 1], mean_var[:, t, 1:2], LN_EPS, None, ALU.add).then_inc(var_done, 1)
            if t >= 1:
                r = t - 1
                eng.wait_ge(std_done, r + 1)
                nc.vector.reciprocal(rstd[:, r:r + 1], std[:, r:r + 1]).then_inc(rstd_done, 1)
                eng.wait_ge(rstd_done, r + 1)
                nc.vector.tensor_scalar(xn[:, r, :], source[:, r, :], mean_var[:, r, 0:1], rstd[:, r:r + 1],
                                        ALU.subtract, ALU.mult).then_inc(xn_done, 1)

        with ExitStack() as stage:
            def sem(name):
                return stage.enter_context(nc.semaphore("c1_" + name))

            o_loaded = [sem(f"o_loaded{i}") for i in range(4)]
            x_loaded = [sem(f"x_loaded{i}") for i in range(4)]
            bias_loaded = sem("bias_loaded")
            w_loaded = {n: sem(f"{n}_loaded") for n in (*w_sb, *SPLIT)}
            w_hi_done, w_lo_done, xn_hi_done, xn_lo_done = sem("w_hi"), sem("w_lo"), sem("xn_hi"), sem("xn_lo")
            router_loaded = sem("router_loaded")
            x_biased, proj_done, x_added = sem("x_biased"), sem("proj_done"), sem("x_added")
            norm_sems = [sem(n) for n in ("stats", "aggr", "var", "std", "rstd", "xn")]
            turned = sem("turned")
            block = stage.enter_context(nc.Block())

            @block.sync
            def _(sp):
                sp.dma_start(w_sb["wout"][:], wout.rearrange("(t p) n -> p t n", p=P)).then_inc(w_loaded["wout"], 16)
                for i in range(4):
                    part = slice(i * NT // 4, (i + 1) * NT // 4)
                    sp.dma_start(o_t[:, :, part], attn_t.rearrange("(g p) n -> p g n", p=P)[:, :, part]
                                 ).then_inc(o_loaded[i], 16)
                    if i == 0:
                        sp.dma_start(bout_sb[:], bout).then_inc(bias_loaded, 16)
                    sp.dma_start(xs[:, 2 * i:2 * i + 2, :], x.rearrange("(t p) d -> p t d", p=P)[:, 2 * i:2 * i + 2, :]
                                 ).then_inc(x_loaded[i], 16)
                for name, w in (("lwq", lwq), ("lwk", lwk), ("lwv", lwv), ("lwo", lwo)):
                    to = w_raw[name] if name in SPLIT else w_sb[name][:]
                    sp.dma_start(to, w.rearrange("(t p) n -> p t n", p=P)).then_inc(w_loaded[name], 16)
                sp.dma_start(router_sb[:], router.rearrange("p (t e) -> p t e", t=DT)).then_inc(router_loaded, 16)
                for name in ("lwq", "lwk", "lwv", "lwo"):
                    sp.wait_ge(w_loaded[name], 16)
                sp.wait_ge(router_loaded, 16)

            @block.scalar
            def _(act):
                for t in range(TT + 1):
                    if t < TT:
                        act.wait_ge(norm_sems[2], t + 1)
                        nc.scalar.activation(std[:, t:t + 1], std[:, t:t + 1], ACT.Sqrt).then_inc(norm_sems[3], 1)
                    if t >= 1:
                        act.wait_ge(turned, t)
                        nc.scalar.copy(xn_hi[:, :, (t - 1) * P:t * P],
                                       ps[2 + (t - 1) % 2][:].rearrange("p (k c) -> p k c", k=DT)).then_inc(xn_hi_done, 1)
                    if t < len(SPLIT):
                        act.wait_ge(w_loaded[SPLIT[t]], 16)
                        nc.scalar.copy(w_hi[SPLIT[t]][:], w_raw[SPLIT[t]]).then_inc(w_hi_done, 1)

            @block.gpsimd
            def _(pool):
                for i, name in enumerate(SPLIT):
                    pool.wait_ge(w_hi_done, i + 1)
                    nc.gpsimd.tensor_tensor(w_lo[name][:], w_raw[name], w_hi[name][:].bitcast(F32),
                                            ALU.subtract).then_inc(w_lo_done, 1)

            @block.vector
            def _(dve):
                def add_bias(t):
                    dve.wait_ge(x_loaded[t // 2], 16)
                    nc.vector.tensor_tensor(xs[:, t, :], xs[:, t, :], bout_sb[:], ALU.add).then_inc(x_biased, 1)

                def ready(t):
                    if t + 2 < TT:
                        add_bias(t + 2)
                    dve.wait_ge(proj_done, t + 1)
                    dve.wait_ge(x_biased, t + 1)
                    nc.vector.tensor_tensor(x2[:, t, :], ps[t % 2][:], xs[:, t, :], ALU.add).then_inc(x_added, 1)
                    dve.wait_ge(x_added, t + 1)

                dve.wait_ge(bias_loaded, 16)
                for t in range(2):
                    add_bias(t)
                for t in range(TT + 3):
                    if t <= TT:
                        norm_rows(dve, t, ready, x2, norm_sems)
                    if t >= 3:
                        r = t - 3
                        dve.wait_ge(xn_hi_done, r + 1)
                        nc.vector.tensor_tensor(xn_lo[:, :, r * P:(r + 1) * P],
                                                ps[2 + r % 2][:].rearrange("p (k c) -> p k c", k=DT),
                                                xn_hi[:, :, r * P:(r + 1) * P].bitcast(F32), ALU.subtract
                                                ).then_inc(xn_lo_done, 1)

            @block.tensor
            def _(pe):
                pe.wait_ge(w_loaded["wout"], 16)
                for t in range(TT + 2):
                    if t < TT:
                        pe.wait_ge(o_loaded[t * 4 // TT], 16)
                        if t >= 2:
                            pe.wait_ge(x_added, t - 1)
                        for g in range(DT):
                            last = nc.tensor.matmul(ps[t % 2][:], o_t[:, g, t * P:(t + 1) * P], w_sb["wout"][:, g, :],
                                                    start=(g == 0), stop=(g == DT - 1))
                        last.then_inc(proj_done, 1)
                    if t >= 2:
                        r = t - 2
                        pe.wait_ge(norm_sems[5], r + 1)
                        if r >= 2:
                            pe.wait_ge(xn_lo_done, r - 1)
                        for k in range(DT):
                            last = nc.tensor.transpose(ps[2 + r % 2][:, k * P:(k + 1) * P], xn[:, r, k * P:(k + 1) * P],
                                                       ident[:])
                        last.then_inc(turned, 1)

        with ExitStack() as stage:
            def sem(name):
                return stage.enter_context(nc.semaphore("c2_" + name))

            made, low_done, expo_done, mapped = sem("made"), sem("low_done"), sem("expo_done"), sem("mapped")
            v_made, v_copied, zero_done, consts_done = sem("v_made"), sem("v_copied"), sem("zero_done"), sem("consts_done")
            kv_done, blocks_done, heads_done, den_done, inv_done, att_done = (
                sem("kv_done"), sem("blocks_done"), sem("heads_done"), sem("den_done"), sem("inv_done"), sem("att_done"))
            att_turned, att_copied = sem("att_turned"), sem("att_copied")
            proj_done, x_added = sem("proj_done"), sem("x_added")
            norm_sems = [sem(n) for n in ("stats", "aggr", "var", "std", "rstd", "xn")]
            turned, xnt_done = sem("turned"), sem("xnt_done")
            block = stage.enter_context(nc.Block())
            NF = 2 * TT
            ps_map = [ps_heads[:, 0], ps_heads[:, 1], ps[2][:], ps[3][:]]
            ps_v, ps_ks, ps_turn, ps_proj = ps[0], ps[1], ps[2], ps[3]
            kv_of = [ps_kv[:, i, :].rearrange("p (n c) -> p n c", n=DT) for i in range(2)]
            heads = ps_heads[:, :, 0:2 * (P + DT)].rearrange("p i (g c) -> p i g c", g=2)
            KV, HEADS, ATT_T, PROJ, TURN = 1, 2, 3, 4, 6

            def mapped_to(n):
                if n < TT:
                    return q_t[:, n // 2, (n % 2) * BANK:(n % 2 + 1) * BANK]
                return k_f[:, n - TT, :]

            @block.tensor
            def _(pe):
                def product(to, still, moving):
                    for k in range(DT):
                        for i, (a, b) in enumerate(((0, 0), (0, 1), (1, 0))):
                            last = nc.tensor.matmul(to, still[a][:, k, :], moving[b][:, k, :],
                                                    start=(k == 0 and i == 0), stop=(k == DT - 1 and i == 2))
                    return last

                for n in range(NF):
                    if n >= 4:
                        pe.wait_ge(mapped, n - 3)
                    if n < TT:
                        dims, rows = slice(n // 2 * P, (n // 2 + 1) * P), slice(n % 2 * BANK, (n % 2 + 1) * BANK)
                        last = product(ps_map[n % 4], (w_hi["lwq"][:, :, dims], w_lo["lwq"][:, :, dims]),
                                       (xn_hi[:, :, rows], xn_lo[:, :, rows]))
                    else:
                        rows = slice((n - TT) * P, (n - TT + 1) * P)
                        last = product(ps_map[n % 4], (xn_hi[:, :, rows], xn_lo[:, :, rows]), (w_hi["lwk"], w_lo["lwk"]))
                    last.then_inc(made, 1)
                for t in range(TT + TURN):
                    if t < TT:
                        if t >= 1:
                            pe.wait_ge(v_copied, 2 * t)
                        rows = slice(t * P, (t + 1) * P)
                        product(ps_v[:], (xn_hi[:, :, rows], xn_lo[:, :, rows]), (w_hi["lwv"], w_lo["lwv"])
                                ).then_inc(v_made, 1)
                    r = t - KV
                    if 0 <= r < TT:
                        pe.wait_ge(mapped, TT + r + 1)
                        pe.wait_ge(v_copied, 2 * r + 2)
                        pe.wait_ge(consts_done, 1)
                        if r >= 1:
                            pe.wait_ge(blocks_done, r)
                        for g in range(DT):
                            keys = k_f[:, r, g * P:(g + 1) * P]
                            nc.tensor.matmul(ps_kv[:, g // 2, (g % 2) * 2 * P:(g % 2 + 1) * 2 * P], keys,
                                             v_two[r % 2][:, g].rearrange("p b c -> p (b c)"),
                                             start=True, stop=True, skip_group_check=True)
                            last = nc.tensor.matmul(ps_ks[:, 2 * g:2 * g + 2], keys, ones_two[:],
                                                    start=True, stop=True, skip_group_check=True)
                        last.then_inc(kv_done, 1)
                    r = t - HEADS
                    if 0 <= r < TT:
                        pe.wait_ge(blocks_done, r + 1)
                        if r == 0:
                            pe.wait_ge(mapped, NF)
                        else:
                            pe.wait_ge(att_done, r)
                        for b in range(2):
                            for g in range(DT):
                                last = nc.tensor.matmul(heads[LQ * b:LQ * b + LQ, g // 2, g % 2, :],
                                                        q_t[:, g, (2 * r + b) * LQ:(2 * r + b + 1) * LQ],
                                                        kv_blocks[r % 2][:, g, b, :],
                                                        start=True, stop=True, skip_group_check=True)
                        last.then_inc(heads_done, 1)
                    r = t - ATT_T
                    if 0 <= r < TT:
                        pe.wait_ge(att_done, r + 1)
                        if r - (TURN - ATT_T) >= 1:
                            pe.wait_ge(xnt_done, r - (TURN - ATT_T))
                        if r >= 1:
                            pe.wait_ge(att_copied, r)
                        for k in range(DT):
                            last = nc.tensor.transpose(ps_turn[:, k * P:(k + 1) * P], att[r % 2][:, k * P:(k + 1) * P],
                                                       ident[:])
                        last.then_inc(att_turned, 1)
                    r = t - PROJ
                    if 0 <= r < TT:
                        pe.wait_ge(att_copied, r + 1)
                        if r >= 1:
                            pe.wait_ge(x_added, r)
                        for g in range(DT):
                            last = nc.tensor.matmul(ps_proj[:], att_t[r % 2][:, g, :], w_sb["lwo"][:, g, :],
                                                    start=(g == 0), stop=(g == DT - 1))
                        last.then_inc(proj_done, 1)
                    r = t - TURN
                    if 0 <= r < TT:
                        pe.wait_ge(norm_sems[5], r + 1)
                        pe.wait_ge(att_copied, min(TT, r + 1 + TURN - ATT_T))
                        if r >= 1:
                            pe.wait_ge(xnt_done, r)
                        for k in range(DT):
                            last = nc.tensor.transpose(ps_turn[:, k * P:(k + 1) * P], xn[:, r, k * P:(k + 1) * P],
                                                       ident[:])
                        last.then_inc(turned, 1)

            @block.vector
            def _(dve):
                for i in range(2):
                    nc.vector.memset(v_two[i], 0.0).then_inc(zero_done, 1)
                for buf in (same_head, head_of, ones_two):
                    nc.vector.memset(buf[:], 0.0).then_inc(zero_done, 1)
                dve.wait_ge(zero_done, 5)
                for h in range(DT):
                    nc.vector.memset(same_head[HD * h:HD * h + HD, HD * h:HD * h + HD], 1.0)
                    nc.vector.memset(head_of[HD * h:HD * h + HD, h:h + 1], 1.0)
                for b in range(2):
                    last = nc.vector.memset(ones_two[LQ * b:LQ * b + LQ, b:b + 1], 1.0)
                last.then_inc(consts_done, 1)
                for n in range(NF + 1):
                    if n < NF:
                        dve.wait_ge(made, n + 1)
                        if n >= 2:
                            dve.wait_ge(expo_done, n - 1)
                        nc.vector.tensor_scalar(low[n % 2][:], ps_map[n % 4], 0.0, None, ALU.min).then_inc(low_done, 1)
                    if n >= 1:
                        r = n - 1
                        dve.wait_ge(expo_done, r + 1)
                        nc.vector.scalar_tensor_tensor(out=mapped_to(r), in0=ps_map[r % 4], scalar=0.0,
                                                       in1=expo[r % 2][:], op0=ALU.max, op1=ALU.add).then_inc(mapped, 1)

                def ready(t):
                    dve.wait_ge(proj_done, t + 1)
                    nc.vector.tensor_tensor(x2[:, t, :], ps_proj[:], x2[:, t, :], ALU.add).then_inc(x_added, 1)
                    dve.wait_ge(x_added, t + 1)

                dve.wait_ge(consts_done, 1)
                for t in range(TT + TURN):
                    r = t - KV
                    if 0 <= r < TT:
                        dve.wait_ge(kv_done, r + 1)
                        if r >= 2:
                            dve.wait_ge(heads_done, r - 1)
                        for i in range(2):
                            nc.vector.tensor_tensor(
                                kv_blocks[r % 2][:, 2 * i:2 * i + 2, :, 0:P].rearrange("p g b c -> p (g b) c"), kv_of[i],
                                same_head[:].unsqueeze(1).to_broadcast([P, DT, P]), ALU.mult)
                        nc.vector.tensor_tensor(
                            kv_blocks[r % 2][:, :, :, P:].rearrange("p g b c -> p (g b) c"),
                            head_of[:].unsqueeze(1).to_broadcast([P, 2 * DT, DT]),
                            ps_ks[:, 0:2 * DT].unsqueeze(2).to_broadcast([P, 2 * DT, DT]), ALU.mult).then_inc(blocks_done, 1)
                    r = t - HEADS
                    if 0 <= r < TT:
                        dve.wait_ge(heads_done, r + 1)
                        nc.vector.tensor_scalar(den[r % 2][:], heads[:, :, :, P:], LIN_EPS, None, ALU.add
                                                ).then_inc(den_done, 1)
                        dve.wait_ge(den_done, r + 1)
                        nc.vector.reciprocal(den[r % 2][:], den[r % 2][:]).then_inc(inv_done, 1)
                        dve.wait_ge(inv_done, r + 1)
                        if r >= 2:
                            dve.wait_ge(att_turned, r - 1)
                        for i in range(2):
                            last = nc.vector.tensor_tensor(
                                att[r % 2][:, i * 2 * P:(i + 1) * 2 * P].rearrange("p (g h c) -> p g h c", g=2, h=DT),
                                heads[:, i, :, 0:P].rearrange("p g (h c) -> p g h c", h=DT),
                                den[r % 2][:, i].unsqueeze(3).to_broadcast([P, 2, DT, HD]), ALU.mult)
                        last.then_inc(att_done, 1)
                    r = t - PROJ
                    if 0 <= r <= TT:
                        norm_rows(dve, r, ready, x2, norm_sems)

            @block.scalar
            def _(act):
                for n in range(NF):
                    act.wait_ge(low_done, n + 1)
                    if n >= 2:
                        act.wait_ge(mapped, n - 1)
                    nc.scalar.activation(expo[n % 2][:], low[n % 2][:], ACT.Exp).then_inc(expo_done, 1)
                act.wait_ge(zero_done, 5)
                for t in range(TT + TURN):
                    if t < TT:
                        act.wait_ge(v_made, t + 1)
                        if t >= 2:
                            act.wait_ge(kv_done, t - 1)
                        for b in range(2):
                            nc.scalar.copy(v_two[t % 2][LQ * b:LQ * b + LQ, :, b, :],
                                           ps_v[LQ * b:LQ * b + LQ, :].rearrange("p (g c) -> p g c", g=DT)
                                           ).then_inc(v_copied, 1)
                    r = t - ATT_T
                    if 0 <= r < TT:
                        act.wait_ge(att_turned, r + 1)
                        if r >= 2:
                            act.wait_ge(proj_done, r - 1)
                        nc.scalar.copy(att_t[r % 2][:], ps_turn[:].rearrange("p (k c) -> p k c", k=DT)
                                       ).then_inc(att_copied, 1)
                    r = t - PROJ
                    if 0 <= r < TT:
                        act.wait_ge(norm_sems[2], r + 1)
                        nc.scalar.activation(std[:, r:r + 1], std[:, r:r + 1], ACT.Sqrt).then_inc(norm_sems[3], 1)
                    r = t - TURN
                    if 0 <= r < TT:
                        act.wait_ge(turned, r + 1)
                        nc.scalar.copy(xn_t[:, :, r * P:(r + 1) * P], ps_turn[:].rearrange("p (k c) -> p k c", k=DT)
                                       ).then_inc(xnt_done, 1)

            @block.gpsimd
            def _(pool):
                nc.gpsimd.iota(lane[:], pattern=[[1, E]], base=0, channel_multiplier=0,
                               allow_small_or_imprecise_dtypes=True)

        with ExitStack() as stage:
            def sem(name):
                return stage.enter_context(nc.semaphore("c3_" + name))

            gated, gmax_done, gneg_done, gexp_done, ginv_done, prob_done = (
                sem("gated"), sem("gmax"), sem("gneg"), sem("gexp"), sem("ginv"), sem("prob"))
            top_done, at_done, atf_done, picked_done, chosen_done = (
                sem("top"), sem("at"), sem("atf"), sem("picked"), sem("chosen"))
            consts, step, ranked = sem("consts"), sem("step"), sem("ranked")
            block = stage.enter_context(nc.Block())

            @block.tensor
            def _(pe):
                for t in range(TT):
                    for k in range(DT):
                        last = nc.tensor.matmul(ps[2][:, t * E:(t + 1) * E], xn_t[:, k, t * P:(t + 1) * P],
                                                router_sb[:, k, :], start=(k == 0), stop=(k == DT - 1))
                last.then_inc(gated, 1)
                pe.wait_ge(consts, 3)
                pe.wait_ge(chosen_done, 1)
                picks = chosen[:].rearrange("p t e -> p (t e)")
                nc.tensor.matmul(ps[0][:, 0:TT * E], before[:], picks, start=True, stop=True)
                nc.tensor.matmul(ps[1][:, 0:TT * E], all_ones[:], picks, start=True, stop=True).then_inc(ranked, 1)

            @block.vector
            def _(dve):
                dve.wait_ge(gated, 1)
                nc.vector.tensor_reduce(small[:, 0, :], ps[2][:, 0:TT * E].rearrange("p (t e) -> p t e", t=TT), AX.X,
                                        ALU.max).then_inc(gmax_done, 1)
                dve.wait_ge(gmax_done, 1)
                nc.vector.tensor_scalar(small[:, 1, :], small[:, 0, :], -1.0, None, ALU.mult).then_inc(gneg_done, 1)
                dve.wait_ge(gexp_done, TT)
                nc.vector.reciprocal(small[:, 3, :], small[:, 2, :]).then_inc(ginv_done, 1)
                dve.wait_ge(ginv_done, 1)
                nc.vector.tensor_tensor(prob[:], logits[:], small[:, 3, :].unsqueeze(2).to_broadcast([P, TT, E]),
                                        ALU.mult).then_inc(prob_done, 1)
                dve.wait_ge(prob_done, 1)
                for t in range(TT):
                    nc.vector.max(top[:, t, :], prob[:, t, :]).then_inc(top_done, 1)
                    dve.wait_ge(top_done, t + 1)
                    nc.vector.max_index(top_at[:, t, :], top[:, t, :], prob[:, t, :]).then_inc(at_done, 1)
                dve.wait_ge(at_done, TT)
                nc.vector.tensor_copy(top_f[:], top_at[:]).then_inc(atf_done, 1)
                dve.wait_ge(atf_done, 1)
                for k in range(2):
                    nc.vector.tensor_tensor(picked[:, k], lane[:].unsqueeze(1).to_broadcast([P, TT, E]),
                                            top_f[:, :, k:k + 1].to_broadcast([P, TT, E]), ALU.is_equal
                                            ).then_inc(picked_done, 1)
                dve.wait_ge(picked_done, 2)
                nc.vector.tensor_tensor(chosen[:], picked[:, 0], picked[:, 1], ALU.add).then_inc(chosen_done, 1)
                steps = [0]

                def then(ins):
                    steps[0] += 1
                    ins.then_inc(step, 1)
                    dve.wait_ge(step, steps[0])

                then(nc.vector.memset(count[:, 0, :], 0.0))
                then(nc.vector.memset(end[:, 0:1], 0.0))
                dve.wait_ge(ranked, 1)
                for t in range(TT):
                    then(nc.vector.tensor_tensor(count[:, t + 1, :], ps[1][:, t * E:(t + 1) * E], count[:, t, :], ALU.add))
                then(nc.vector.tensor_scalar(blocks[:], count[:, TT, :], 0.0, None, ALU.is_gt))
                for j in range(1, -(-NT // BLOCK)):
                    then(nc.vector.scalar_tensor_tensor(out=blocks[:], in0=count[:, TT, :], scalar=float(BLOCK * j),
                                                        in1=blocks[:], op0=ALU.is_gt, op1=ALU.add))
                for e in range(E):
                    then(nc.vector.tensor_tensor(end[:, e + 1:e + 2], end[:, e:e + 1], blocks[:, e:e + 1], ALU.add))
                then(nc.vector.tensor_scalar(first[:], end[:, 0:E], float(BLOCK), None, ALU.mult))
                then(nc.vector.tensor_tensor(rank[:], ps[0][:, 0:TT * E].rearrange("p (t e) -> p t e", t=TT),
                                             count[:, 0:TT, :], ALU.add))
                then(nc.vector.tensor_tensor(rank[:], rank[:], first[:].unsqueeze(1).to_broadcast([P, TT, E]), ALU.add))
                for k in range(2):
                    then(nc.vector.tensor_tensor(at[:, k], rank[:], picked[:, k], ALU.mult))
                then(nc.vector.tensor_reduce(place_f[:], at[:], AX.X, ALU.add))
                then(nc.vector.tensor_copy(place[:], place_f[:]))
                then(nc.vector.tensor_scalar(slot_f[:], slot[:], end[:, 1:2], None, ALU.is_ge))
                for e in range(1, E - 1):
                    then(nc.vector.scalar_tensor_tensor(out=slot_f[:], in0=slot[:], scalar=end[:, e + 1:e + 2],
                                                        in1=slot_f[:], op0=ALU.is_ge, op1=ALU.add))
                then(nc.vector.tensor_copy(slot_expert[:], slot_f[0:1, :]))
                then(nc.vector.tensor_scalar(pair_f[:], slot[:, 0:PAIRS_MAX], 2.0, 2.0, ALU.mult, ALU.add))
                then(nc.vector.tensor_scalar(pair_f[:], pair_f[:], end[:, E:E + 1], None, ALU.is_lt))
                then(nc.vector.tensor_reduce(pairs_f[:], pair_f[:], AX.X, ALU.add))
                then(nc.vector.tensor_copy(slot_pairs[:], pairs_f[0:1, :]))

            @block.gpsimd
            def _(pool):
                nc.gpsimd.memset(all_ones[:], 1.0).then_inc(consts, 1)
                nc.gpsimd.iota(slot[:], pattern=[[1, SLOTS + 1]], base=0, channel_multiplier=0,
                               allow_small_or_imprecise_dtypes=True).then_inc(consts, 1)
                pool.wait_ge(consts, 2)
                nc.gpsimd.affine_select(out=before[:], in_=all_ones[:], compare_op=ALU.is_gt, fill=0.0, base=0,
                                        pattern=[[1, P]], channel_multiplier=-1).then_inc(consts, 1)

            @block.scalar
            def _(act):
                act.wait_ge(gneg_done, 1)
                for t in range(TT):
                    nc.scalar.activation(logits[:, t, :], ps[2][:, t * E:(t + 1) * E], ACT.Exp, bias=small[:, 1, t:t + 1],
                                         accum_out=small[:, 2, t:t + 1]).then_inc(gexp_done, 1)




def experts(nc, ident, x2, xn, weight, place, slot_expert, slot_pairs, rows_in, rows_out, w1, w2, out):
    with ExitStack() as mem:
        def sb(name, shape, dt=F32):
            return mem.enter_context(nc.sbuf_tensor(name, shape, dt))

        def sem(name):
            return mem.enter_context(nc.semaphore("e_" + name))

        RAW = 4
        TAKEN = 4
        AHEAD = 2
        NW2 = IT // WC
        TURN = 3
        rows = sb("rows", [P, RB, D])
        rows_hi = [sb(f"rows_hi{i}", [P, DT, BLOCK], F32R) for i in range(2)]
        rows_lo = [sb(f"rows_lo{i}", [P, DT, BLOCK], F32R) for i in range(2)]
        w1_raw = [sb(f"w1_raw{i}", [P, DT, 2, P]) for i in range(RAW)]
        w1_hi = [sb(f"w1_hi{i}", [P, DT, 2, P], F32R) for i in range(RAW)]
        w1_lo = [sb(f"w1_lo{i}", [P, DT, 2, P], F32R) for i in range(RAW)]
        w2_raw = [sb(f"w2_raw{i}", [P, WC, D]) for i in range(2)]
        w2_hi = sb("w2_hi", [P, IT, D], F32R)
        w2_lo = sb("w2_lo", [P, IT, D], F32R)
        silu = [sb(f"silu{i}", [P, BLOCK]) for i in range(2)]
        y = [sb(f"y{i}", [P, BLOCK]) for i in range(2)]
        y_hi = sb("y_hi", [P, IT, BLOCK], F32R)
        y_lo = sb("y_lo", [P, IT, BLOCK], F32R)
        down = sb("down", [P, RB, D])
        taken = [sb(f"taken{i}", [P, D]) for i in range(TAKEN)]
        stored_mark = sb("stored_mark", [P, 1])
        ps_up = [mem.enter_context(nc.psum_tensor(f"ps_up{i}", [P, 2, BANK], F32)) for i in range(2)]
        ps_r = mem.enter_context(nc.psum_tensor("ps_r", [P, DT, P], F32))
        ps_d = [mem.enter_context(nc.psum_tensor(f"ps_d{i}", [P, D], F32)) for i in range(RB)]

        rows_loaded = sem("rows_loaded")
        w1_loaded = [sem(f"w1_loaded{i}") for i in range(RAW)]
        w2_loaded = [sem(f"w2_loaded{i}") for i in range(2)]
        w1_hi_done, w1_lo_done, w2_hi_done, w2_lo_done = sem("w1_hi"), sem("w1_lo"), sem("w2_hi"), sem("w2_lo")
        rows_turned, rows_hi_done, rows_lo_done = sem("rows_turned"), sem("rows_hi"), sem("rows_lo")
        up_done, silu_done, y_done, y_hi_done, y_lo_done = sem("up"), sem("silu"), sem("y"), sem("y_hi"), sem("y_lo")
        parts_done, down_free, down_stored = sem("down_parts"), sem("down_free"), sem("down_stored")
        taken_done = [sem(f"taken{i}") for i in range(TAKEN)]
        weighed, stored, all_stored = sem("weighed"), sem("stored"), sem("all_stored")
        dispatched = sem("dispatched")

        block = mem.enter_context(nc.Block())

        def over_slots(engine, slot):
            pairs = engine.value_load(slot_pairs[0:1, 0:1], min_val=PAIRS_MIN, max_val=PAIRS_MAX)
            slot(0, 0, False)
            with engine.Fori(0, PAIRS_MAX) as i:
                with engine.If(i < pairs):
                    slot(i * 2 + 1, 1, False)
                    slot(i * 2 + 2, 0, False)
            slot(pairs * 2 + 1, 1, True)
            return pairs * 2 + 1

        def is_first(s):
            return isinstance(s, int) and s == 0

        @block.sync
        def _(sp):
            def load_rows(s):
                if positive(s):
                    sp.wait_ge(rows_turned, s * RB)
                sp.dma_start(rows[:], rows_in[bass.ds(s * BLOCK, BLOCK), :].rearrange("(r p) d -> p r d", p=P)
                             ).then_inc(rows_loaded, 16)

            def slot(s, par, last):
                e = sp.value_load(slot_expert[0:1, bass.ds(s, 1)], min_val=0, max_val=E - 1)
                for u in range(IT):
                    n = IT * s + u
                    if u == AHEAD and is_first(s):
                        sp.wait_ge(dispatched, 16 * 2 * TT)
                        load_rows(0)
                    if u == IT // 2 and not last:
                        load_rows(s + 1)
                    if positive(n - RAW + 1):
                        sp.wait_ge(w1_lo_done, n - RAW + 1)
                    sp.dma_start(w1_raw[u % RAW][:], w1[bass.ds(e, 1), u].rearrange(
                        "a p (t s c) -> (a p) t s c", t=DT, s=2)).then_inc(w1_loaded[u % RAW], 16)
                    if u % WC == WC - 1:
                        c = u // WC
                        m = NW2 * s + c
                        if positive(m - 1):
                            sp.wait_ge(w2_lo_done, m - 1)
                        sp.dma_start(w2_raw[c % 2][:], w2[bass.ds(e, 1), c].rearrange(
                            "a p (k n) -> (a p) k n", k=WC)).then_inc(w2_loaded[c % 2], 16)

            over_slots(sp, slot)
            ov = out.rearrange("(t p) d -> p t d", p=P)
            for t in range(TT):
                sp.wait_ge(weighed, 2 * t + 2)
                sp.dma_start(ov[:, t, :], x2[:, t, :]).then_inc(stored, 16)
            sp.wait_ge(stored, 16 * TT)

        @block.gpsimd
        def _(pool):
            def slot(s, par, last):
                for c in range(NW2):
                    pool.wait_ge(w2_hi_done, NW2 * s + c + 1)
                    nc.gpsimd.tensor_tensor(w2_lo[:, WC * c:WC * c + WC, :], w2_raw[c % 2][:],
                                            w2_hi[:, WC * c:WC * c + WC, :].bitcast(F32), ALU.subtract
                                            ).then_inc(w2_lo_done, 1)

            for t in range(TT):
                for k in range(2):
                    nc.gpsimd.indirect_dma_start(
                        out=rows_in, out_offset=bass.IndirectOffsetOnAxis(ap=place[:, k, t:t + 1], axis=0),
                        in_=xn[:, t, :], in_offset=None).then_inc(dispatched, 16)
            end = over_slots(pool, slot)
            pool.wait_ge(down_stored, 16 * (end + 1))
            nc.gpsimd.tensor_tensor(stored_mark[:], ident[:, 0:1], ident[:, 1:2], ALU.subtract).then_inc(all_stored, 1)
            pool.wait_ge(all_stored, 1)
            for t in range(TT):
                for k in range(2):
                    n = 2 * t + k
                    if n >= TAKEN:
                        pool.wait_ge(weighed, n - TAKEN + 1)
                    nc.gpsimd.indirect_dma_start(
                        out=taken[n % TAKEN][:], out_offset=None, in_=rows_out,
                        in_offset=bass.IndirectOffsetOnAxis(ap=place[:, k, t:t + 1], axis=0)
                        ).then_inc(taken_done[n % TAKEN], 16)

        @block.scalar
        def _(act):
            def split_w1(s, u):
                n = IT * s + u
                act.wait_ge(w1_loaded[u % RAW], 16 * (s * (IT // RAW) + u // RAW + 1))
                if positive(n - RAW + 1):
                    act.wait_ge(up_done, n - RAW + 1)
                nc.scalar.copy(w1_hi[u % RAW][:], w1_raw[u % RAW][:]).then_inc(w1_hi_done, 1)

            def split_w2(s, c):
                act.wait_ge(w2_loaded[c % 2], 16 * (s * (NW2 // 2) + c // 2 + 1))
                if positive(s):
                    act.wait_ge(parts_done, IT * (s - 1) + WC * (c + 1))
                nc.scalar.copy(w2_hi[:, WC * c:WC * c + WC, :], w2_raw[c % 2][:]).then_inc(w2_hi_done, 1)

            def round_y(s, u):
                act.wait_ge(y_done, IT * s + u + 1)
                if positive(s):
                    act.wait_ge(parts_done, IT * (s - 1) + u + 1)
                nc.scalar.copy(y_hi[:, u, :], y[u % 2][:]).then_inc(y_hi_done, 1)

            def round_rows(s, par, r):
                act.wait_ge(rows_turned, s * RB + r + 1)
                nc.scalar.copy(rows_hi[par][:, :, r * P:(r + 1) * P], ps_r[:]).then_inc(rows_hi_done, 1)

            def store_down(s):
                act.wait_ge(parts_done, IT * (s + 1))
                if positive(s):
                    act.wait_ge(down_stored, 16 * s)
                for r in range(RB):
                    nc.scalar.copy(down[:, r, :], ps_d[r][:]).then_inc(down_free, 1)
                act.wait_ge(down_free, RB * (s + 1))
                act.dma_start(rows_out[bass.ds(s * BLOCK, BLOCK), :].rearrange("(r p) d -> p r d", p=P), down[:]
                              ).then_inc(down_stored, 16)

            def slot(s, par, last):
                first = is_first(s)
                for u in range(IT):
                    n = IT * s + u
                    if u == 0 and not first:
                        round_y(s - 1, IT - 1)
                    if u + AHEAD < IT:
                        split_w1(s, u + AHEAD)
                    elif not last:
                        split_w1(s + 1, u + AHEAD - IT)
                    if u == 0 and not first:
                        split_w2(s - 1, NW2 - 1)
                    if u > 0 and u % WC == 0:
                        split_w2(s, u // WC - 1)
                    if u > 0:
                        round_y(s, u - 1)
                    act.wait_ge(up_done, n + 1)
                    if positive(n - 1):
                        act.wait_ge(y_done, n - 1)
                    nc.scalar.activation(silu[u % 2][:], ps_up[u % 2][:, 0, 0:BLOCK], ACT.Silu).then_inc(silu_done, 1)
                    if TURN < u <= TURN + RB and not last:
                        round_rows(s + 1, 1 - par, u - TURN - 1)
                if not first:
                    store_down(s - 1)

            for u in range(AHEAD):
                split_w1(0, u)
            for r in range(RB):
                round_rows(0, 0, r)
            end = over_slots(act, slot)
            round_y(end, IT - 1)
            split_w2(end, NW2 - 1)
            store_down(end)

        @block.vector
        def _(dve):
            def split_w1(s, u):
                dve.wait_ge(w1_hi_done, IT * s + u + 1)
                nc.vector.tensor_tensor(w1_lo[u % RAW][:], w1_raw[u % RAW][:], w1_hi[u % RAW][:].bitcast(F32),
                                        ALU.subtract).then_inc(w1_lo_done, 1)

            def rest_y(s, u):
                dve.wait_ge(y_hi_done, IT * s + u + 1)
                nc.vector.tensor_tensor(y_lo[:, u, :], y[u % 2][:], y_hi[:, u, :].bitcast(F32), ALU.subtract
                                        ).then_inc(y_lo_done, 1)

            def rest_rows(s, par, r):
                dve.wait_ge(rows_hi_done, s * RB + r + 1)
                nc.vector.tensor_tensor(rows_lo[par][:, :, r * P:(r + 1) * P], ps_r[:],
                                        rows_hi[par][:, :, r * P:(r + 1) * P].bitcast(F32), ALU.subtract
                                        ).then_inc(rows_lo_done, 1)

            def slot(s, par, last):
                for u in range(IT):
                    if u == 0 and not is_first(s):
                        rest_y(s - 1, IT - 1)
                    if u + AHEAD < IT:
                        split_w1(s, u + AHEAD)
                    elif not last:
                        split_w1(s + 1, u + AHEAD - IT)
                    if u > 0:
                        rest_y(s, u - 1)
                    dve.wait_ge(silu_done, IT * s + u + 1)
                    nc.vector.tensor_tensor(y[u % 2][:], ps_up[u % 2][:, 1, 0:BLOCK], silu[u % 2][:], ALU.mult
                                            ).then_inc(y_done, 1)
                    if TURN < u <= TURN + RB and not last:
                        rest_rows(s + 1, 1 - par, u - TURN - 1)

            for u in range(AHEAD):
                split_w1(0, u)
            for r in range(RB):
                rest_rows(0, 0, r)
            end = over_slots(dve, slot)
            rest_y(end, IT - 1)
            for t in range(TT):
                for k in range(2):
                    n = 2 * t + k
                    dve.wait_ge(taken_done[n % TAKEN], 16 * (n // TAKEN + 1))
                    if n:
                        dve.wait_ge(weighed, n)
                    nc.vector.scalar_tensor_tensor(out=x2[:, t, :], in0=taken[n % TAKEN][:], scalar=weight[:, t, k:k + 1],
                                                   in1=x2[:, t, :], op0=ALU.mult, op1=ALU.add).then_inc(weighed, 1)

        @block.tensor
        def _(pe):
            def turn_rows(s, r):
                if r == 0:
                    pe.wait_ge(rows_loaded, 16 * (s + 1))
                if positive(RB * s + r):
                    pe.wait_ge(rows_lo_done, RB * s + r)
                for k in range(DT):
                    last = nc.tensor.transpose(ps_r[:, k, :], rows[:, r, k * P:(k + 1) * P], ident[:])
                last.then_inc(rows_turned, 1)

            def up(s, par, u):
                n = IT * s + u
                pe.wait_ge(w1_lo_done, n + 1)
                if u == 0:
                    pe.wait_ge(rows_lo_done, RB * (s + 1))
                if positive(n - 1):
                    pe.wait_ge(y_done, n - 1)
                for side in range(2):
                    for k in range(DT):
                        hi, lo = w1_hi[u % RAW][:, k, side, :], w1_lo[u % RAW][:, k, side, :]
                        for i, (still, moving) in enumerate([(hi, rows_hi[par]), (hi, rows_lo[par]), (lo, rows_hi[par])]):
                            last = nc.tensor.matmul(ps_up[u % 2][:, side, 0:BLOCK], still, moving[:, k, :],
                                                    start=(k == 0 and i == 0), stop=(k == DT - 1 and i == 2))
                last.then_inc(up_done, 1)

            def down_part(s, k):
                pe.wait_ge(y_lo_done, IT * s + k + 1)
                pe.wait_ge(w2_lo_done, NW2 * s + k // WC + 1)
                if k == 0 and positive(s):
                    pe.wait_ge(down_free, RB * s)
                for r in range(RB):
                    yh, yl = (part[:, k, r * P:(r + 1) * P] for part in (y_hi, y_lo))
                    for i, (still, moving) in enumerate([(yh, w2_hi), (yh, w2_lo), (yl, w2_hi)]):
                        last = nc.tensor.matmul(ps_d[r][:], still, moving[:, k, :], start=(k == 0 and i == 0),
                                                stop=(k == IT - 1 and i == 2))
                last.then_inc(parts_done, 1)

            def slot(s, par, last):
                for u in range(IT):
                    up(s, par, u)
                    if not is_first(s):
                        down_part(s - 1, u)
                    if TURN <= u < TURN + RB and not last:
                        turn_rows(s + 1, u - TURN)

            for r in range(RB):
                turn_rows(0, r)
            end = over_slots(pe, slot)
            for k in range(IT):
                down_part(end, k)


_OUT = "out_dram"


def kernel(x, ctx_1024, L0_xattn_Wq, L0_xattn_bq, L0_xattn_Wkv, L0_xattn_bkv, L0_xattn_Wout, L0_xattn_bout,
           L0_attn_Wq, L0_attn_Wk, L0_attn_Wv, L0_attn_Wo, L0_ffn_w1, L0_ffn_w2, L0_ffn_router_w):
    import numpy as np
    import concourse.bacc as bacc
    from concourse.bass_utils import run_bass_kernel_spmd

    def by_partition(v):
        return np.asarray(v).reshape(DT, P).T

    ctx = np.zeros((B + 1, DT, P, LC2), np.float32)
    ctx[:B, :, :, :LC] = np.asarray(ctx_1024).transpose(0, 2, 1).reshape(B, DT, P, LC)
    ctx = np.concatenate([ctx[:, :, :, c * CW:c * CW + CHUNK_W[c]].transpose(0, 2, 1, 3).reshape(B + 1, P, -1)
                          for c in range(CHUNKS)], axis=2)
    wkv = np.asarray(L0_xattn_Wkv).reshape(D, D, 2)
    bkv = np.asarray(L0_xattn_bkv).reshape(D, 2)
    w1 = np.asarray(L0_ffn_w1).reshape(E, 2, IT, P, DT, P).transpose(0, 2, 5, 4, 1, 3).reshape(E, IT, P, DT * 2 * P)
    w2 = np.asarray(L0_ffn_w2).reshape(E, D, IT // WC, WC, P).transpose(0, 2, 4, 3, 1).reshape(E, IT // WC, P, WC * D)
    arrays = {
        "x": np.asarray(x).reshape(NT, D),
        "ctx": ctx,
        "wq": L0_xattn_Wq, "bq": by_partition(L0_xattn_bq),
        "wk": wkv[:, :, 0], "wv": wkv[:, :, 1], "bk": by_partition(bkv[:, 0]), "bv": bkv[:, 1].reshape(PAIRS, 2 * HD).T,
        "wout": L0_xattn_Wout, "bout": np.broadcast_to(np.asarray(L0_xattn_bout), (P, D)),
        "lwq": np.asarray(L0_attn_Wq).T, "lwk": np.asarray(L0_attn_Wk).T,
        "lwv": np.asarray(L0_attn_Wv).T, "lwo": np.asarray(L0_attn_Wo).T,
        "router": np.asarray(L0_ffn_router_w).reshape(E, DT, P).transpose(2, 1, 0).reshape(P, DT * E),
        "w1": w1, "w2": w2,
    }
    arrays = {f"{n}_dram": np.ascontiguousarray(a) for n, a in arrays.items()}
    nc = bacc.Bacc("TRN2", target_bir_lowering=False, num_devices=1, dynamic_dma_scratch_size=SCRATCH)
    args = [nc.dram_tensor(n, a.shape, F32, kind="ExternalInput").ap() for n, a in arrays.items()]
    args.append(nc.dram_tensor(_OUT, (NT, D), F32, kind="ExternalOutput").ap())
    names = [n[:-5] for n in arrays] + ["out"]
    build(nc, **dict(zip(names, args)))
    r = run_bass_kernel_spmd(nc, [arrays], core_ids=[0])
    return r.results[0][_OUT].reshape(B, LQ, D)
```
